# Optimizing a Trainium2 kernel written in Bass

```python
import numpy as np
import jax
import jax.numpy as jnp

def _softmax(x, axis=-1):
    return jax.nn.softmax(x, axis=axis)

def _gelu(x):
    return jax.nn.gelu(x, approximate=True)

def _silu(x):
    return jax.nn.silu(x)

def _sigmoid(x):
    return jax.nn.sigmoid(x)

def _layernorm(x, axis=-1, eps=1e-05):
    m = jnp.mean(x, axis=axis, keepdims=True)
    v = jnp.var(x, axis=axis, keepdims=True)
    return (x - m) / jnp.sqrt(v + eps)

def _scatter_add(tgt, idx, src, axis=0):
    return tgt.at[idx].add(src)

def _segment_sum(src, seg, n):
    return jax.ops.segment_sum(src, seg, n)
kernel_name = 'mk_xattn_seq_d2_seqx_r8_0c1eec'

def setup_inputs(seed: int=0):
    np.random.seed(seed)
    _w = jnp.asarray

    def _rec_inputs():
        import jax
        import jax.numpy as jnp
        _rk = jax.random.key(seed)
        x = 7.22e-05 + 1 * jax.random.normal(jax.random.fold_in(_rk, 1), (4, 256, 256), jnp.float32)
        _lenS = 256 - jax.random.randint(jax.random.fold_in(_rk, 7), (4,), 0, max(1, 256 // 4) + 1, jnp.int32)
        _lenS2 = 1601 - jax.random.randint(jax.random.fold_in(_rk, 8), (4,), 0, max(1, 1601 // 4) + 1, jnp.int32)
        _ctx_2048P = jax.random.normal(jax.random.fold_in(_rk, 11), (4, 16, 256), jnp.float32)
        _ctx_2048c = jax.random.dirichlet(jax.random.fold_in(_rk, 511), 0.3 * jnp.ones((16,), jnp.float32), (4, 1601))
        _ctx_2048t = jnp.einsum('bsk,bkd->bsd', _ctx_2048c, _ctx_2048P)
        _ctx_2048t = _ctx_2048t * jax.lax.rsqrt(jnp.mean(jnp.square(_ctx_2048t)) + 1e-12) * 0.953939
        ctx_2048 = 4.13588e-05 + 0.999923 * (_ctx_2048t + 0.3 * jax.random.normal(jax.random.fold_in(_rk, 611), (4, 1601, 256), jnp.float32))
        _validS = jnp.arange(256)[None, :] < _lenS[:, None]
        _validS2 = jnp.arange(1601)[None, :] < _lenS2[:, None]
        _causal = jnp.tril(jnp.ones((256, 256), dtype=bool))
        mask_Bx1xSxS2_ff0 = jnp.where(jnp.ones((4, 1, 256, 1601), dtype=bool), 0.0, -1000000000.0).astype(jnp.float32)
        return (x, ctx_2048, mask_Bx1xSxS2_ff0)
    x, ctx_2048, mask_Bx1xSxS2_ff0 = _rec_inputs()

    def _L0_xattn_setup():
        import jax, jax.numpy as jnp
        import numpy as np
        H = 256
        NH = 32
        KVH = 8
        HD = H // NH
        GROUPS = NH // KVH
        EPS = 1e-06
        B, L, S = (4, 128, 128)

        def _gqa_forward(hidden_state, encoder_hidden_state, encoder_attention_mask, Wq, bq, Wk, bk, Wv, bv, Wo, bo, gamma, beta):
            b, l, _ = hidden_state.shape
            s = encoder_hidden_state.shape[1]
            q = hidden_state @ Wq + bq
            k = encoder_hidden_state @ Wk + bk
            v = encoder_hidden_state @ Wv + bv
            q = q.reshape(b, l, KVH, GROUPS, HD).transpose(0, 2, 3, 1, 4)
            k = k.reshape(b, s, KVH, HD).transpose(0, 2, 1, 3)
            v = v.reshape(b, s, KVH, HD).transpose(0, 2, 1, 3)
            scale = 1.0 / jnp.sqrt(jnp.asarray(HD, q.dtype))
            scores = jnp.einsum('bkgld,bksd->bkgls', q, k) * scale
            scores = scores + encoder_attention_mask[:, :, None, :, :]
            attn = jax.nn.softmax(scores, axis=-1)
            out = jnp.einsum('bkgls,bksd->bkgld', attn, v)
            out = out.transpose(0, 3, 1, 2, 4).reshape(b, l, H)
            out = out @ Wo + bo
            x = out + hidden_state
            mu = jnp.mean(x, axis=-1, keepdims=True)
            var = jnp.var(x, axis=-1, keepdims=True)
            return (x - mu) * jax.lax.rsqrt(var + EPS) * gamma + beta
        key = jax.random.key(seed)
        ks = jax.random.split(key, 12)
        sd = 0.02
        return {'hidden_state': jax.random.normal(ks[0], (B, L, H), jnp.float32), 'encoder_hidden_state': jax.random.normal(ks[1], (B, S, H), jnp.float32), 'encoder_attention_mask': jnp.zeros((B, 1, L, S), jnp.float32), 'Wq': jax.random.normal(ks[2], (H, H), jnp.float32) * sd, 'bq': jnp.zeros((H,), jnp.float32), 'Wk': jax.random.normal(ks[3], (H, KVH * HD), jnp.float32) * sd, 'bk': jnp.zeros((KVH * HD,), jnp.float32), 'Wv': jax.random.normal(ks[4], (H, KVH * HD), jnp.float32) * sd, 'bv': jnp.zeros((KVH * HD,), jnp.float32), 'Wo': jax.random.normal(ks[5], (H, H), jnp.float32) * sd, 'bo': jnp.zeros((H,), jnp.float32), 'gamma': jnp.ones((H,), jnp.float32), 'beta': jnp.zeros((H,), jnp.float32)}
    _L0_xattn_all = _L0_xattn_setup()
    _L0_xattn_in = {k: v for k, v in _L0_xattn_all.items() if k in ('Wq', 'bq', 'Wk', 'bk', 'Wv', 'bv', 'Wo', 'bo', 'gamma', 'beta')}
    del _L0_xattn_all

    def _L1_xattn_setup():
        import jax, jax.numpy as jnp
        import numpy as np
        N_HEAD = 32
        EPS = 1e-05

        def _ln(x, w, b):
            m = jnp.mean(x, axis=-1, keepdims=True)
            v = jnp.mean((x - m) ** 2, axis=-1, keepdims=True)
            return (x - m) * jax.lax.rsqrt(v + EPS) * w + b

        def _forward(x, state, i, ln1_w, ln1_b, ln2_w, ln2_b, maa_x, maa_w, maa_k, maa_v, maa_r, maa_g, maa_w1, maa_w2, time_decay, decay_w1, decay_w2, faaaa, Wr, Wk, Wv, Wg, Wo, gn_w, gn_b, fmaa_k, fmaa_r, fWk, fWr, fWv):
            B, L, C = x.shape
            H = N_HEAD
            S = C // H
            i0 = (2 + S) * i
            xa = _ln(x, ln1_w, ln1_b)
            sx = jnp.concatenate([state[:, i0 + 1][:, None], xa[:, :-1]], axis=1) - xa
            xxx = xa + sx * maa_x
            t = jnp.tanh(xxx @ maa_w1).reshape(B, L, 5, -1)
            m = jnp.einsum('blfd,fdc->blfc', t, maa_w2)
            mw, mk, mv, mr, mg = (m[:, :, j] for j in range(5))
            xw = xa + sx * (maa_w + mw)
            xk = xa + sx * (maa_k + mk)
            xv = xa + sx * (maa_v + mv)
            xr = xa + sx * (maa_r + mr)
            xg = xa + sx * (maa_g + mg)
            w = time_decay + jnp.tanh(xw @ decay_w1) @ decay_w2
            w = jnp.exp(-jnp.exp(w)).reshape(B, L, H, S)
            r = (xr @ Wr.T).reshape(B, L, H, S)
            k = (xk @ Wk.T).reshape(B, L, H, S)
            v = (xv @ Wv.T).reshape(B, L, H, S)
            g = jax.nn.silu(xg @ Wg.T)
            s0 = state[:, i0 + 2:i0 + 2 + S].reshape(B, H, S, S)

            def step(s, inp):
                k_l, v_l, w_l, r_l = inp
                a = k_l[..., :, None] * v_l[..., None, :]
                out = jnp.einsum('bhs,bhst->bht', r_l, faaaa * a + s)
                s_new = a + w_l[..., None] * s
                return (s_new, out)
            seq = tuple((z.transpose(1, 0, 2, 3) for z in (k, v, w, r)))
            _, outs = jax.lax.scan(step, s0, seq)
            y = outs.transpose(1, 0, 2, 3)
            gm = jnp.mean(y, axis=-1, keepdims=True)
            gv = jnp.mean((y - gm) ** 2, axis=-1, keepdims=True)
            y = ((y - gm) * jax.lax.rsqrt(gv + EPS)).reshape(B, L, C) * gn_w + gn_b
            x = x + y * g @ Wo.T
            xc = _ln(x, ln2_w, ln2_b)
            sxc = jnp.concatenate([state[:, i0][:, None], xc[:, :-1]], axis=1) - xc
            xk2 = xc + sxc * fmaa_k
            xr2 = xc + sxc * fmaa_r
            rr = jax.nn.sigmoid(xr2 @ fWr.T)
            kk = jnp.square(jax.nn.relu(xk2 @ fWk.T))
            x = x + rr * (kk @ fWv.T)
            return x
        key = jax.random.key(seed)
        B, L, C, H = (8, 64, 256, N_HEAD)
        S = C // H
        DM, DD = (32, 64)
        ks = jax.random.split(key, 32)
        n = lambda k, shp, s=1.0: jax.random.normal(k, shp, dtype=jnp.float32) * s
        u = lambda k, shp: jax.random.uniform(k, shp, dtype=jnp.float32)
        inp = {'x': n(ks[0], (B, L, C)), 'state': n(ks[1], (B, 2 + S, C), 0.1), 'i': 0, 'ln1_w': jnp.ones((C,), jnp.float32), 'ln1_b': jnp.zeros((C,), jnp.float32), 'ln2_w': jnp.ones((C,), jnp.float32), 'ln2_b': jnp.zeros((C,), jnp.float32), 'maa_x': u(ks[2], (C,)), 'maa_w': u(ks[3], (C,)), 'maa_k': u(ks[4], (C,)), 'maa_v': u(ks[5], (C,)), 'maa_r': u(ks[6], (C,)), 'maa_g': u(ks[7], (C,)), 'maa_w1': n(ks[8], (C, 5 * DM), 0.02), 'maa_w2': n(ks[9], (5, DM, C), 0.02), 'time_decay': n(ks[10], (C,), 0.5), 'decay_w1': n(ks[11], (C, DD), 0.02), 'decay_w2': n(ks[12], (DD, C), 0.02), 'faaaa': n(ks[13], (H, S, 1), 0.1), 'Wr': n(ks[14], (C, C), 0.02), 'Wk': n(ks[15], (C, C), 0.02), 'Wv': n(ks[16], (C, C), 0.02), 'Wg': n(ks[17], (C, C), 0.02), 'Wo': n(ks[18], (C, C), 0.02), 'gn_w': jnp.ones((C,), jnp.float32), 'gn_b': jnp.zeros((C,), jnp.float32), 'fmaa_k': u(ks[19], (C,)), 'fmaa_r': u(ks[20], (C,)), 'fWk': n(ks[21], (C, C), 0.02), 'fWr': n(ks[22], (C, C), 0.02), 'fWv': n(ks[23], (C, C), 0.02)}
        return inp
    _L1_xattn_all = _L1_xattn_setup()
    _L1_xattn_in = {k: v for k, v in _L1_xattn_all.items() if k in ('ln1_w', 'ln1_b', 'ln2_w', 'ln2_b', 'maa_x', 'maa_w', 'maa_k', 'maa_v', 'maa_r', 'maa_g', 'maa_w1', 'maa_w2', 'time_decay', 'decay_w1', 'decay_w2', 'faaaa', 'Wr', 'Wk', 'Wv', 'Wg', 'Wo', 'gn_w', 'gn_b', 'fmaa_k', 'fmaa_r', 'fWk', 'fWr', 'fWv')}
    del _L1_xattn_all
    return {'x': x, 'ctx_2048': ctx_2048, 'mask_Bx1xSxS2_ff0': mask_Bx1xSxS2_ff0, 'L0_xattn_Wq': _L0_xattn_in['Wq'], 'L0_xattn_bq': _L0_xattn_in['bq'], 'L0_xattn_Wk': _L0_xattn_in['Wk'], 'L0_xattn_bk': _L0_xattn_in['bk'], 'L0_xattn_Wv': _L0_xattn_in['Wv'], 'L0_xattn_bv': _L0_xattn_in['bv'], 'L0_xattn_Wo': _L0_xattn_in['Wo'], 'L0_xattn_bo': _L0_xattn_in['bo'], 'L0_xattn_gamma': _L0_xattn_in['gamma'], 'L0_xattn_beta': _L0_xattn_in['beta'], 'L1_xattn_ln1_w': _L1_xattn_in['ln1_w'], 'L1_xattn_ln1_b': _L1_xattn_in['ln1_b'], 'L1_xattn_ln2_w': _L1_xattn_in['ln2_w'], 'L1_xattn_ln2_b': _L1_xattn_in['ln2_b'], 'L1_xattn_maa_x': _L1_xattn_in['maa_x'], 'L1_xattn_maa_w': _L1_xattn_in['maa_w'], 'L1_xattn_maa_k': _L1_xattn_in['maa_k'], 'L1_xattn_maa_v': _L1_xattn_in['maa_v'], 'L1_xattn_maa_r': _L1_xattn_in['maa_r'], 'L1_xattn_maa_g': _L1_xattn_in['maa_g'], 'L1_xattn_maa_w1': _L1_xattn_in['maa_w1'], 'L1_xattn_maa_w2': _L1_xattn_in['maa_w2'], 'L1_xattn_time_decay': _L1_xattn_in['time_decay'], 'L1_xattn_decay_w1': _L1_xattn_in['decay_w1'], 'L1_xattn_decay_w2': _L1_xattn_in['decay_w2'], 'L1_xattn_faaaa': _L1_xattn_in['faaaa'], 'L1_xattn_Wr': _L1_xattn_in['Wr'], 'L1_xattn_Wk': _L1_xattn_in['Wk'], 'L1_xattn_Wv': _L1_xattn_in['Wv'], 'L1_xattn_Wg': _L1_xattn_in['Wg'], 'L1_xattn_Wo': _L1_xattn_in['Wo'], 'L1_xattn_gn_w': _L1_xattn_in['gn_w'], 'L1_xattn_gn_b': _L1_xattn_in['gn_b'], 'L1_xattn_fmaa_k': _L1_xattn_in['fmaa_k'], 'L1_xattn_fmaa_r': _L1_xattn_in['fmaa_r'], 'L1_xattn_fWk': _L1_xattn_in['fWk'], 'L1_xattn_fWr': _L1_xattn_in['fWr'], 'L1_xattn_fWv': _L1_xattn_in['fWv']}

def reference(x, ctx_2048, mask_Bx1xSxS2_ff0, L0_xattn_Wq, L0_xattn_bq, L0_xattn_Wk, L0_xattn_bk, L0_xattn_Wv, L0_xattn_bv, L0_xattn_Wo, L0_xattn_bo, L0_xattn_gamma, L0_xattn_beta, L1_xattn_ln1_w, L1_xattn_ln1_b, L1_xattn_ln2_w, L1_xattn_ln2_b, L1_xattn_maa_x, L1_xattn_maa_w, L1_xattn_maa_k, L1_xattn_maa_v, L1_xattn_maa_r, L1_xattn_maa_g, L1_xattn_maa_w1, L1_xattn_maa_w2, L1_xattn_time_decay, L1_xattn_decay_w1, L1_xattn_decay_w2, L1_xattn_faaaa, L1_xattn_Wr, L1_xattn_Wk, L1_xattn_Wv, L1_xattn_Wg, L1_xattn_Wo, L1_xattn_gn_w, L1_xattn_gn_b, L1_xattn_fmaa_k, L1_xattn_fmaa_r, L1_xattn_fWk, L1_xattn_fWr, L1_xattn_fWv):
    import jax
    import jax.numpy as jnp

    def _L0_xattn_ref(hidden_state, encoder_hidden_state, encoder_attention_mask, Wq, bq, Wk, bk, Wv, bv, Wo, bo, gamma, beta):
        import jax, jax.numpy as jnp
        import numpy as np
        H = 256
        NH = 32
        KVH = 8
        HD = H // NH
        GROUPS = NH // KVH
        EPS = 1e-06
        B, L, S = (4, 128, 128)

        def _gqa_forward(hidden_state, encoder_hidden_state, encoder_attention_mask, Wq, bq, Wk, bk, Wv, bv, Wo, bo, gamma, beta):
            b, l, _ = hidden_state.shape
            s = encoder_hidden_state.shape[1]
            q = hidden_state @ Wq + bq
            k = encoder_hidden_state @ Wk + bk
            v = encoder_hidden_state @ Wv + bv
            q = q.reshape(b, l, KVH, GROUPS, HD).transpose(0, 2, 3, 1, 4)
            k = k.reshape(b, s, KVH, HD).transpose(0, 2, 1, 3)
            v = v.reshape(b, s, KVH, HD).transpose(0, 2, 1, 3)
            scale = 1.0 / jnp.sqrt(jnp.asarray(HD, q.dtype))
            scores = jnp.einsum('bkgld,bksd->bkgls', q, k) * scale
            scores = scores + encoder_attention_mask[:, :, None, :, :]
            attn = jax.nn.softmax(scores, axis=-1)
            out = jnp.einsum('bkgls,bksd->bkgld', attn, v)
            out = out.transpose(0, 3, 1, 2, 4).reshape(b, l, H)
            out = out @ Wo + bo
            x = out + hidden_state
            mu = jnp.mean(x, axis=-1, keepdims=True)
            var = jnp.var(x, axis=-1, keepdims=True)
            return (x - mu) * jax.lax.rsqrt(var + EPS) * gamma + beta
        return _gqa_forward(hidden_state, encoder_hidden_state, encoder_attention_mask, Wq, bq, Wk, bk, Wv, bv, Wo, bo, gamma, beta)

    def _L1_xattn_ref(x, state, i, ln1_w, ln1_b, ln2_w, ln2_b, maa_x, maa_w, maa_k, maa_v, maa_r, maa_g, maa_w1, maa_w2, time_decay, decay_w1, decay_w2, faaaa, Wr, Wk, Wv, Wg, Wo, gn_w, gn_b, fmaa_k, fmaa_r, fWk, fWr, fWv):
        import jax, jax.numpy as jnp
        import numpy as np
        N_HEAD = 32
        EPS = 1e-05

        def _ln(x, w, b):
            m = jnp.mean(x, axis=-1, keepdims=True)
            v = jnp.mean((x - m) ** 2, axis=-1, keepdims=True)
            return (x - m) * jax.lax.rsqrt(v + EPS) * w + b

        def _forward(x, state, i, ln1_w, ln1_b, ln2_w, ln2_b, maa_x, maa_w, maa_k, maa_v, maa_r, maa_g, maa_w1, maa_w2, time_decay, decay_w1, decay_w2, faaaa, Wr, Wk, Wv, Wg, Wo, gn_w, gn_b, fmaa_k, fmaa_r, fWk, fWr, fWv):
            B, L, C = x.shape
            H = N_HEAD
            S = C // H
            i0 = (2 + S) * i
            xa = _ln(x, ln1_w, ln1_b)
            sx = jnp.concatenate([state[:, i0 + 1][:, None], xa[:, :-1]], axis=1) - xa
            xxx = xa + sx * maa_x
            t = jnp.tanh(xxx @ maa_w1).reshape(B, L, 5, -1)
            m = jnp.einsum('blfd,fdc->blfc', t, maa_w2)
            mw, mk, mv, mr, mg = (m[:, :, j] for j in range(5))
            xw = xa + sx * (maa_w + mw)
            xk = xa + sx * (maa_k + mk)
            xv = xa + sx * (maa_v + mv)
            xr = xa + sx * (maa_r + mr)
            xg = xa + sx * (maa_g + mg)
            w = time_decay + jnp.tanh(xw @ decay_w1) @ decay_w2
            w = jnp.exp(-jnp.exp(w)).reshape(B, L, H, S)
            r = (xr @ Wr.T).reshape(B, L, H, S)
            k = (xk @ Wk.T).reshape(B, L, H, S)
            v = (xv @ Wv.T).reshape(B, L, H, S)
            g = jax.nn.silu(xg @ Wg.T)
            s0 = state[:, i0 + 2:i0 + 2 + S].reshape(B, H, S, S)

            def step(s, inp):
                k_l, v_l, w_l, r_l = inp
                a = k_l[..., :, None] * v_l[..., None, :]
                out = jnp.einsum('bhs,bhst->bht', r_l, faaaa * a + s)
                s_new = a + w_l[..., None] * s
                return (s_new, out)
            seq = tuple((z.transpose(1, 0, 2, 3) for z in (k, v, w, r)))
            _, outs = jax.lax.scan(step, s0, seq)
            y = outs.transpose(1, 0, 2, 3)
            gm = jnp.mean(y, axis=-1, keepdims=True)
            gv = jnp.mean((y - gm) ** 2, axis=-1, keepdims=True)
            y = ((y - gm) * jax.lax.rsqrt(gv + EPS)).reshape(B, L, C) * gn_w + gn_b
            x = x + y * g @ Wo.T
            xc = _ln(x, ln2_w, ln2_b)
            sxc = jnp.concatenate([state[:, i0][:, None], xc[:, :-1]], axis=1) - xc
            xk2 = xc + sxc * fmaa_k
            xr2 = xc + sxc * fmaa_r
            rr = jax.nn.sigmoid(xr2 @ fWr.T)
            kk = jnp.square(jax.nn.relu(xk2 @ fWk.T))
            x = x + rr * (kk @ fWv.T)
            return x
        return _forward(x, state, i, ln1_w, ln1_b, ln2_w, ln2_b, maa_x, maa_w, maa_k, maa_v, maa_r, maa_g, maa_w1, maa_w2, time_decay, decay_w1, decay_w2, faaaa, Wr, Wk, Wv, Wg, Wo, gn_w, gn_b, fmaa_k, fmaa_r, fWk, fWr, fWv)
    x = _L0_xattn_ref(x, ctx_2048, mask_Bx1xSxS2_ff0, L0_xattn_Wq, L0_xattn_bq, L0_xattn_Wk, L0_xattn_bk, L0_xattn_Wv, L0_xattn_bv, L0_xattn_Wo, L0_xattn_bo, L0_xattn_gamma, L0_xattn_beta)
    x = _L1_xattn_ref(x, ctx_2048, 0, L1_xattn_ln1_w, L1_xattn_ln1_b, L1_xattn_ln2_w, L1_xattn_ln2_b, L1_xattn_maa_x, L1_xattn_maa_w, L1_xattn_maa_k, L1_xattn_maa_v, L1_xattn_maa_r, L1_xattn_maa_g, L1_xattn_maa_w1, L1_xattn_maa_w2, L1_xattn_time_decay, L1_xattn_decay_w1, L1_xattn_decay_w2, L1_xattn_faaaa, L1_xattn_Wr, L1_xattn_Wk, L1_xattn_Wv, L1_xattn_Wg, L1_xattn_Wo, L1_xattn_gn_w, L1_xattn_gn_b, L1_xattn_fmaa_k, L1_xattn_fmaa_r, L1_xattn_fWk, L1_xattn_fWr, L1_xattn_fWv)
    return x

_drawn_inputs = setup_inputs


def setup_inputs(seed=0):
    import zlib

    import numpy as np

    out = dict(_drawn_inputs(seed))
    spreads = {'L0_xattn_bq': (0.0, 0.8),
     'L0_xattn_bk': (0.0, 2.0),
     'L0_xattn_bv': (0.0, 0.309),
     'L0_xattn_bo': (0.0, 0.1),
     'L0_xattn_gamma': (1.0, 0.2),
     'L0_xattn_beta': (0.0, 0.1),
     'L1_xattn_ln1_w': (1.0, 0.6),
     'L1_xattn_ln1_b': (0.0, 0.585),
     'L1_xattn_ln2_w': (1.0, 0.6),
     'L1_xattn_ln2_b': (0.0, 0.8),
     'L1_xattn_gn_w': (1.0, 0.6),
     'L1_xattn_gn_b': (0.0, 0.8)}
    factors = {'L0_xattn_Wq': 8.0,
     'L0_xattn_Wk': 8.0,
     'L1_xattn_maa_x': 8.0,
     'L1_xattn_maa_w': 8.0,
     'L1_xattn_maa_v': 2.669,
     'L1_xattn_maa_w1': 8.0,
     'L1_xattn_maa_w2': 8.0,
     'L1_xattn_time_decay': 3.927,
     'L1_xattn_decay_w1': 8.0,
     'L1_xattn_decay_w2': 8.0,
     'L1_xattn_faaaa': 7.854,
     'L1_xattn_fmaa_k': 7.615,
     'L1_xattn_fmaa_r': 8.0,
     'L1_xattn_fWk': 4.291,
     'L1_xattn_fWr': 8.0,
     'L1_xattn_fWv': 3.925}
    for name, (base, spread) in spreads.items():
        noise = np.random.default_rng([zlib.crc32(name.encode()), seed]).standard_normal(out[name].shape)
        drawn = base * np.exp(spread * noise) if base else spread * noise
        out[name] = jnp.asarray(drawn.astype(out[name].dtype))
    for name, factor in factors.items():
        out[name] = (out[name] * factor).astype(out[name].dtype)
    return out
```

```python
from contextlib import ExitStack

import concourse.bass as bass
from concourse import mybir

ALU = mybir.AluOpType
ACT = mybir.ActivationFunctionType
AX = mybir.AxisListType
F32 = mybir.dt.float32
BF16 = mybir.dt.bfloat16
I32 = mybir.dt.int32

P = 128

B, L, C = 4, 256, 256
S = 1601
NH, KVH, HD = 32, 8, 8
GROUPS = NH // KVH
LT = L // P
CT = C // P
ST = -(-S // P)
SLAST = S - (ST - 1) * P
UNITS = KVH // 2
UH = 2 * GROUPS
SPLIT = 64
TERMS = 6
BANK = 512
SCALE = HD ** -0.5
NEG = -3.0e38
EPS0, EPS1 = 1e-6, 1e-5

Q_PART = (0, 0, 1, 1, 0, 2)
K_PART = (0, 1, 0, 1, 2, 0)

ACHUNK = (0, 2 * BANK, S)
A_PER_UNIT = UH * LT * 2
A_PER_BATCH = A_PER_UNIT * UNITS
E_PER_TILE = 4
E_PER_UNIT = E_PER_TILE * ST
E_PER_BATCH = E_PER_UNIT * UNITS

PREP = ([("ctxT", n, "act") for n in range(-(-ST // 2))] + [("xT", 0, "act"), ("q", 0, "dve")]
        + [("kv", n, "dve") for n in range(-(-ST // 4))] + [("qT", n, "act") for n in range(UNITS)]
        + [("kT", n, "act" if n % 2 else "dve") for n in range(2 * UNITS)])
PREP_ACT = sum(r[2] == "act" for r in PREP)
PREP_DVE = len(PREP) - PREP_ACT


def emptied_before(n):
    done = PREP[:n - 3] if n >= 4 else []
    return sum(r[2] == "act" for r in done), sum(r[2] == "dve" for r in done)


MIXES, DM, DD = 5, 32, 64
TURNED = ("Wk", "Wv", "Wr", "Wg", "Wo", "fWk", "fWr", "fWv")
VECTORS = ("ln1_w", "ln1_b", "ln2_w", "ln2_b", "maa_x", "maa_w", "maa_k", "maa_v", "maa_r", "maa_g",
           "time_decay", "faaaa", "gn_w", "gn_b", "fmaa_k", "fmaa_r")

LEAD, TURN = 6, 2


def batch_order():
    order = []
    for u in range(UNITS):
        for n in range(A_PER_UNIT):
            order.append((A_PER_UNIT * u + n, "max", u, n))
        after = A_PER_UNIT * (u + 1)
        order.append((after + TURN - 0.9, "turn", u, 0))
        tile = A_PER_UNIT / ST
        for t in range(ST):
            at = after + LEAD + tile * t
            for j in range(E_PER_TILE):
                order.append((at + tile * j / 5 + 0.1, "exp", u, (t, j)))
            if t:
                order.append((at + tile * 0.65, "values", u, t - 1))
        order.append((after + LEAD + A_PER_UNIT + 0.05, "values", u, ST - 1))
        order.append((after + LEAD + A_PER_UNIT + 0.06, "copy", u, 0))
        order.append((after + LEAD + A_PER_UNIT + 2 * tile, "normal", u, 0))
    return [x[1:] for x in sorted(order, key=lambda x: x[0])]


ORDER = batch_order()


def rows_of(tile):
    return SLAST if tile == ST - 1 else P


def build(nc, a, out):
    with ExitStack() as whole:
        def sb(name, shape, dt):
            return whole.enter_context(nc.sbuf_tensor(name, shape, dt))

        def sem(name):
            return whole.enter_context(nc.semaphore(name))

        held = {
            "ident_f": sb("ident_f", [P, P], F32),
            "x_nat": sb("x_nat", [P, B, LT, C], F32),
            "o_nat": sb("o_nat", [P, B, LT, C], F32),
            "w_nat": sb("w_nat", [P, len(TURNED), CT, C], F32),
            "wo": sb("wo", [P, CT, C], F32),
            "maa_w1": sb("maa_w1", [P, CT, MIXES * DM], F32),
            "maa_w2": sb("maa_w2", [P, C], F32),
            "maa_w2_last": sb("maa_w2_last", [DM, C], F32),
            "decay_w1": sb("decay_w1", [P, CT, DD], F32),
            "decay_w2": sb("decay_w2", [DD, C], F32),
            "rows": sb("rows", [P, 3, C], F32),
            "vec_nat": sb("vec_nat", [CT * len(VECTORS), P], F32),
            "state_nat": sb("state_nat", [2 * B, C], F32),
            "s0": sb("s0", [P, CT, B, HD], F32),
        }
        loads_in = sem("loads_in")
        attention(nc, sem, held, loads_in, a)
        mixing(nc, sem, held, loads_in, out)


def load_second_part(eng, held, loads_in, a):
    pairs = [(held["x_nat"][:], a["x"].rearrange("b (t p) c -> p b t c", p=P)),
             (held["wo"][:], a["Wo0"].rearrange("(t p) n -> p t n", p=P)),
             (held["maa_w1"][:], a["maa_w1"].rearrange("(t p) n -> p t n", p=P)),
             (held["maa_w2"][:], a["maa_w2"][0:MIXES - 1].rearrange("f d c -> (f d) c")),
             (held["maa_w2_last"][:], a["maa_w2"][MIXES - 1]),
             (held["decay_w1"][:], a["decay_w1"].rearrange("(t p) n -> p t n", p=P)),
             (held["decay_w2"][:], a["decay_w2"])]
    pairs += [(held["rows"][:, n, :], a[name].partition_broadcast(P)) for n, name in enumerate(("bo", "gamma", "beta"))]
    pairs += [(held["w_nat"][:, n], a[name].rearrange("(t p) n -> p t n", p=P)) for n, name in enumerate(TURNED)]
    for n, name in enumerate(VECTORS):
        v = a[name]
        if len(v.shape) > 1:
            v = v.rearrange("h s a -> (h s a)")
        pairs.append((held["vec_nat"][CT * n:CT * (n + 1), :], v.rearrange("(t p) -> t p", p=P)))
    for b in range(B):
        pairs.append((held["state_nat"][2 * b:2 * b + 2, :], a["ctx"][b, 0:2, :]))
        pairs.append((held["s0"][:, :, b, :],
                      a["ctx"][b, 2:2 + HD, :].rearrange("r c -> (r c)").rearrange("(j p t) -> p j t", j=CT, t=HD)))
    for to, of in pairs:
        eng.dma_start(to, of).then_inc(loads_in, 16)
    return len(pairs)


def attention(nc, sem, held, loads_in, a):
    x, ctx_in, mask, Wq, bq, Wk, bk, Wv, bv = (a[n] for n in ("x", "ctx", "mask", "Wq", "bq", "Wk0", "bk", "Wv0", "bv"))
    ident_f, o_nat = held["ident_f"], held["o_nat"]
    with ExitStack() as here:
        def sb(name, shape, dt):
            return here.enter_context(nc.sbuf_tensor(name, shape, dt))

        def psum(name, shape, dt):
            return here.enter_context(nc.psum_tensor(name, shape, dt))

        ident_b = sb("ident_b", [P, P], BF16)
        wq = sb("wq", [P, CT, C], F32)
        wkv = sb("wkv", [P, CT, 2 * KVH * HD], F32)
        bq_row = sb("bq_row", [P, C], F32)
        bkv_row = sb("bkv_row", [P, 2 * KVH * HD], F32)
        ones_col = sb("ones_col", [P, 1], F32)
        x_bat = sb("x_bat", [P, LT, C], F32)
        ctx_nat = sb("ctx_nat", [P, ST, C], F32)
        ctx_t = sb("ctx_t", [P, CT, ST * P], F32)
        mask_nat = sb("mask_nat", [P, LT, S], F32)
        mask_abs = sb("mask_abs", [P, LT, S], BF16)
        mask_sum = sb("mask_sum", [P, 1], F32)
        mask_any = sb("mask_any", [P, 1], F32)
        mask_flag = sb("mask_flag", [1, 1], I32)
        x_t = sb("x_t", [P, CT, L], F32)
        q_f = sb("q_f", [P, LT * C], F32)
        q_part = sb("q_part", [P, 2, LT * C], F32)
        q_aug = sb("q_aug", [P, LT, NH, SPLIT], BF16)
        k_f = sb("k_f", [P, ST, KVH * HD], F32)
        k_part = sb("k_part", [P, 2, ST * KVH * HD], F32)
        k_aug = sb("k_aug", [P, ST, KVH, SPLIT], BF16)
        v_aug = sb("v_aug", [P, ST, KVH, 32], F32)
        q_t = sb("q_t", [P, UNITS, 2, GROUPS, L], BF16)
        k_t = sb("k_t", [P, UNITS, ST * P], BF16)
        max_part = sb("max_part", [P, LT, 2, GROUPS, 2], F32)
        zeros = sb("zeros", [P, LT, 2, GROUPS], F32)
        neg_max = sb("neg_max", [P, LT, 2, GROUPS], F32)
        max_rest = sb("max_rest", [P, 2, LT, 2, GROUPS], F32)
        max_split = sb("max_split", [P, LT, 2, 3, GROUPS], BF16)
        max_t = sb("max_t", [24, L], BF16)
        probs = sb("probs", [P, 2, E_PER_TILE, BANK], F32)
        pv_sb = sb("pv_sb", [P, BANK], F32)
        row_sum = sb("row_sum", [P, LT, 2, 4], F32)

        p_max = psum("p_max", [P, 2, 2, BANK], F32)
        p_sc = psum("p_sc", [P, 2, BANK], F32)
        p_pv = psum("p_pv", [P, BANK], F32)
        p_side = psum("p_side", [P, BANK], F32)
        def t_buf(u, t):
            return (ST * u + t) % 2

        def block_of(aug, term):
            return aug.rearrange("p t h c -> p (t h) c")[:, :, term * HD:(term + 1) * HD]

        def operand(what, i, src):
            src_b = src.bitcast(BF16)
            if what == "qT":
                return [(q_t[SPLIT * half:SPLIT * (half + 1), i, half].rearrange("p h l -> p (h l)"),
                         src_b[SPLIT * half:SPLIT * (half + 1), :]) for half in range(2)]
            lo = 8 * (i % 2) * P
            hi = min(lo + 8 * P, S)
            return [(k_t[:, i // 2, lo:hi], src_b[:, 0:hi - lo])]

        ring = [p_max[:, k // 2, k % 2, :] for k in range(4)]

        weights_in = sem("weights_in")
        ctx_loaded = sem("ctx_loaded")
        mask_loaded = sem("mask_loaded")
        const_ready = sem("const_ready")
        bias_in = sem("bias_in")
        prep_full = sem("prep_full")
        prep_act = sem("prep_act")
        prep_dve = sem("prep_dve")
        operands_clear = sem("operands_clear")
        q_split = sem("q_split")
        k_split = sem("k_split")
        q_copied = sem("q_copied")
        k_copied = sem("k_copied")
        mask_summed = sem("mask_summed")
        mask_counted = sem("mask_counted")
        mask_anyed = sem("mask_anyed")
        mask_flagged = sem("mask_flagged")
        max_full = sem("max_full")
        max_seen = sem("max_seen")
        max_done = sem("max_done")
        max_ready = sem("max_ready")
        max_turned = sem("max_turned")
        max_copied = sem("max_copied")
        max_placed = sem("max_placed")
        sc_full = sem("sc_full")
        exp_done = sem("exp_done")
        pv_done = sem("pv_done")
        pv_copied = sem("pv_copied")
        o_turned = sem("o_turned")
        o_summed = sem("o_summed")
        bias_scaled = sem("bias_scaled")
        o_done = sem("o_done")
        o_free = sem("o_free")
        pool_step = sem("pool_step")

        POOL_START = 4
        POOL_PER_BATCH = UNITS * 5

        with nc.Block() as block:

            @block.sync
            def _(sp):
                sp.dma_start(wkv[:, :, 0:KVH * HD], Wk.rearrange("(t p) n -> p t n", p=P)).then_inc(weights_in, 16)
                sp.dma_start(wkv[:, :, KVH * HD:], Wv.rearrange("(t p) n -> p t n", p=P)).then_inc(weights_in, 16)
                sp.dma_start(wq[:], Wq.rearrange("(t p) n -> p t n", p=P)).then_inc(weights_in, 16)
                sp.sem_inc(max_placed, 16)

                def load_context(b):
                    sp.dma_start(ctx_nat[:, 0:ST - 1, :],
                                 ctx_in[b, 0:(ST - 1) * P, :].rearrange("(t p) c -> p t c", p=P)).then_inc(ctx_loaded, 16)
                    sp.dma_start(ctx_nat[0:SLAST, ST - 1, :], ctx_in[b, (ST - 1) * P:S, :]).then_inc(ctx_loaded, 16)
                    sp.dma_start(x_bat[:], x[b, :, :].rearrange("(t p) c -> p t c", p=P)).then_inc(ctx_loaded, 16)

                def load_mask(b):
                    sp.dma_start(mask_nat[:], mask[b, 0, :, :].rearrange("(t p) s -> p t s", p=P)).then_inc(mask_loaded, 16)

                def place_maxima(b):
                    for u in range(UNITS):
                        sp.wait_ge(max_copied, b * UNITS + (u + 1))
                        for half in range(2):
                            row = SPLIT * half + TERMS * HD
                            sp.dma_start(q_t[row:row + 3, u, half, :, :], max_t[12 * half:12 * half + 12, :]).then_inc(max_placed, 16)

                load_context(0)
                load_mask(0)
                with sp.Fori(0, B - 1) as b:
                    sp.wait_ge(prep_act, b * PREP_ACT + (-(-ST // 2) + 1))
                    load_context(b + 1)
                    place_maxima(b)
                    sp.wait_ge(mask_summed, b + 1)
                    sp.wait_ge(max_done, b * A_PER_BATCH + (A_PER_BATCH + 1))
                    sp.wait_ge(sc_full, b * E_PER_BATCH + E_PER_BATCH)
                    load_mask(b + 1)
                place_maxima(B - 1)
                sp.wait_ge(max_placed, 16 + 32 * UNITS * B)

            @block.gpsimd
            def _(pool):
                pool.memset(ident_f[:], 0.0).then_inc(pool_step, 1)
                pool.memset(ident_b[:], 0.0).then_inc(pool_step, 1)
                pool.memset(ones_col[:], 1.0)
                pool.memset(v_aug[:], 0.0).then_inc(pool_step, 1)
                pool.memset(zeros[:], 0.0).then_inc(pool_step, 1)
                pool.wait_ge(pool_step, POOL_START)
                for m in (ident_f, ident_b):
                    pool.affine_select(out=m[:], in_=m[:], compare_op=ALU.not_equal, fill=1.0, base=0,
                                       pattern=[[-1, P]], channel_multiplier=1)
                pool.memset(v_aug[:, :, :, HD:HD + 1], 1.0).then_inc(const_ready, 1)

                chain = [0]

                def step(ins, b):
                    chain[0] += 1
                    ins.then_inc(pool_step, 1)
                    pool.wait_ge(pool_step, b * POOL_PER_BATCH + (POOL_START + chain[0]))

                with pool.Fori(0, B) as b:
                    for u in range(UNITS):
                        pool.wait_ge(max_ready, b * UNITS + (u + 1))
                        pool.wait_ge(max_turned, b * UNITS + (u + 1))
                        c = [max_split[:, :, :, k, :] for k in range(3)]
                        step(pool.tensor_tensor(c[0], neg_max[:], zeros[:], ALU.add), b)
                        step(pool.tensor_tensor(max_rest[:, 0], neg_max[:], c[0], ALU.subtract), b)
                        step(pool.tensor_tensor(c[1], max_rest[:, 0], zeros[:], ALU.add), b)
                        step(pool.tensor_tensor(max_rest[:, 1], max_rest[:, 0], c[1], ALU.subtract), b)
                        step(pool.tensor_tensor(c[2], max_rest[:, 1], zeros[:], ALU.add), b)
                    assert chain[0] == POOL_PER_BATCH, chain[0]

            @block.tensor
            def _(pe):
                pe.sem_inc(pv_done, 2)
                pe.sem_inc(o_turned, 1)
                pe.sem_inc(max_turned, 1)
                pe.wait_ge(const_ready, 1)
                pe.wait_ge(weights_in, 48)

                def prep(b):
                    for n, (what, i, _) in enumerate(PREP):
                        if n < 4:
                            pe.wait_ge(max_done, b * A_PER_BATCH + 1)
                        else:
                            by_act, by_dve = emptied_before(n)
                            if by_act:
                                pe.wait_ge(prep_act, b * PREP_ACT + by_act)
                            if by_dve:
                                pe.wait_ge(prep_dve, b * PREP_DVE + by_dve)
                        out = ring[n % 4]
                        out_b = out.bitcast(BF16)
                        if what == "ctxT":
                            if i == 0:
                                pe.wait_ge(ctx_loaded, b * 48 + 48)
                            for t in range(2 * i, min(2 * i + 2, ST)):
                                r = rows_of(t)
                                for j in range(CT):
                                    at = (2 * (t % 2) + j) * P
                                    mm = pe.transpose(out[:, at:at + r], ctx_nat[0:r, t, j * P:(j + 1) * P], ident_f[0:r, 0:r])
                        elif what == "xT":
                            for lt in range(LT):
                                for j in range(CT):
                                    mm = pe.transpose(out[:, j * L + lt * P:j * L + (lt + 1) * P],
                                                      x_bat[:, lt, j * P:(j + 1) * P], ident_f[:])
                        elif what == "q":
                            pe.wait_ge(prep_act, b * PREP_ACT + (-(-ST // 2) + 1))
                            for lt in range(LT):
                                for j in range(CT):
                                    mm = pe.matmul(out[:, lt * C:(lt + 1) * C], x_t[:, j, lt * P:(lt + 1) * P], wq[:, j, :],
                                                   start=(j == 0), stop=(j == CT - 1))
                        elif what == "kv":
                            for t in range(4 * i, min(4 * i + 4, ST)):
                                r = rows_of(t)
                                for j in range(CT):
                                    mm = pe.matmul(out[0:r, (t % 4) * P:(t % 4 + 1) * P], ctx_t[:, j, t * P:t * P + r],
                                                   wkv[:, j, :], start=(j == 0), stop=(j == CT - 1))
                        elif what == "qT":
                            if i == 0:
                                pe.wait_ge(q_split, b * 5 + 5)
                                pe.wait_ge(q_copied, b + 1)
                            for hh in range(GROUPS):
                                for lt in range(LT):
                                    pair = q_aug[:, lt, UH * i + 2 * hh:UH * i + 2 * hh + 2, :].rearrange("p h c -> p (h c)")
                                    at = hh * L + lt * P
                                    mm = pe.transpose(out_b[:, at:at + P], pair, ident_b[:])
                        else:
                            if i == 0:
                                pe.wait_ge(k_split, b * 5 + 5)
                                pe.wait_ge(k_copied, b + 1)
                            for t in range(8 * (i % 2), min(8 * (i % 2) + 8, ST)):
                                r = rows_of(t) + rows_of(t) % 2
                                at = (t % 8) * P
                                mm = pe.transpose(out_b[:, at:at + r],
                                                  k_aug[0:r, t, i - i % 2:i - i % 2 + 2, :].rearrange("p h c -> p (h c)"), ident_b[0:r, 0:r])
                        mm.then_inc(prep_full, 1)

                def row_max(b, u, n):
                    lt, half, hh, k = n // (2 * UH), n // UH % 2, n // 2 % GROUPS, n % 2
                    a = A_PER_UNIT * u + n
                    if a < 2:
                        pe.wait_ge(prep_act, b * PREP_ACT + PREP_ACT)
                        pe.wait_ge(prep_dve, b * PREP_DVE + PREP_DVE)
                    else:
                        pe.wait_ge(max_done, b * A_PER_BATCH + a)
                    for bank, s0 in enumerate(range(ACHUNK[k], ACHUNK[k + 1], BANK)):
                        s1 = min(s0 + BANK, ACHUNK[k + 1])
                        mm = pe.matmul(p_max[:, n % 2, bank, 0:s1 - s0], q_t[:, u, half, hh, lt * P:(lt + 1) * P],
                                       k_t[:, u, s0:s1], start=True, stop=True)
                    mm.then_inc(max_full, 1)

                def turn_maxima(b, u):
                    pe.wait_ge(pool_step, b * POOL_PER_BATCH + (POOL_START + 5 * (u + 1)))
                    side_bank_free(b)
                    for lt in range(LT):
                        mm = pe.transpose(p_side[0:24, :].bitcast(BF16)[:, lt * P:(lt + 1) * P],
                                          max_split[:, lt].rearrange("p a k h -> p (a k h)"), ident_b[:])
                    mm.then_inc(max_turned, 1)

                def scores(b, u, t, j, masked):
                    e = E_PER_UNIT * u + E_PER_TILE * t + j
                    half, r = j // 2, rows_of(t)
                    heads = slice(2 * (j % 2), 2 * (j % 2) + 2)
                    if t == 0 and j == 0:
                        pe.wait_ge(max_placed, b * (32 * UNITS) + (32 * (u + 1) + 16))
                    pe.wait_ge(exp_done, b * E_PER_BATCH + (e + 1))
                    out = p_sc[0:r, e % 2, :]
                    mm = pe.matmul(out, k_t[:, u, t * P:t * P + r], q_t[:, u, half, heads, :], start=True, stop=not masked)
                    if masked:
                        for h in range(2):
                            for lt in range(LT):
                                at = h * L + lt * P
                                mm = pe.matmul(out[:, at:at + P], mask_nat[:, lt, t * P:t * P + r], ident_f[:],
                                               start=False, stop=(lt == LT - 1 and h == 1))
                    mm.then_inc(sc_full, 1)

                def values(b, u, t):
                    r = rows_of(t)
                    pe.wait_ge(exp_done, b * E_PER_BATCH + (E_PER_UNIT * u + E_PER_TILE * (t + 1) + 2))
                    if t == 0:
                        pe.wait_ge(pv_copied, b * UNITS + (u + 1))
                    for j in range(4):
                        mm = pe.matmul(p_pv[32 * j:32 * j + 32, :], v_aug[0:r, t, 2 * u + j // 2, :], probs[0:r, t_buf(u, t), j, :],
                                       start=(t == 0), stop=(t == ST - 1), tile_position=(0, 32 * j))
                    mm.then_inc(pv_done, 1)

                def turn_output(b, u):
                    pe.wait_ge(pv_copied, b * UNITS + (u + 2))
                    side_bank_free(b)
                    for lt in range(LT):
                        for e in range(2):
                            k = 2 * lt + e
                            mm = pe.transpose(p_side[:, k * P:(k + 1) * P], pv_sb[:, e * L + lt * P:e * L + (lt + 1) * P], ident_f[:])
                    mm.then_inc(o_turned, 1)

                side_user = [None]

                def side_bank_free(b):
                    kind, u = side_user[0]
                    if kind == "flag":
                        pe.wait_ge(mask_flagged, b + 1)
                    elif kind == "turn":
                        pe.wait_ge(max_copied, b * UNITS + (u + 1))
                    else:
                        pe.wait_ge(o_done, b * UNITS + (u + 2))

                def batch(b, masked):
                    side_user[0] = ("flag", 0)
                    for kind, u, at in ORDER:
                        if kind == "max":
                            row_max(b, u, at)
                        elif kind == "exp":
                            scores(b, u, *at, masked)
                        elif kind == "values":
                            values(b, u, at)
                        elif kind == "turn":
                            turn_maxima(b, u)
                            side_user[0] = (kind, u)
                        elif kind == "normal":
                            turn_output(b, u)
                            side_user[0] = (kind, u)

                with pe.Fori(0, B) as b:
                    prep(b)
                    pe.wait_ge(mask_anyed, b + 1)
                    pe.wait_ge(o_done, b * UNITS + 1)
                    pe.matmul(p_side[0:1, 0:1], mask_any[:], ones_col[:], start=True, stop=True).then_inc(mask_counted, 1)
                    pe.wait_ge(const_ready, 1)
                    pe.wait_ge(mask_flagged, b + 1)
                    flag = pe.value_load(mask_flag[0:1, 0:1])
                    with pe.If(flag > 0):
                        batch(b, True)
                    with pe.Else():
                        batch(b, False)

            @block.scalar
            def _(act):
                act.dma_start(bq_row[:], bq.partition_broadcast(P)).then_inc(bias_in, 16)
                act.dma_start(bkv_row[:, 0:KVH * HD], bk.partition_broadcast(P)).then_inc(bias_in, 16)
                act.dma_start(bkv_row[:, KVH * HD:], bv.partition_broadcast(P)).then_inc(bias_in, 16)
                load_second_part(act, held, loads_in, a)
                act.sem_inc(exp_done, 2)
                act.sem_inc(pv_copied, 1)

                def copy_terms(b, aug, parts, split, copied):
                    for term, part in enumerate(parts):
                        first = parts.index(part)
                        if term != first:
                            act.wait_ge(split, b * 5 + (2 * part + 1))
                            last = act.activation(block_of(aug, term), block_of(aug, first), ACT.Copy)
                    last.then_inc(copied, 1)

                with act.Fori(0, B) as b:
                    for n, (what, i, who) in enumerate(PREP):
                        if (what, i) == ("qT", 0):
                            copy_terms(b, q_aug[:], Q_PART, q_split, q_copied)
                        elif (what, i) == ("kT", 0):
                            copy_terms(b, k_aug[:], K_PART, k_split, k_copied)
                        if who != "act":
                            continue
                        act.wait_ge(prep_full, b * len(PREP) + (n + 1))
                        src = ring[n % 4]
                        if what == "ctxT":
                            tiles = min(2, ST - 2 * i)
                            w = rows_of(2 * i)
                            ins = act.activation(
                                ctx_t[:, :, 2 * i * P:(2 * i + tiles) * P].rearrange("p j (t s) -> p t j s", s=P)[:, :, :, 0:w],
                                src[:, 0:tiles * CT * P].rearrange("p (t j s) -> p t j s", j=CT, s=P)[:, :, :, 0:w], ACT.Copy)
                        elif what == "xT":
                            ins = act.activation(x_t[:].rearrange("p j l -> p (j l)"), src, ACT.Copy)
                        else:
                            for to, of in operand(what, i, src):
                                ins = act.activation(to, of, ACT.Copy)
                        ins.then_inc(prep_act, 1)
                    act.wait_ge(mask_loaded, b * 16 + 16)
                    act.activation(mask_abs[:], mask_nat[:], ACT.Abs, accum_out=mask_sum[:]).then_inc(mask_summed, 1)
                    for kind, u, at in ORDER:
                        if kind == "exp":
                            t, j = at
                            r, e = rows_of(t), E_PER_UNIT * u + E_PER_TILE * t + j
                            act.wait_ge(sc_full, b * E_PER_BATCH + (e + 1))
                            if j == 0:
                                act.wait_ge(pv_done, b * (UNITS * ST) + (ST * u + t + 1))
                            act.activation(probs[0:r, t_buf(u, t), j, :], p_sc[0:r, e % 2, :], ACT.Exp).then_inc(exp_done, 1)
                        elif kind == "turn":
                            act.wait_ge(max_turned, b * UNITS + (u + 2))
                            act.wait_ge(max_placed, b * (32 * UNITS) + (32 * u + 16))
                            act.activation(max_t[:], p_side[0:24, :].bitcast(BF16)[:, 0:L], ACT.Copy).then_inc(max_copied, 1)
                        elif kind == "copy":
                            act.wait_ge(pv_done, b * (UNITS * ST) + (ST * (u + 1) + 2))
                            act.wait_ge(o_turned, b * UNITS + (u + 1))
                            act.activation(pv_sb[:], p_pv[:], ACT.Copy).then_inc(pv_copied, 1)

            @block.vector
            def _(dve):
                dve.sem_inc(max_done, 1)
                dve.sem_inc(o_done, 1)
                dve.memset(q_aug[:], 0.0).then_inc(operands_clear, 1)
                dve.memset(k_aug[:], 0.0).then_inc(operands_clear, 1)
                dve.memset(k_f[:], 0.0).then_inc(operands_clear, 1)
                dve.memset(q_t[:], 0.0).then_inc(operands_clear, 1)
                dve.wait_ge(operands_clear, 4)
                dve.memset(k_aug[:, :, :, TERMS * HD:TERMS * HD + 3], 1.0).then_inc(operands_clear, 1)
                dve.wait_ge(const_ready, 1)
                dve.wait_ge(operands_clear, 5)
                dve.wait_ge(bias_in, 48)
                dve.tensor_scalar(bq_row[:], bq_row[:], SCALE, None, ALU.mult).then_inc(bias_scaled, 1)
                dve.wait_ge(bias_scaled, 1)

                def split(b, full, rest, aug, parts, done):
                    value = full.rearrange("p (h d) -> p h d", d=HD)
                    for k in range(3):
                        part = block_of(aug, parts.index(k))
                        dve.tensor_copy(part, value).then_inc(done, 1)
                        dve.wait_ge(done, b * 5 + (2 * k + 1))
                        if k < 2:
                            left = rest[:, k, :].rearrange("p (h d) -> p h d", d=HD)
                            dve.tensor_tensor(left, value, part, ALU.subtract).then_inc(done, 1)
                            dve.wait_ge(done, b * 5 + (2 * k + 2))
                            value = left

                with dve.Fori(0, B) as b:
                    for n, (what, i, who) in enumerate(PREP):
                        if who != "dve":
                            continue
                        dve.wait_ge(prep_full, b * len(PREP) + (n + 1))
                        src = ring[n % 4]
                        if what == "q":
                            for lt in range(LT):
                                for half in range(2):
                                    def cols(ap, order):
                                        return ap.rearrange(order, u=UNITS, half=2, h=GROUPS)
                                    ins = dve.scalar_tensor_tensor(
                                        out=cols(q_f[:, lt * C:(lt + 1) * C], "p (u h half d) -> p u h half d")[:, :, :, half, :],
                                        in0=cols(src[:, lt * C:(lt + 1) * C], "p (u half h d) -> p u half h d")[:, :, half, :, :],
                                        scalar=SCALE, in1=cols(bq_row[:], "p (u half h d) -> p u half h d")[:, :, half, :, :],
                                        op0=ALU.mult, op1=ALU.add)
                        elif what == "kv":
                            tiles, r, w = min(4, ST - 4 * i), rows_of(4 * i), KVH * HD
                            both = src[0:r, 0:tiles * P].rearrange("p (t n) -> p t n", n=P)
                            bias = bkv_row[0:r, :].unsqueeze(1).to_broadcast([r, tiles, P])
                            dve.tensor_tensor(k_f[0:r, 4 * i:4 * i + tiles, :], both[:, :, 0:w], bias[:, :, 0:w], ALU.add)
                            ins = dve.tensor_tensor(v_aug[0:r, 4 * i:4 * i + tiles, :, 0:HD],
                                                    both[:, :, w:].rearrange("p t (h d) -> p t h d", d=HD),
                                                    bias[:, :, w:].rearrange("p t (h d) -> p t h d", d=HD), ALU.add)
                        else:
                            for to, of in operand(what, i, src):
                                ins = dve.tensor_copy(to, of)
                        ins.then_inc(prep_dve, 1)
                        if what == "q":
                            dve.wait_ge(prep_dve, b * PREP_DVE + 1)
                            split(b, q_f[:], q_part, q_aug[:], Q_PART, q_split)
                        elif (what, i) == ("kv", -(-ST // 4) - 1):
                            dve.wait_ge(prep_dve, b * PREP_DVE + (1 + -(-ST // 4)))
                            split(b, k_f[:].rearrange("p t n -> p (t n)"), k_part, k_aug[:], K_PART, k_split)
                    dve.wait_ge(mask_summed, b + 1)
                    dve.tensor_scalar(mask_any[:], mask_sum[:], 0.0, None, ALU.is_gt).then_inc(mask_anyed, 1)
                    dve.wait_ge(mask_counted, b + 1)
                    dve.tensor_scalar(mask_flag[:], p_side[0:1, 0:1], 0.5, None, ALU.is_gt).then_inc(mask_flagged, 1)
                    for kind, u, at in ORDER:
                        if kind == "max":
                            lt, half, hh, k = at // (2 * UH), at // UH % 2, at // 2 % GROUPS, at % 2
                            lo, hi = ACHUNK[k], ACHUNK[k + 1]
                            dve.wait_ge(max_full, b * A_PER_BATCH + (A_PER_UNIT * u + at + 1))
                            dve.sem_inc(max_seen, 1)
                            sc = p_max[:, at % 2].rearrange("p a n -> p (a n)")[:, 0:hi - lo]
                            dve.tensor_tensor_reduce(sc, sc, mask_nat[:, lt, lo:hi], 1.0, NEG, ALU.add, ALU.max,
                                                     max_part[:, lt, half, hh, k:k + 1]).then_inc(max_done, 1)
                            if at == A_PER_UNIT - 1:
                                dve.wait_ge(max_done, b * A_PER_BATCH + (A_PER_UNIT * (u + 1) + 1))
                                if u:
                                    dve.wait_ge(pool_step, b * POOL_PER_BATCH + (POOL_START + 5 * u))
                                dve.tensor_reduce(neg_max[:], max_part[:], AX.X, ALU.max, negate=True).then_inc(max_ready, 1)
                                dve.wait_ge(max_ready, b * UNITS + (u + 1))
                        elif kind == "normal":
                            dve.wait_ge(o_turned, b * UNITS + (u + 2))
                            turned = p_side[:].rearrange("p (t e j c) -> p t e j c", t=LT, e=2, j=4)
                            dve.reciprocal(row_sum[:].rearrange("p t e j -> p (t e) j"),
                                           p_side[:].rearrange("p (k j c) -> p k j c", k=4, j=4)[:, :, :, HD]).then_inc(o_summed, 1)
                            dve.wait_ge(o_summed, b * UNITS + (u + 1))
                            for lt in range(LT):
                                ins = dve.tensor_tensor(
                                    o_nat[:, b, lt, UH * HD * u:UH * HD * (u + 1)].rearrange("p (j e d) -> p e j d", e=2, d=HD),
                                    turned[:, lt, :, :, 0:HD],
                                    row_sum[:, lt].unsqueeze(3).to_broadcast([P, 2, 4, HD]), ALU.mult)
                            ins.then_inc(o_done, 1)



STAGES = [("turn_w", 8, "act"), ("turn_vec", 1, "act"), ("turn_o", B, "act"), ("out0", B, "dve"), ("turn_x", B, "dve"),
          ("mix", 4, "act"), ("m0", 4, "dve"), ("m1", 4, "dve"), ("dec1", 2, "act"), ("m2", 4, "dve"), ("dec2", 4, "act"),
          ("p1", 4, "act"), ("m3", 4, "dve"), ("p2", 4, "act"), ("m4", 4, "dve"), ("p3", 4, "act"), ("p4", 4, "act"),
          ("own", 4, "dve")]
for _n in range(CT * B):
    STAGES.append((f"vb{_n}", 4, "dve"))
    if _n:
        STAGES.append((f"y{_n - 1}", 1, "dve"))
STAGES += [(f"y{CT * B - 1}", 1, "dve"), ("mean", 4, "dve"), ("var", 4, "act"), ("out1", B, "dve"), ("turn_c", B, "dve"),
           ("fk", 4, "act"), ("fr", B, "act"), ("fv", B, "dve")]
FIRST, ROUNDS = {}, []
for _name, _count, _who in STAGES:
    FIRST[_name] = len(ROUNDS)
    ROUNDS += [(_name, n) for n in range(_count)]
COUNT = {name: count for name, count, _ in STAGES}


def mixing(nc, sem, held, loads_in, out):
    with ExitStack() as here:
        def sb(name, shape, dt=F32):
            return here.enter_context(nc.sbuf_tensor(name, shape, dt))

        ident, x_nat, o_nat, rows = held["ident_f"], held["x_nat"], held["o_nat"], held["rows"]
        w_t = sb("w_t", [P, len(TURNED), CT, C])
        cols = sb("cols", [P, CT * len(VECTORS)])
        state = sb("state", [P, CT, 2 * B])
        spread = sb("spread", [P, HD, NH // 2, HD])
        gather = sb("gather", [P, HD, NH // 2, HD])
        heads = sb("heads", [P, NH // 2, HD])
        eighth = sb("eighth", [P, NH // 2, HD])
        eps_col = sb("eps_col", [P, 1])
        power = sb("power", [P, B * LT])
        stats = sb("stats", [P, B * LT, 6])
        moments = sb("moments", [P, B * LT, 2])
        var_eps = sb("var_eps", [P, B * LT])
        rstd = sb("rstd", [P, B * LT])
        xa_t = sb("xa_t", [P, CT, B, L + 1])
        sx = sb("sx", [P, CT, B, L])
        xxx = sb("xxx", [P, CT, B, L])
        k_all = sb("k_all", [P, CT, B, L])
        v_all = sb("v_all", [P, CT, B, L])
        r_all = sb("r_all", [P, CT, B, L])
        g_all = sb("g_all", [P, CT, B, L])
        w_all = sb("w_all", [P, CT, B, L])
        area = sb("area", [P, 6 * HD * (L + 1)])
        bank = [here.enter_context(nc.psum_tensor(f"bank{n}", [P, BANK], F32)) for n in range(8)]

        FULL = CT * B * L

        def wide(n):
            return area[:, n * FULL:(n + 1) * FULL].rearrange("p (j b l) -> p j b l", j=CT, b=B)

        mixed = [wide(n) for n in range(3)]
        o_t = wide(3)
        lo_rank = area[:, 4 * FULL:4 * FULL + B * L]
        lo_last = area[:, 4 * FULL + B * L:5 * FULL]
        dec = area[:, 5 * FULL:5 * FULL + B * L]
        pad = HD * (L + 1)
        kv_in, states, read = ([area[:, (2 * k + n) * pad:(2 * k + n + 1) * pad].rearrange("p (t l) -> p t l", t=HD)
                                for n in range(2)] for k in range(3))

        def col(name, j):
            n = CT * VECTORS.index(name) + j
            return cols[:, n:n + 1]

        full = {name: sem(f"{name}_full") for name in COUNT}
        done = {name: sem(f"{name}_done") for name in COUNT}
        const_ready2 = sem("const_ready2")
        const_step = sem("const_step")
        bo_added = sem("bo_added")
        ln_stats = sem("ln_stats")
        ln_moments = sem("ln_moments")
        ln_eps = sem("ln_eps")
        ln_rstd = sem("ln_rstd")
        ln_applied = sem("ln_applied")
        gamma_done = sem("gamma_done")
        x1_ready = sem("x1_ready")
        shift_ready = sem("shift_ready")
        sx_ready = sem("sx_ready")
        xxx_ready = sem("xxx_ready")
        mixed_ready = [sem(f"mixed_ready{f}") for f in range(MIXES)]
        w_ready = sem("w_ready")
        silu_ready = sem("silu_ready")
        rku_ready = sem("rku_ready")
        s0_placed = sem("s0_placed")
        scanned = sem("scanned")
        read_ready = sem("read_ready")
        squared = sem("squared")
        inverted = sem("inverted")
        normed = sem("normed")
        scaled = sem("scaled")
        z_ready = sem("z_ready")
        shift2_ready = sem("shift2_ready")
        sx2_ready = sem("sx2_ready")
        ffn_in = sem("ffn_in")
        kk_ready = sem("kk_ready")
        out_ready = sem("out_ready")
        gn_halved = sem("gn_halved")
        stored = sem("stored")
        n_loads = 10 + len(TURNED) + len(VECTORS) + 2 * B

        def two(ap, n):
            return ap[:, 2 * n:2 * n + 2, :]

        def half(ps):
            return ps.rearrange("p (b l) -> p b l", b=2)

        def place(n):
            return n // 2, n % 2

        with nc.Block() as block:

            x_hat = area[:, 3 * FULL:4 * FULL].rearrange("p (b t c) -> p b t c", b=B, t=LT)

            def product(pool, n):
                j, b = n // B, n % B
                pool.wait_ge(scanned, n + 1)
                if n >= 2:
                    pool.wait_ge(full[f"y{n - 2}"], 1)
                pool.tensor_tensor(read[n % 2][:, :, 0:L], states[n % 2][:, :, 0:L],
                                   r_all[:, j, b, :].unsqueeze(1).to_broadcast([P, HD, L]), ALU.mult).then_inc(read_ready, 1)

            @block.gpsimd
            def _(pool):
                for m, v in ((spread, 0.0), (gather, 1.0), (heads, 1.0)):
                    pool.memset(m[:], v).then_inc(const_step, 1)
                pool.memset(eps_col[:], EPS1)
                pool.memset(power[:], -0.5)
                pool.wait_ge(const_step, 3)
                pool.affine_select(out=spread[:], in_=spread[:], compare_op=ALU.not_equal, fill=1.0, base=0,
                                   pattern=[[-1, HD], [-HD, NH // 2], [0, HD]], channel_multiplier=1).then_inc(const_step, 1)
                steps = 4
                for m, pattern in ((heads, [[HD, NH // 2], [0, HD]]), (gather, [[0, HD], [HD, NH // 2], [0, HD]])):
                    pool.affine_select(out=m[:], in_=m[:], compare_op=ALU.is_ge, fill=0.0, base=0,
                                       pattern=[[-step, n] for step, n in pattern], channel_multiplier=1).then_inc(const_step, 1)
                    steps += 1
                    pool.wait_ge(const_step, steps)
                    pool.affine_select(out=m[:], in_=m[:], compare_op=ALU.is_ge, fill=0.0, base=HD - 1,
                                       pattern=pattern, channel_multiplier=-1).then_inc(const_step, 1)
                    steps += 1
                    pool.wait_ge(const_step, steps)
                pool.affine_select(out=gather[:], in_=gather[:], compare_op=ALU.is_equal, fill=0.0, base=0,
                                   pattern=[[1, HD], [0, NH // 2], [-1, HD]], channel_multiplier=0)
                pool.tensor_scalar(eighth[:], heads[:], 1.0 / HD, None, ALU.mult).then_inc(const_ready2, 1)
                pool.wait_ge(loads_in, 16 * n_loads)
                pool.tensor_tensor(x_nat[:].rearrange("p b t c -> p (b t) c"), x_nat[:].rearrange("p b t c -> p (b t) c"),
                                   rows[:, 0, :].unsqueeze(1).to_broadcast([P, B * LT, C]), ALU.add).then_inc(bo_added, 1)

                def root(n):
                    pool.wait_ge(ln_eps, n + 1)
                    pool.tensor_tensor(rstd[:], var_eps[:], power[:], ALU.pow).then_inc(ln_rstd, 1)

                root(0)
                root(1)
                pool.wait_ge(done["turn_vec"], 1)
                for j in range(CT):
                    ins = pool.tensor_scalar(xa_t[:, j, :, 0], state[:, j, 1:2 * B:2], 1.0, None, ALU.mult)
                ins.then_inc(shift_ready, 1)
                for f in range(MIXES):
                    for n in range(4):
                        nb, j = place(n)
                        pool.wait_ge(done[f"m{f}"], n + 1)
                        x_f = two(mixed[f % 3][:, j], nb)
                        pool.tensor_tensor(x_f, x_f, two(xa_t[:, j], nb)[:, :, 1:], ALU.add).then_inc(mixed_ready[f], 1)
                for n in range(CT * B):
                    j, b = n // B, n % B
                    if n < 2:
                        for f in range(1, MIXES):
                            pool.wait_ge(full[f"p{f}"], COUNT[f"p{f}"])
                        pool.wait_ge(full["own"], COUNT["own"])
                    else:
                        pool.wait_ge(read_ready, n - 1)
                    pool.tensor_scalar(states[n % 2][:, :, 0], held["s0"][:, j, b, :], 1.0, None, ALU.mult).then_inc(s0_placed, 1)
                    if n:
                        product(pool, n - 1)
                product(pool, CT * B - 1)
                root(2)

            @block.tensor
            def _(pe):
                pe.wait_ge(loads_in, 16 * n_loads)

                at = [0]

                def next_bank():
                    n = at[0]
                    at[0] += 1
                    if n >= 8:
                        name, k = ROUNDS[n - 8]
                        pe.wait_ge(done[name], k + 1)
                    return bank[n % 8]

                def starts(name):
                    assert at[0] == FIRST[name], (name, at[0])

                def turned(name, n, source):
                    out = next_bank()
                    for lt in range(LT):
                        for j in range(CT):
                            mm = pe.transpose(out[:, j * L + lt * P:j * L + (lt + 1) * P], source[:, n, lt, j * P:(j + 1) * P], ident[:])
                    mm.then_inc(full[name], 1)

                def rows_out(name, n, source, weight):
                    out = next_bank()
                    for lt in range(LT):
                        for j in range(CT):
                            mm = pe.matmul(out[:, lt * C:(lt + 1) * C], source[:, j, n, lt * P:(lt + 1) * P], weight[:, j, :],
                                           start=(j == 0), stop=(j == CT - 1))
                    mm.then_inc(full[name], 1)

                def channels_out(name, n, source, weight):
                    nb, jo = place(n)
                    out = next_bank()
                    for j in range(CT):
                        mm = pe.matmul(half(out), weight[:, j, jo * P:(jo + 1) * P], two(source[:, j], nb),
                                       start=(j == 0), stop=(j == CT - 1))
                    mm.then_inc(full[name], 1)

                for k in range(len(TURNED)):
                    out = next_bank()
                    for jo in range(CT):
                        for j in range(CT):
                            mm = pe.transpose(out[:, j * C + jo * P:j * C + (jo + 1) * P], held["w_nat"][:, k, jo, j * P:(j + 1) * P], ident[:])
                    mm.then_inc(full["turn_w"], 1)
                out = next_bank()
                V = CT * len(VECTORS)
                pe.transpose(out[:, 0:V], held["vec_nat"][:], ident[0:V, 0:V])
                for j in range(CT):
                    mm = pe.transpose(out[:, V + 2 * B * j:V + 2 * B * (j + 1)], held["state_nat"][:, j * P:(j + 1) * P], ident[0:2 * B, 0:2 * B])
                mm.then_inc(full["turn_vec"], 1)
                for b in range(B):
                    turned("turn_o", b, o_nat)
                for b in range(B):
                    pe.wait_ge(done["turn_o"], b + 1)
                    rows_out("out0", b, o_t, held["wo"])
                pe.wait_ge(ln_applied, 2)
                for b in range(B):
                    turned("turn_x", b, x_hat)
                starts("mix")
                pe.wait_ge(xxx_ready, CT)
                for n in range(4):
                    nb, last = n % 2, n // 2
                    out = next_bank()
                    lo, hi = ((MIXES - 1) * DM, MIXES * DM) if last else (0, (MIXES - 1) * DM)
                    for j in range(CT):
                        mm = pe.matmul(half(out[0:hi - lo, :]), held["maa_w1"][:, j, lo:hi], two(xxx[:, j], nb), start=(j == 0), stop=(j == CT - 1))
                    mm.then_inc(full["mix"], 1)

                def mix(f):
                    for n in range(4):
                        nb, j = place(n)
                        out = next_bank()
                        if f < MIXES - 1:
                            pe.wait_ge(done["mix"], nb + 1)
                            w, t = held["maa_w2"][f * DM:(f + 1) * DM, :], lo_rank[f * DM:(f + 1) * DM, :]
                        else:
                            pe.wait_ge(done["mix"], nb + 3)
                            w, t = held["maa_w2_last"][:], lo_last[0:DM, :]
                        pe.matmul(out[:], w[:, j * P:(j + 1) * P], t[:, nb * BANK:(nb + 1) * BANK], start=True, stop=True)\
                            .then_inc(full[f"m{f}"], 1)

                def project(f):
                    pe.wait_ge(done["turn_w"], f)
                    for n in range(4):
                        pe.wait_ge(mixed_ready[f], 2 * (n // 2) + 2)
                        channels_out(f"p{f}", n, mixed[f % 3], w_t[:, f - 1])

                mix(0)
                mix(1)
                starts("dec1")
                for n in range(2):
                    pe.wait_ge(mixed_ready[0], 2 * n + 2)
                    out = next_bank()
                    for j in range(CT):
                        mm = pe.matmul(half(out[0:DD, :]), held["decay_w1"][:, j, :], two(mixed[0][:, j], n), start=(j == 0), stop=(j == CT - 1))
                    mm.then_inc(full["dec1"], 1)
                mix(2)
                for n in range(4):
                    nb, j = place(n)
                    pe.wait_ge(done["dec1"], nb + 1)
                    out = next_bank()
                    pe.matmul(out[:], held["decay_w2"][:, j * P:(j + 1) * P], dec[0:DD, nb * BANK:(nb + 1) * BANK], start=True, stop=True)\
                        .then_inc(full["dec2"], 1)
                project(1)
                mix(3)
                project(2)
                mix(4)
                project(3)
                project(4)
                starts("own")
                pe.wait_ge(const_ready2, 1)
                for n in range(4):
                    nb, j = place(n)
                    pe.wait_ge(rku_ready, j + 1)
                    out = next_bank()
                    pe.matmul(half(out), heads[:].rearrange("p h s -> p (h s)"), two(mixed[2][:, j], nb), start=True, stop=True)\
                        .then_inc(full["own"], 1)

                def values_of(n):
                    j, b = n // B, n % B
                    for i in range(4):
                        out = next_bank()
                        for t in range(2):
                            mm = pe.matmul(out[:, t * L:(t + 1) * L], spread[:, 2 * i + t].rearrange("p h s -> p (h s)"), v_all[:, j, b, :],
                                           start=True, stop=True)
                        mm.then_inc(full[f"vb{n}"], 1)

                def summed(n):
                    pe.wait_ge(read_ready, n + 1)
                    out = next_bank()
                    for t in range(HD):
                        mm = pe.matmul(out[:, 0:L], gather[:, t].rearrange("p h s -> p (h s)"), read[n % 2][:, t, 0:L],
                                       start=(t == 0), stop=(t == HD - 1))
                    mm.then_inc(full[f"y{n}"], 1)

                for n in range(CT * B):
                    values_of(n)
                    if n:
                        summed(n - 1)
                summed(CT * B - 1)
                starts("mean")
                for name, source, sem_in in (("mean", xxx, done[f"y{CT * B - 1}"]), ("var", r_all, squared)):
                    for n in range(4):
                        nb, j = place(n)
                        pe.wait_ge(sem_in, 1 if name == "mean" else n + 1)
                        out = next_bank()
                        pe.matmul(half(out), eighth[:].rearrange("p h s -> p (h s)"), two(source[:, j], nb), start=True, stop=True)\
                            .then_inc(full[name], 1)
                for b in range(B):
                    pe.wait_ge(z_ready, 2 * (b // 2) + 2)
                    rows_out("out1", b, k_all, w_t[:, TURNED.index("Wo")])
                pe.wait_ge(ln_applied, 3)
                for b in range(B):
                    turned("turn_c", b, x_hat)
                for n in range(4):
                    pe.wait_ge(ffn_in, CT)
                    channels_out("fk", n, r_all, w_t[:, TURNED.index("fWk")])
                for b in range(B):
                    pe.wait_ge(ffn_in, 2 * CT)
                    rows_out("fr", b, v_all, w_t[:, TURNED.index("fWr")])
                for b in range(B):
                    pe.wait_ge(kk_ready, 2 * (b // 2) + 2)
                    rows_out("fv", b, k_all, w_t[:, TURNED.index("fWv")])
                assert at[0] == len(ROUNDS)

            def of_round(name, n):
                return bank[(FIRST[name] + n) % 8]

            @block.scalar
            def _(act):
                def each(name):
                    for n in range(COUNT[name]):
                        act.wait_ge(full[name], n + 1)
                        yield n, of_round(name, n)

                for n, ps in each("turn_w"):
                    act.activation(w_t[:, n].rearrange("p j c -> p (j c)"), ps[:], ACT.Copy).then_inc(done["turn_w"], 1)
                V = CT * len(VECTORS)
                for n, ps in each("turn_vec"):
                    act.activation(cols[:], ps[:, 0:V], ACT.Copy)
                    act.activation(state[:].rearrange("p j n -> p (j n)"), ps[:, V:V + 2 * B * CT], ACT.Copy).then_inc(done["turn_vec"], 1)
                act.wait_ge(done["turn_vec"], 1)
                lo, hi = CT * VECTORS.index("gn_w"), CT * VECTORS.index("gn_b") + CT
                act.activation(cols[:, lo:hi], cols[:, lo:hi], ACT.Copy, scale=0.5).then_inc(gn_halved, 1)
                for n, ps in each("turn_o"):
                    act.activation(o_t[:, :, n, :], ps[:].rearrange("p (j l) -> p j l", j=CT), ACT.Copy).then_inc(done["turn_o"], 1)
                for n, ps in each("mix"):
                    nb, last = n % 2, n // 2
                    to = (lo_last[0:DM] if last else lo_rank)[:, nb * BANK:(nb + 1) * BANK]
                    act.activation(to, ps[0:DM, :] if last else ps[:], ACT.Tanh).then_inc(done["mix"], 1)
                for n, ps in each("dec1"):
                    act.activation(dec[0:DD, n * BANK:(n + 1) * BANK], ps[0:DD, :], ACT.Tanh).then_inc(done["dec1"], 1)
                for n, ps in each("dec2"):
                    nb, j = place(n)
                    w = two(w_all[:, j], nb)
                    act.activation(w, half(ps), ACT.Exp, bias=col("time_decay", j)).then_inc(done["dec2"], 1)
                    act.wait_ge(done["dec2"], n + 1)
                    act.activation(w, w, ACT.Exp, scale=-1.0).then_inc(w_ready, 1)
                for f, to in ((1, k_all), (2, v_all), (3, r_all), (4, g_all)):
                    for n, ps in each(f"p{f}"):
                        nb, j = place(n)
                        if f < 4:
                            act.activation(two(to[:, j], nb), half(ps), ACT.Copy).then_inc(done[f"p{f}"], 1)
                        else:
                            act.activation(two(to[:, j], nb), half(ps), ACT.Copy)
                            act.activation(two(xxx[:, j], nb), half(ps), ACT.Tanh, scale=0.5).then_inc(done[f"p{f}"], 1)
                for n in range(4):
                    nb, j = place(n)
                    act.wait_ge(done["mean"], n + 1)
                    act.activation(two(r_all[:, j], nb), two(k_all[:, j], nb), ACT.Square).then_inc(squared, 1)
                for n, ps in each("var"):
                    nb, j = place(n)
                    act.activation(two(v_all[:, j], nb), half(ps), ACT.Sqrt, bias=eps_col[:]).then_inc(done["var"], 1)
                for n, ps in each("fk"):
                    nb, j = place(n)
                    act.activation(two(k_all[:, j], nb), half(ps), ACT.Relu).then_inc(done["fk"], 1)
                    act.wait_ge(done["fk"], n + 1)
                    act.activation(two(k_all[:, j], nb), two(k_all[:, j], nb), ACT.Square).then_inc(kk_ready, 1)
                for n, ps in each("fr"):
                    act.activation(g_all[:].rearrange("p j b l -> p (j b l)")[:, n * BANK:(n + 1) * BANK], ps[:], ACT.Tanh, scale=0.5)\
                        .then_inc(done["fr"], 1)

            @block.vector
            def _(dve):
                def each(name):
                    for n in range(COUNT[name]):
                        dve.wait_ge(full[name], n + 1)
                        yield n, of_round(name, n)

                def norm(n, source, to, eps):
                    for k in range(B * LT):
                        ins = dve.bn_stats(stats[:, k, :], source[:, k // LT, k % LT, :])
                    ins.then_inc(ln_stats, 1)
                    dve.wait_ge(ln_stats, n + 1)
                    for k in range(B * LT):
                        ins = dve.bn_aggr(moments[:, k, :], stats[:, k, :])
                    ins.then_inc(ln_moments, 1)
                    dve.wait_ge(ln_moments, n + 1)
                    dve.tensor_scalar(var_eps[:], moments[:, :, 1], eps, None, ALU.add).then_inc(ln_eps, 1)
                    dve.wait_ge(ln_rstd, n + 1)
                    for k in range(B * LT):
                        ins = dve.tensor_scalar(to[:, k // LT, k % LT, :], source[:, k // LT, k % LT, :], moments[:, k, 0:1], rstd[:, k:k + 1],
                                                ALU.subtract, ALU.mult)
                    ins.then_inc(ln_applied, 1)
                    dve.wait_ge(ln_applied, n + 1)

                def all_rows(ap):
                    return ap.rearrange("p b t c -> p (b t) c")

                def row(n):
                    return rows[:, n, :].unsqueeze(1).to_broadcast([P, B * LT, C])

                dve.wait_ge(bo_added, 1)
                for b, ps in each("out0"):
                    dve.tensor_tensor(x_nat[:, b], ps[:].rearrange("p (t c) -> p t c", t=LT), x_nat[:, b], ALU.add).then_inc(done["out0"], 1)
                dve.wait_ge(done["out0"], B)
                norm(0, x_nat, o_nat, EPS0)
                dve.tensor_tensor(all_rows(o_nat[:]), all_rows(o_nat[:]), row(1), ALU.mult).then_inc(gamma_done, 1)
                dve.wait_ge(gamma_done, 1)
                dve.tensor_tensor(all_rows(o_nat[:]), all_rows(o_nat[:]), row(2), ALU.add).then_inc(x1_ready, 1)
                dve.wait_ge(x1_ready, 1)
                norm(1, o_nat, x_hat, EPS1)
                dve.wait_ge(shift_ready, 1)
                for b, ps in each("turn_x"):
                    for j in range(CT):
                        ins = dve.tensor_scalar(xa_t[:, j, b, 1:], ps[:, j * L:(j + 1) * L], col("ln1_w", j), col("ln1_b", j), ALU.mult, ALU.add)
                    ins.then_inc(done["turn_x"], 1)
                dve.wait_ge(done["turn_x"], B)
                dve.tensor_tensor(sx[:].rearrange("p j b l -> p (j b) l"), xa_t[:, :, :, 0:L].rearrange("p j b l -> p (j b) l"),
                                  xa_t[:, :, :, 1:].rearrange("p j b l -> p (j b) l"), ALU.subtract).then_inc(sx_ready, 1)
                dve.wait_ge(sx_ready, 1)
                for j in range(CT):
                    dve.scalar_tensor_tensor(out=xxx[:, j], in0=sx[:, j], scalar=col("maa_x", j), in1=xa_t[:, j, :, 1:],
                                             op0=ALU.mult, op1=ALU.add).then_inc(xxx_ready, 1)

                def mix(f):
                    if f >= 3:
                        dve.wait_ge(full["dec1" if f == 3 else "p1"], COUNT["dec1" if f == 3 else "p1"])
                    for n, ps in each(f"m{f}"):
                        nb, j = place(n)
                        dve.scalar_tensor_tensor(out=two(mixed[f % 3][:, j], nb), in0=half(ps), scalar=col("maa_" + "wkvrg"[f], j),
                                                 in1=two(sx[:, j], nb), op0=ALU.add, op1=ALU.mult).then_inc(done[f"m{f}"], 1)

                for f in range(MIXES):
                    mix(f)
                dve.wait_ge(done["p1"], 4)
                dve.wait_ge(done["p3"], 4)
                dve.wait_ge(full["p2"], 4)
                for j in range(CT):
                    dve.scalar_tensor_tensor(out=mixed[2][:, j], in0=r_all[:, j], scalar=col("faaaa", j), in1=k_all[:, j],
                                             op0=ALU.mult, op1=ALU.mult).then_inc(rku_ready, 1)
                dve.wait_ge(done["p2"], 4)
                for n, ps in each("own"):
                    nb, j = place(n)
                    dve.tensor_tensor(two(sx[:, j], nb), half(ps), two(v_all[:, j], nb), ALU.mult).then_inc(done["own"], 1)
                dve.wait_ge(done["p4"], 4)
                dve.scalar_tensor_tensor(out=g_all[:], in0=xxx[:], scalar=1.0, in1=g_all[:], op0=ALU.add, op1=ALU.mult).then_inc(silu_ready, 1)
                dve.wait_ge(w_ready, 4)
                dve.wait_ge(silu_ready, 1)

                def recur(n):
                    j, b = n // B, n % B
                    dve.wait_ge(s0_placed, n + 1)
                    for i, ps in each(f"vb{n}"):
                        dve.tensor_tensor(kv_in[n % 2][:, 2 * i:2 * i + 2, 0:L], half(ps),
                                          k_all[:, j, b, :].unsqueeze(1).to_broadcast([P, 2, L]), ALU.mult).then_inc(done[f"vb{n}"], 1)
                    dve.wait_ge(done[f"vb{n}"], 4)
                    if n >= 2:
                        dve.wait_ge(read_ready, n - 1)
                    for t in range(HD):
                        ins = dve.tensor_tensor_scan(states[n % 2][:, t, 1:], w_all[:, j, b, :], kv_in[n % 2][:, t, 0:L],
                                                     states[n % 2][:, t, 0:1], ALU.mult, ALU.add)
                    ins.then_inc(scanned, 1)

                def add_own(n):
                    j, b = n // B, n % B
                    for _, ps in each(f"y{n}"):
                        dve.tensor_tensor(xxx[:, j, b, :], ps[:, 0:L], sx[:, j, b, :], ALU.add).then_inc(done[f"y{n}"], 1)

                for n in range(CT * B):
                    recur(n)
                    if n:
                        add_own(n - 1)
                add_own(CT * B - 1)
                dve.wait_ge(done[f"y{CT * B - 1}"], 1)
                for n, ps in each("mean"):
                    nb, j = place(n)
                    dve.tensor_tensor(two(k_all[:, j], nb), two(xxx[:, j], nb), half(ps), ALU.subtract).then_inc(done["mean"], 1)
                dve.wait_ge(gn_halved, 1)
                for n in range(4):
                    nb, j = place(n)
                    dve.wait_ge(done["var"], n + 1)
                    v, d = two(v_all[:, j], nb), two(k_all[:, j], nb)
                    dve.reciprocal(v, v).then_inc(inverted, 1)
                    dve.wait_ge(inverted, n + 1)
                    dve.wait_ge(squared, n + 1)
                    dve.tensor_tensor(d, d, v, ALU.mult).then_inc(normed, 1)
                    dve.wait_ge(normed, n + 1)
                    dve.tensor_scalar(d, d, col("gn_w", j), col("gn_b", j), ALU.mult, ALU.add).then_inc(scaled, 1)
                    dve.wait_ge(scaled, n + 1)
                    dve.tensor_tensor(d, d, two(g_all[:, j], nb), ALU.mult).then_inc(z_ready, 1)
                for b, ps in each("out1"):
                    dve.tensor_tensor(x_nat[:, b], ps[:].rearrange("p (t c) -> p t c", t=LT), o_nat[:, b], ALU.add).then_inc(done["out1"], 1)
                dve.wait_ge(done["out1"], B)
                for j in range(CT):
                    ins = dve.tensor_copy(xa_t[:, j, :, 0], state[:, j, 0:2 * B:2])
                ins.then_inc(shift2_ready, 1)
                norm(2, x_nat, x_hat, EPS1)
                for b, ps in each("turn_c"):
                    for j in range(CT):
                        ins = dve.tensor_scalar(xa_t[:, j, b, 1:], ps[:, j * L:(j + 1) * L], col("ln2_w", j), col("ln2_b", j), ALU.mult, ALU.add)
                    ins.then_inc(done["turn_c"], 1)
                dve.wait_ge(done["turn_c"], B)
                dve.tensor_tensor(sx[:].rearrange("p j b l -> p (j b) l"), xa_t[:, :, :, 0:L].rearrange("p j b l -> p (j b) l"),
                                  xa_t[:, :, :, 1:].rearrange("p j b l -> p (j b) l"), ALU.subtract).then_inc(sx2_ready, 1)
                dve.wait_ge(sx2_ready, 1)
                for to, name in ((r_all, "fmaa_k"), (v_all, "fmaa_r")):
                    for j in range(CT):
                        dve.scalar_tensor_tensor(out=to[:, j], in0=sx[:, j], scalar=col(name, j), in1=xa_t[:, j, :, 1:],
                                                 op0=ALU.mult, op1=ALU.add).then_inc(ffn_in, 1)
                gate = g_all[:].rearrange("p j b l -> p (j b l)")
                for b, ps in each("fv"):
                    dve.wait_ge(done["fr"], b + 1)
                    g = gate[:, b * BANK:(b + 1) * BANK]
                    dve.scalar_tensor_tensor(out=g, in0=g, scalar=1.0, in1=ps[:], op0=ALU.add, op1=ALU.mult).then_inc(done["fv"], 1)
                    dve.wait_ge(done["fv"], b + 1)
                    dve.scalar_tensor_tensor(out=o_nat[:, b], in0=g.rearrange("p (t c) -> p t c", t=LT), scalar=0.5, in1=x_nat[:, b],
                                             op0=ALU.mult, op1=ALU.add).then_inc(out_ready, 1)

            @block.sync
            def _(sp):
                for b in range(B):
                    sp.wait_ge(out_ready, b + 1)
                    sp.dma_start(out[b].rearrange("(t p) c -> p t c", p=P), o_nat[:, b]).then_inc(stored, 16)
                sp.wait_ge(stored, 16 * B)


_INS = {'x': 'x', 'ctx_2048': 'ctx', 'mask_Bx1xSxS2_ff0': 'mask', 'L0_xattn_Wq': 'Wq', 'L0_xattn_bq': 'bq', 'L0_xattn_Wk': 'Wk0',
        'L0_xattn_bk': 'bk', 'L0_xattn_Wv': 'Wv0', 'L0_xattn_bv': 'bv', 'L0_xattn_Wo': 'Wo0', 'L0_xattn_bo': 'bo',
        'L0_xattn_gamma': 'gamma', 'L0_xattn_beta': 'beta'}
_INS.update({f'L1_xattn_{n}': n for n in (*VECTORS, *TURNED, 'maa_w1', 'maa_w2', 'decay_w1', 'decay_w2')})


def kernel(**inputs):
    import numpy as _np
    import concourse.bacc as _bacc
    from concourse import mybir as _mybir
    from concourse.bass_utils import run_bass_kernel_spmd as _run

    nc = _bacc.Bacc("TRN2", target_bir_lowering=False, num_devices=1)
    arrays, args = {}, {}
    for name, short in _INS.items():
        v = _np.ascontiguousarray(inputs[name])
        arrays[f"in_{name}_dram"] = v
        args[short] = nc.dram_tensor(f"in_{name}_dram", v.shape, _mybir.dt.from_np(v.dtype), kind="ExternalInput").ap()
    out = nc.dram_tensor("out_0_dram", (B, L, C), _mybir.dt.float32, kind="ExternalOutput").ap()
    build(nc, args, out)
    r = _run(nc, [arrays], core_ids=[0])
    return r.results[0]["out_0_dram"]
```

```python
from contextlib import ExitStack

import concourse.bass as bass
from concourse import mybir

ALU = mybir.AluOpType
ACT = mybir.ActivationFunctionType
AX = mybir.AxisListType
F32 = mybir.dt.float32
BF16 = mybir.dt.bfloat16
I32 = mybir.dt.int32

P = 128

B, L, C = 4, 256, 256
S = 1601
NH, KVH, HD = 32, 8, 8
GROUPS = NH // KVH
LT = L // P
CT = C // P
ST = -(-S // P)
SLAST = S - (ST - 1) * P
UNITS = KVH // 2
UH = 2 * GROUPS
SPLIT = 64
TERMS = 6
BANK = 512
SCALE = HD ** -0.5
NEG = -3.0e38
EPS0, EPS1 = 1e-6, 1e-5

Q_PART = (0, 0, 1, 1, 0, 2)
K_PART = (0, 1, 0, 1, 2, 0)

ACHUNK = (0, 2 * BANK, S)
A_PER_UNIT = UH * LT * 2
A_PER_BATCH = A_PER_UNIT * UNITS
E_PER_TILE = 4
E_PER_UNIT = E_PER_TILE * ST
E_PER_BATCH = E_PER_UNIT * UNITS

CTX_ROUNDS, KV_ROUNDS = -(-ST // 2), -(-ST // 4)
PREP = ([("ctxT", n, "act") for n in range(CTX_ROUNDS)] + [("xT", 0, "act"), ("q", 0, "dve")]
        + [("kv", n, "dve") for n in range(KV_ROUNDS)])
for _u in range(UNITS):
    PREP += [("qT", _u, "act"), ("kT", 2 * _u, "act"), ("kT", 2 * _u + 1, "act")]
PREP_ACT = sum(r[2] == "act" for r in PREP)
PREP_DVE = len(PREP) - PREP_ACT
BEFORE_UNITS = len(PREP) - 3 * UNITS


def emptied(n):
    return sum(r[2] == "act" for r in PREP[:n]), sum(r[2] == "dve" for r in PREP[:n])


def count(batch, per_batch, n):
    reg, more = batch
    return more * per_batch + n if reg is None else reg * per_batch + (more * per_batch + n)


MIXES, DM, DD = 5, 32, 64
TURNED = ("Wk", "Wv", "Wr", "Wg", "Wo", "fWk", "fWr", "fWv")
VECTORS = ("ln1_w", "ln1_b", "ln2_w", "ln2_b", "maa_x", "maa_w", "maa_k", "maa_v", "maa_r", "maa_g",
           "time_decay", "faaaa", "gn_w", "gn_b", "fmaa_k", "fmaa_r")

LEAD, TURN = 6, 2
AHEAD = LEAD + 2


def order():
    tile = A_PER_UNIT / ST
    items = []

    def add(at, *item):
        items.append((at, item))

    for g in range(UNITS + 2):
        for n in range(A_PER_UNIT):
            add(A_PER_UNIT * g + n, "max", g // UNITS, g % UNITS, n)
        if g <= UNITS:
            add(A_PER_UNIT * (g + 1) + TURN - 0.9, "turn", g // UNITS, g % UNITS, 0)
    start, end = A_PER_UNIT + AHEAD, A_PER_UNIT * (UNITS + 1) + AHEAD
    for u in range(UNITS):
        after = A_PER_UNIT * (u + 1) + LEAD
        for t in range(ST):
            for j in range(E_PER_TILE):
                add(after + tile * (t + j / 5) + 0.1, "exp", 0, u, (t, j))
            if t:
                add(after + tile * (t + 0.65), "values", 0, u, t - 1)
        add(after + A_PER_UNIT + 0.05, "values", 0, u, ST - 1)
        add(after + A_PER_UNIT + 0.06, "copy", 0, u, 0)
        add(after + A_PER_UNIT + (2 * tile if u < UNITS - 1 else 1.5), "normal", 0, u, 0)

    def turned(at, batch, u):
        for k in range(3):
            add(at + 2 * k + 0.5, "prep", batch, 0, BEFORE_UNITS + 3 * u + k)
        add(at + 5.5, "v_copy", batch, u, 0)

    turned(start + 1, 0, UNITS - 1)
    at = start + 14
    for n in range(BEFORE_UNITS):
        add(at + 0.4, "prep", 1, 0, n)
        at += 3
        if n in (CTX_ROUNDS + 1, BEFORE_UNITS - 1):
            which = 0 if n == CTX_ROUNDS + 1 else 1
            for k in range(5):
                add(at + 0.45 + k, "split", 1, which, k)
            add(at + 6.45, "copy_terms", 1, which, 0)
            if which:
                at += 7
    for u in range(UNITS - 1):
        turned(max(at, A_PER_UNIT * (u + 2) + LEAD + 1), 1, u)
        at += 9
    after = A_PER_UNIT * UNITS
    for lt in range(LT):
        add(after - 4 + 20 * lt + 0.7, "mask_sum", 1, lt, 0)
    add(after + 20 + 0.7, "mask_any", 1, 0, 0)
    add(after + 22 + 0.7, "mask_count", 1, 0, 0)
    add(after + 24 + 0.7, "mask_flag", 1, 0, 0)
    items.sort(key=lambda x: x[0])
    step = [item for at, item in items if (start <= at < end if item[0] == "max" else A_PER_UNIT + TURN < at)]
    last = [item for item in step if item[1] == 0]

    first = []
    for n in range(BEFORE_UNITS + 3 * (UNITS - 1)):
        if n == BEFORE_UNITS:
            first.append(("copy_terms", 0, 0, 0))
        if n == BEFORE_UNITS + 1:
            first.append(("copy_terms", 0, 1, 0))
        first.append(("prep", 0, 0, n))
        if n in (CTX_ROUNDS + 1, BEFORE_UNITS - 1):
            first += [("split", 0, int(n == BEFORE_UNITS - 1), k) for k in range(5)]
        if n >= BEFORE_UNITS and (n - BEFORE_UNITS) % 3 == 2:
            first.append(("v_copy", 0, (n - BEFORE_UNITS) // 3, 0))
    first += [("mask_sum", 0, lt, 0) for lt in range(LT)]
    for at, item in items:
        if item[0] == "max" and at < start:
            first.append(item)
            if at == A_PER_UNIT - 4:
                first += [("mask_any", 0, 0, 0), ("mask_count", 0, 0, 0), ("mask_flag", 0, 0, 0)]
        elif item[0] == "turn" and at < start:
            first.append(item)
    return first, step, last


FIRST_STEP, STEP, LAST_STEP = order()


def rows_of(tile):
    return SLAST if tile == ST - 1 else P


def build(nc, a, out):
    with ExitStack() as whole:
        def sb(name, shape, dt):
            return whole.enter_context(nc.sbuf_tensor(name, shape, dt))

        def sem(name):
            return whole.enter_context(nc.semaphore(name))

        held = {
            "ident_f": sb("ident_f", [P, P], F32),
            "x_nat": sb("x_nat", [P, B, LT, C], F32),
            "o_nat": sb("o_nat", [P, B, LT, C], F32),
            "w_nat": sb("w_nat", [P, len(TURNED), CT, C], F32),
            "wo": sb("wo", [P, CT, C], F32),
            "maa_w1": sb("maa_w1", [P, CT, MIXES * DM], F32),
            "maa_w2": sb("maa_w2", [P, C], F32),
            "maa_w2_last": sb("maa_w2_last", [DM, C], F32),
            "decay_w1": sb("decay_w1", [P, CT, DD], F32),
            "decay_w2": sb("decay_w2", [DD, C], F32),
            "rows": sb("rows", [P, 3, C], F32),
            "vec_nat": sb("vec_nat", [CT * len(VECTORS), P], F32),
            "state_nat": sb("state_nat", [2 * B, C], F32),
            "s0": sb("s0", [P, CT, B, HD], F32),
        }
        loads_in = sem("loads_in")
        attention(nc, sem, held, loads_in, a)
        mixing(nc, sem, held, loads_in, out)


def load_second_part(eng, held, loads_in, a):
    pairs = [(held["x_nat"][:], a["x"].rearrange("b (t p) c -> p b t c", p=P)),
             (held["wo"][:], a["Wo0"].rearrange("(t p) n -> p t n", p=P)),
             (held["maa_w1"][:], a["maa_w1"].rearrange("(t p) n -> p t n", p=P)),
             (held["maa_w2"][:], a["maa_w2"][0:MIXES - 1].rearrange("f d c -> (f d) c")),
             (held["maa_w2_last"][:], a["maa_w2"][MIXES - 1]),
             (held["decay_w1"][:], a["decay_w1"].rearrange("(t p) n -> p t n", p=P)),
             (held["decay_w2"][:], a["decay_w2"])]
    pairs += [(held["rows"][:, n, :], a[name].partition_broadcast(P)) for n, name in enumerate(("bo", "gamma", "beta"))]
    pairs += [(held["w_nat"][:, n], a[name].rearrange("(t p) n -> p t n", p=P)) for n, name in enumerate(TURNED)]
    for n, name in enumerate(VECTORS):
        v = a[name]
        if len(v.shape) > 1:
            v = v.rearrange("h s a -> (h s a)")
        pairs.append((held["vec_nat"][CT * n:CT * (n + 1), :], v.rearrange("(t p) -> t p", p=P)))
    for b in range(B):
        pairs.append((held["state_nat"][2 * b:2 * b + 2, :], a["ctx"][b, 0:2, :]))
        pairs.append((held["s0"][:, :, b, :],
                      a["ctx"][b, 2:2 + HD, :].rearrange("r c -> (r c)").rearrange("(j p t) -> p j t", j=CT, t=HD)))
    for to, of in pairs:
        eng.dma_start(to, of).then_inc(loads_in, 16)
    return len(pairs)


def attention(nc, sem, held, loads_in, a):
    x, ctx_in, mask, Wq, bq, Wk, bk, Wv, bv = (a[n] for n in ("x", "ctx", "mask", "Wq", "bq", "Wk0", "bk", "Wv0", "bv"))
    ident_f, o_nat = held["ident_f"], held["o_nat"]
    with ExitStack() as here:
        def sb(name, shape, dt):
            return here.enter_context(nc.sbuf_tensor(name, shape, dt))

        def psum(name, shape, dt):
            return here.enter_context(nc.psum_tensor(name, shape, dt))

        ident_b = sb("ident_b", [P, P], BF16)
        wq = sb("wq", [P, CT, C], F32)
        wkv = sb("wkv", [P, CT, 2 * KVH * HD], F32)
        bq_row = sb("bq_row", [P, C], F32)
        bkv_row = sb("bkv_row", [P, 2 * KVH * HD], F32)
        ones_col = sb("ones_col", [P, 1], F32)
        x_bat = sb("x_bat", [P, LT, C], F32)
        ctx_nat = sb("ctx_nat", [P, ST, C], F32)
        ctx_t = sb("ctx_t", [P, CT, ST * P], F32)
        mask_max = sb("mask_max", [P, LT, S], F32)
        mask_exp = sb("mask_exp", [P, LT, S], F32)
        mask_abs = sb("mask_abs", [P, S], BF16)
        mask_sum = sb("mask_sum", [P, LT], F32)
        mask_any = sb("mask_any", [P, LT], F32)
        mask_flag = sb("mask_flag", [1, 1], I32)
        x_t = sb("x_t", [P, CT, L], F32)
        q_f = sb("q_f", [P, LT * C], F32)
        q_rest = sb("q_rest", [P, LT * C], F32)
        q_aug = sb("q_aug", [P, LT, NH, SPLIT], BF16)
        k_f = sb("k_f", [P, ST, KVH * HD], F32)
        k_rest = sb("k_rest", [P, ST * KVH * HD], F32)
        k_aug = sb("k_aug", [P, ST, KVH, SPLIT], BF16)
        v_f = sb("v_f", [P, ST, KVH * HD], F32)
        v_aug = sb("v_aug", [P, ST, KVH, 32], F32)
        q_t = sb("q_t", [P, UNITS, 2, GROUPS, L], BF16)
        k_t = sb("k_t", [P, UNITS, ST * P], BF16)
        max_part = sb("max_part", [P, LT, 2, GROUPS, 2], F32)
        zeros = sb("zeros", [P, LT, 2, GROUPS], F32)
        neg_max = sb("neg_max", [P, LT, 2, GROUPS], F32)
        max_rest = sb("max_rest", [P, 2, LT, 2, GROUPS], F32)
        max_split = sb("max_split", [P, LT, 2, 3, GROUPS], BF16)
        max_t = sb("max_t", [24, L], BF16)
        probs = sb("probs", [P, 2, E_PER_TILE, BANK], F32)
        pv_sb = sb("pv_sb", [P, BANK], F32)
        row_sum = sb("row_sum", [P, LT, 2, 4], F32)

        p_max = psum("p_max", [P, 2, 2, BANK], F32)
        p_sc = psum("p_sc", [P, 2, BANK], F32)
        p_pv = psum("p_pv", [P, BANK], F32)
        p_side = psum("p_side", [P, BANK], F32)
        def t_buf(u, t):
            return (ST * u + t) % 2

        def block_of(aug, term):
            return aug.rearrange("p t h c -> p (t h) c")[:, :, term * HD:(term + 1) * HD]

        def operand(what, i, src):
            src_b = src.bitcast(BF16)
            if what == "qT":
                return [(q_t[SPLIT * half:SPLIT * (half + 1), i, half].rearrange("p h l -> p (h l)"),
                         src_b[SPLIT * half:SPLIT * (half + 1), :]) for half in range(2)]
            lo = 8 * (i % 2) * P
            hi = min(lo + 8 * P, S)
            return [(k_t[:, i // 2, lo:hi], src_b[:, 0:hi - lo])]

        ring = [p_max[:, k // 2, k % 2, :] for k in range(4)]

        weights_in = sem("weights_in")
        ctx_loaded = sem("ctx_loaded")
        mask_loaded = [sem(f"mask_loaded{lt}") for lt in range(LT)]
        mask_exp_loaded = sem("mask_exp_loaded")
        v_copied = sem("v_copied")
        const_ready = sem("const_ready")
        bias_in = sem("bias_in")
        prep_full = sem("prep_full")
        prep_act = sem("prep_act")
        prep_dve = sem("prep_dve")
        operands_clear = sem("operands_clear")
        q_split = sem("q_split")
        k_split = sem("k_split")
        q_copied = sem("q_copied")
        k_copied = sem("k_copied")
        mask_summed = [sem(f"mask_summed{lt}") for lt in range(LT)]
        mask_counted = sem("mask_counted")
        mask_anyed = sem("mask_anyed")
        mask_flagged = sem("mask_flagged")
        max_full = sem("max_full")
        max_seen = sem("max_seen")
        flag_seen = sem("flag_seen")
        max_done = sem("max_done")
        max_ready = sem("max_ready")
        max_turned = sem("max_turned")
        max_copied = sem("max_copied")
        max_placed = sem("max_placed")
        sc_full = sem("sc_full")
        exp_done = sem("exp_done")
        pv_done = sem("pv_done")
        pv_copied = sem("pv_copied")
        o_turned = sem("o_turned")
        o_summed = sem("o_summed")
        bias_scaled = sem("bias_scaled")
        o_done = sem("o_done")
        o_free = sem("o_free")
        pool_step = sem("pool_step")

        POOL_START, MAX_STEPS = 5, 5
        POOL_PER_BATCH = UNITS * MAX_STEPS

        with nc.Block() as block:

            @block.sync
            def _(sp):
                sp.dma_start(wkv[:, :, 0:KVH * HD], Wk.rearrange("(t p) n -> p t n", p=P)).then_inc(weights_in, 16)
                sp.dma_start(wkv[:, :, KVH * HD:], Wv.rearrange("(t p) n -> p t n", p=P)).then_inc(weights_in, 16)
                sp.dma_start(wq[:], Wq.rearrange("(t p) n -> p t n", p=P)).then_inc(weights_in, 16)
                sp.sem_inc(max_placed, 16)

                def load_context(b):
                    sp.dma_start(x_bat[:], x[b, :, :].rearrange("(t p) c -> p t c", p=P)).then_inc(ctx_loaded, 16)
                    sp.dma_start(ctx_nat[:, 0:ST - 1, :],
                                 ctx_in[b, 0:(ST - 1) * P, :].rearrange("(t p) c -> p t c", p=P)).then_inc(ctx_loaded, 16)
                    sp.dma_start(ctx_nat[0:SLAST, ST - 1, :], ctx_in[b, (ST - 1) * P:S, :]).then_inc(ctx_loaded, 16)

                def load_mask(b, lt):
                    sp.dma_start(mask_max[:, lt, :], mask[b, 0, lt * P:(lt + 1) * P, :]).then_inc(mask_loaded[lt], 16)

                def load_mask_exp(b):
                    sp.dma_start(mask_exp[:], mask[b, 0, :, :].rearrange("(t p) s -> p t s", p=P)).then_inc(mask_exp_loaded, 16)

                def place_maxima(batch, u):
                    sp.wait_ge(max_copied, count(batch, UNITS, u + 1))
                    for half in range(2):
                        row = SPLIT * half + TERMS * HD
                        sp.dma_start(q_t[row:row + 3, u, half, :, :], max_t[12 * half:12 * half + 12, :]).then_inc(max_placed, 16)

                load_context(0)
                for lt in range(LT):
                    load_mask(0, lt)
                load_mask_exp(0)
                place_maxima((None, 0), 0)
                with sp.Fori(0, B - 1) as b:
                    sp.wait_ge(prep_act, b * PREP_ACT + (CTX_ROUNDS + 1))
                    load_context(b + 1)
                    for u in range(1, UNITS):
                        if u == UNITS - 1:
                            sp.wait_ge(max_done, b * A_PER_BATCH + (A_PER_BATCH - A_PER_UNIT // 2 + 1))
                            sp.wait_ge(mask_summed[0], b + 1)
                            load_mask(b + 1, 0)
                        place_maxima((b, 0), u)
                    sp.wait_ge(max_done, b * A_PER_BATCH + (A_PER_BATCH + 1))
                    sp.wait_ge(mask_summed[1], b + 1)
                    load_mask(b + 1, 1)
                    place_maxima((b, 1), 0)
                    sp.wait_ge(mask_exp_loaded, b * 16 + 16)
                    sp.wait_ge(sc_full, b * E_PER_BATCH + E_PER_BATCH)
                    load_mask_exp(b + 1)
                for u in range(1, UNITS):
                    place_maxima((None, B - 1), u)
                sp.wait_ge(max_placed, 16 + 32 * UNITS * B)
                sp.wait_ge(mask_exp_loaded, 16 * B)

            @block.gpsimd
            def _(pool):
                pool.memset(ident_f[:], 0.0).then_inc(pool_step, 1)
                pool.memset(ident_b[:], 0.0).then_inc(pool_step, 1)
                pool.memset(ones_col[:], 1.0)
                pool.memset(v_aug[:], 0.0).then_inc(pool_step, 1)
                pool.memset(zeros[:], 0.0).then_inc(pool_step, 1)
                pool.memset(v_f[:], 0.0).then_inc(pool_step, 1)
                pool.wait_ge(pool_step, POOL_START)
                for m in (ident_f, ident_b):
                    pool.affine_select(out=m[:], in_=m[:], compare_op=ALU.not_equal, fill=1.0, base=0,
                                       pattern=[[-1, P]], channel_multiplier=1)
                pool.memset(v_aug[:, :, :, HD:HD + 1], 1.0).then_inc(const_ready, 1)

                def split_maxima(batch, u):
                    pool.wait_ge(max_ready, count(batch, UNITS, u + 1))
                    pool.wait_ge(max_turned, count(batch, UNITS, u + 1))
                    value = neg_max[:]
                    for k in range(3):
                        part = max_split[:, :, :, k, :]
                        done = POOL_START + MAX_STEPS * u + 2 * k + 1
                        pool.tensor_tensor(part, value, zeros[:], ALU.add).then_inc(pool_step, 1)
                        pool.wait_ge(pool_step, count(batch, POOL_PER_BATCH, done))
                        if k < 2:
                            pool.tensor_tensor(max_rest[:, k], value, part, ALU.subtract).then_inc(pool_step, 1)
                            pool.wait_ge(pool_step, count(batch, POOL_PER_BATCH, done + 1))
                            value = max_rest[:, k]

                def copy_values(batch, u, first):
                    pool.wait_ge(prep_dve, count(batch, PREP_DVE, 1 + KV_ROUNDS))
                    if not first:
                        pool.wait_ge(pv_done, count(batch, UNITS * ST, ST * (u + 1) + 2 - UNITS * ST))
                    pool.tensor_tensor(v_aug[:, :, 2 * u:2 * u + 2, 0:HD],
                                       v_f[:, :, 2 * u * HD:2 * (u + 1) * HD].rearrange("p t (h d) -> p t h d", d=HD),
                                       zeros[:].rearrange("p t a h -> p (t a h)")[:, 0:2 * HD].rearrange("p (h d) -> p h d", d=HD)
                                       .unsqueeze(1).to_broadcast([P, ST, 2, HD]), ALU.add).then_inc(v_copied, 1)

                def walk(items, reg, first, more=0):
                    for kind, batch, u, _ in items:
                        if kind == "turn":
                            split_maxima((reg, more + batch), u)
                        elif kind == "v_copy":
                            copy_values((reg, more + batch), u, first)

                walk(FIRST_STEP, None, True)
                with pool.Fori(0, B - 1) as b:
                    walk(STEP, b, False)
                walk(LAST_STEP, None, False, B - 1)

            @block.tensor
            def _(pe):
                pe.sem_inc(pv_done, 2)
                pe.sem_inc(o_turned, 1)
                pe.sem_inc(max_turned, 1)
                pe.wait_ge(const_ready, 1)
                pe.wait_ge(weights_in, 48)

                def prep(batch, n, ahead):
                        what, i, _ = PREP[n]
                        if ahead:
                            out = p_side[:]
                            side_bank_free()
                            side_user[0] = ("prep", batch, n)
                        else:
                            out = ring[n % 4]
                            if n >= 4:
                                by_act, by_dve = emptied(n - 3)
                                pe.wait_ge(prep_act, by_act)
                                if by_dve:
                                    pe.wait_ge(prep_dve, by_dve)
                        out_b = out.bitcast(BF16)
                        if what == "ctxT":
                            if i == 0:
                                pe.wait_ge(ctx_loaded, count(batch, 48, 48))
                            for t in range(2 * i, min(2 * i + 2, ST)):
                                r = rows_of(t)
                                for j in range(CT):
                                    at = (2 * (t % 2) + j) * P
                                    mm = pe.transpose(out[:, at:at + r], ctx_nat[0:r, t, j * P:(j + 1) * P], ident_f[0:r, 0:r])
                        elif what == "xT":
                            for lt in range(LT):
                                for j in range(CT):
                                    mm = pe.transpose(out[:, j * L + lt * P:j * L + (lt + 1) * P],
                                                      x_bat[:, lt, j * P:(j + 1) * P], ident_f[:])
                        elif what == "q":
                            pe.wait_ge(prep_act, count(batch, PREP_ACT, CTX_ROUNDS + 1))
                            for lt in range(LT):
                                for j in range(CT):
                                    mm = pe.matmul(out[:, lt * C:(lt + 1) * C], x_t[:, j, lt * P:(lt + 1) * P], wq[:, j, :],
                                                   start=(j == 0), stop=(j == CT - 1))
                        elif what == "kv":
                            for t in range(4 * i, min(4 * i + 4, ST)):
                                r = rows_of(t)
                                for j in range(CT):
                                    mm = pe.matmul(out[0:r, (t % 4) * P:(t % 4 + 1) * P], ctx_t[:, j, t * P:t * P + r],
                                                   wkv[:, j, :], start=(j == 0), stop=(j == CT - 1))
                        elif what == "qT":
                            if i == 0:
                                pe.wait_ge(q_split, count(batch, 5, 5))
                                pe.wait_ge(q_copied, count(batch, 1, 1))
                            for hh in range(GROUPS):
                                for lt in range(LT):
                                    pair = q_aug[:, lt, UH * i + 2 * hh:UH * i + 2 * hh + 2, :].rearrange("p h c -> p (h c)")
                                    at = hh * L + lt * P
                                    mm = pe.transpose(out_b[:, at:at + P], pair, ident_b[:])
                        else:
                            if i == 0:
                                pe.wait_ge(k_split, count(batch, 5, 5))
                                pe.wait_ge(k_copied, count(batch, 1, 1))
                            for t in range(8 * (i % 2), min(8 * (i % 2) + 8, ST)):
                                r = rows_of(t) + rows_of(t) % 2
                                at = (t % 8) * P
                                mm = pe.transpose(out_b[:, at:at + r],
                                                  k_aug[0:r, t, i - i % 2:i - i % 2 + 2, :].rearrange("p h c -> p (h c)"), ident_b[0:r, 0:r])
                        mm.then_inc(prep_full, 1)

                def row_max(batch, u, n, first):
                    lt, half, hh, k = n // (2 * UH), n // UH % 2, n // 2 % GROUPS, n % 2
                    a = A_PER_UNIT * u + n
                    if n == 0:
                        pe.wait_ge(prep_act, count(batch, PREP_ACT, emptied(BEFORE_UNITS + 3 * (u + 1))[0]))
                    if first and u == 0 and n < 2:
                        pe.wait_ge(prep_act, emptied(BEFORE_UNITS + 3 * (UNITS - 1))[0])
                        pe.wait_ge(prep_dve, PREP_DVE)
                    else:
                        pe.wait_ge(max_done, count(batch, A_PER_BATCH, a))
                    for bank, s0 in enumerate(range(ACHUNK[k], ACHUNK[k + 1], BANK)):
                        s1 = min(s0 + BANK, ACHUNK[k + 1])
                        mm = pe.matmul(p_max[:, n % 2, bank, 0:s1 - s0], q_t[:, u, half, hh, lt * P:(lt + 1) * P],
                                       k_t[:, u, s0:s1], start=True, stop=True)
                    mm.then_inc(max_full, 1)

                def turn_maxima(batch, u):
                    pe.wait_ge(pool_step, count(batch, POOL_PER_BATCH, POOL_START + MAX_STEPS * (u + 1)))
                    side_bank_free()
                    side_user[0] = ("turn", batch, u)
                    for lt in range(LT):
                        mm = pe.transpose(p_side[0:24, :].bitcast(BF16)[:, lt * P:(lt + 1) * P],
                                          max_split[:, lt].rearrange("p a k h -> p (a k h)"), ident_b[:])
                    mm.then_inc(max_turned, 1)

                def scores(batch, u, t, j, masked):
                    e = E_PER_UNIT * u + E_PER_TILE * t + j
                    half, r = j // 2, rows_of(t)
                    heads = slice(2 * (j % 2), 2 * (j % 2) + 2)
                    if t == 0 and j == 0:
                        pe.wait_ge(max_placed, count(batch, 32 * UNITS, 32 * (u + 1) + 16))
                        if masked and u == 0:
                            pe.wait_ge(mask_exp_loaded, count(batch, 16, 16))
                    pe.wait_ge(exp_done, count(batch, E_PER_BATCH, e + 1))
                    out = p_sc[0:r, e % 2, :]
                    mm = pe.matmul(out, k_t[:, u, t * P:t * P + r], q_t[:, u, half, heads, :], start=True, stop=not masked)
                    if masked:
                        for h in range(2):
                            for lt in range(LT):
                                at = h * L + lt * P
                                mm = pe.matmul(out[:, at:at + P], mask_exp[:, lt, t * P:t * P + r], ident_f[:],
                                               start=False, stop=(lt == LT - 1 and h == 1))
                    mm.then_inc(sc_full, 1)

                def values(batch, u, t):
                    r = rows_of(t)
                    pe.wait_ge(exp_done, count(batch, E_PER_BATCH, E_PER_UNIT * u + E_PER_TILE * (t + 1) + 2))
                    if t == 0:
                        pe.wait_ge(v_copied, count(batch, UNITS, u + 1))
                        pe.wait_ge(pv_copied, count(batch, UNITS, u + 1))
                    for j in range(4):
                        mm = pe.matmul(p_pv[32 * j:32 * j + 32, :], v_aug[0:r, t, 2 * u + j // 2, :], probs[0:r, t_buf(u, t), j, :],
                                       start=(t == 0), stop=(t == ST - 1), tile_position=(0, 32 * j))
                    mm.then_inc(pv_done, 1)

                def turn_output(batch, u):
                    pe.wait_ge(pv_copied, count(batch, UNITS, u + 2))
                    side_bank_free()
                    side_user[0] = ("normal", batch, u)
                    for lt in range(LT):
                        for e in range(2):
                            k = 2 * lt + e
                            mm = pe.transpose(p_side[:, k * P:(k + 1) * P], pv_sb[:, e * L + lt * P:e * L + (lt + 1) * P], ident_f[:])
                    mm.then_inc(o_turned, 1)

                def count_mask(batch):
                    pe.wait_ge(mask_anyed, count(batch, 1, 1))
                    side_bank_free()
                    side_user[0] = ("mask_count", batch, 0)
                    for lt in range(LT):
                        mm = pe.matmul(p_side[0:1, 0:1], mask_any[:, lt:lt + 1], ones_col[:], start=(lt == 0), stop=(lt == LT - 1))
                    mm.then_inc(mask_counted, 1)

                side_user = [None]

                def side_bank_free():
                    if side_user[0] is None:
                        return
                    kind, batch, n = side_user[0]
                    if kind == "prep":
                        if PREP[n][2] == "act":
                            pe.wait_ge(prep_act, count(batch, PREP_ACT, emptied(n + 1)[0]))
                        else:
                            pe.wait_ge(prep_dve, count(batch, PREP_DVE, emptied(n + 1)[1]))
                    elif kind == "mask_count":
                        pe.wait_ge(mask_flagged, count(batch, 1, 1))
                    elif kind == "turn":
                        pe.wait_ge(max_copied, count(batch, UNITS, n + 1))
                    elif kind == "normal":
                        pe.wait_ge(o_done, count(batch, UNITS, n + 2))
                    else:
                        pe.wait_ge(max_copied, count(batch, UNITS, 1))
                        pe.wait_ge(o_done, count(batch, UNITS, 1))

                def walk(items, reg, masked, more=0, first=False):
                    side_user[0] = None if first else ("step", (reg, more), 0)
                    for kind, batch, u, n in items:
                        batch = (reg, more + batch)
                        if kind == "max":
                            row_max(batch, u, n, first)
                        elif kind == "exp":
                            scores(batch, u, *n, masked)
                        elif kind == "values":
                            values(batch, u, n)
                        elif kind == "turn":
                            turn_maxima(batch, u)
                        elif kind == "normal":
                            turn_output(batch, u)
                        elif kind == "prep":
                            prep(batch, n, not first)
                        elif kind == "mask_count":
                            count_mask(batch)

                def by_mask(items, reg, more=0):
                    pe.wait_ge(mask_flagged, count((reg, more), 1, 1))
                    pe.sem_inc(flag_seen, 1)
                    flag = pe.value_load(mask_flag[0:1, 0:1])
                    with pe.If(flag > 0):
                        walk(items, reg, True, more)
                    with pe.Else():
                        walk(items, reg, False, more)

                walk(FIRST_STEP, None, False, first=True)
                with pe.Fori(0, B - 1) as b:
                    by_mask(STEP, b)
                by_mask(LAST_STEP, None, B - 1)

            @block.scalar
            def _(act):
                act.dma_start(bq_row[:], bq.partition_broadcast(P)).then_inc(bias_in, 16)
                act.dma_start(bkv_row[:, 0:KVH * HD], bk.partition_broadcast(P)).then_inc(bias_in, 16)
                act.dma_start(bkv_row[:, KVH * HD:], bv.partition_broadcast(P)).then_inc(bias_in, 16)
                load_second_part(act, held, loads_in, a)
                act.sem_inc(exp_done, 2)
                act.sem_inc(pv_copied, 1)

                def copy_terms(batch, which):
                    aug, parts, split, copied = ((q_aug[:], Q_PART, q_split, q_copied), (k_aug[:], K_PART, k_split, k_copied))[which]
                    for term, part in enumerate(parts):
                        first = parts.index(part)
                        if term != first:
                            act.wait_ge(split, count(batch, 5, 2 * part + 1))
                            last = act.activation(block_of(aug, term), block_of(aug, first), ACT.Copy)
                    last.then_inc(copied, 1)

                def prep(batch, n, ahead):
                    what, i, who = PREP[n]
                    if who != "act":
                        return
                    act.wait_ge(prep_full, count(batch, len(PREP), n + 1))
                    src = p_side[:] if ahead else ring[n % 4]
                    if what == "ctxT":
                        tiles = min(2, ST - 2 * i)
                        w = rows_of(2 * i)
                        ins = act.activation(
                            ctx_t[:, :, 2 * i * P:(2 * i + tiles) * P].rearrange("p j (t s) -> p t j s", s=P)[:, :, :, 0:w],
                            src[:, 0:tiles * CT * P].rearrange("p (t j s) -> p t j s", j=CT, s=P)[:, :, :, 0:w], ACT.Copy)
                    elif what == "xT":
                        ins = act.activation(x_t[:].rearrange("p j l -> p (j l)"), src, ACT.Copy)
                    else:
                        for to, of in operand(what, i, src):
                            ins = act.activation(to, of, ACT.Copy)
                    ins.then_inc(prep_act, 1)

                def exponential(batch, u, t, j):
                    r, e = rows_of(t), E_PER_UNIT * u + E_PER_TILE * t + j
                    act.wait_ge(sc_full, count(batch, E_PER_BATCH, e + 1))
                    if j == 0:
                        act.wait_ge(pv_done, count(batch, UNITS * ST, ST * u + t + 1))
                    act.activation(probs[0:r, t_buf(u, t), j, :], p_sc[0:r, e % 2, :], ACT.Exp).then_inc(exp_done, 1)

                def walk(items, reg, more=0, first=False):
                    for kind, batch, u, n in items:
                        batch = (reg, more + batch)
                        if kind == "exp":
                            exponential(batch, u, *n)
                        elif kind == "turn":
                            act.wait_ge(max_turned, count(batch, UNITS, u + 2))
                            act.wait_ge(max_placed, count(batch, 32 * UNITS, 32 * u + 16))
                            act.activation(max_t[:], p_side[0:24, :].bitcast(BF16)[:, 0:L], ACT.Copy).then_inc(max_copied, 1)
                        elif kind == "copy":
                            act.wait_ge(pv_done, count(batch, UNITS * ST, ST * (u + 1) + 2))
                            act.wait_ge(o_turned, count(batch, UNITS, u + 1))
                            act.activation(pv_sb[:], p_pv[:], ACT.Copy).then_inc(pv_copied, 1)
                        elif kind == "prep":
                            prep(batch, n, not first)
                        elif kind == "copy_terms":
                            copy_terms(batch, u)
                        elif kind == "mask_sum":
                            act.wait_ge(mask_loaded[u], count(batch, 16, 16))
                            if not (first and u == 0):
                                act.wait_ge(mask_summed[1 - u], count(batch, 1, u))
                            act.activation(mask_abs[:], mask_max[:, u, :], ACT.Abs, accum_out=mask_sum[:, u:u + 1])\
                                .then_inc(mask_summed[u], 1)

                walk(FIRST_STEP, None, first=True)
                with act.Fori(0, B - 1) as b:
                    walk(STEP, b)
                walk(LAST_STEP, None, B - 1)

            @block.vector
            def _(dve):
                dve.sem_inc(max_done, 1)
                dve.sem_inc(o_done, 1)
                dve.memset(q_aug[:], 0.0).then_inc(operands_clear, 1)
                dve.memset(k_aug[:], 0.0).then_inc(operands_clear, 1)
                dve.memset(k_f[:], 0.0).then_inc(operands_clear, 1)
                dve.memset(q_t[:], 0.0).then_inc(operands_clear, 1)
                dve.wait_ge(operands_clear, 4)
                dve.memset(k_aug[:, :, :, TERMS * HD:TERMS * HD + 3], 1.0).then_inc(operands_clear, 1)
                dve.wait_ge(const_ready, 1)
                dve.wait_ge(operands_clear, 5)
                dve.wait_ge(bias_in, 48)
                dve.tensor_scalar(bq_row[:], bq_row[:], SCALE, None, ALU.mult).then_inc(bias_scaled, 1)
                dve.wait_ge(bias_scaled, 1)

                def split(batch, which, step):
                    full, rest, aug, parts, done = (
                        (q_f[:], q_rest, q_aug[:], Q_PART, q_split),
                        (k_f[:].rearrange("p t n -> p (t n)"), k_rest, k_aug[:], K_PART, k_split))[which]

                    def left(k):
                        value = full if k == 0 else rest[:]
                        return value.rearrange("p (h d) -> p h d", d=HD)

                    k = step // 2
                    part = block_of(aug, parts.index(k))
                    if step:
                        dve.wait_ge(done, count(batch, 5, step))
                    else:
                        dve.wait_ge(prep_dve, count(batch, PREP_DVE, 1 + KV_ROUNDS if which else 1))
                    if step % 2 == 0:
                        dve.tensor_copy(part, left(k)).then_inc(done, 1)
                    else:
                        dve.tensor_tensor(left(k + 1), left(k), part, ALU.subtract).then_inc(done, 1)

                def prep(batch, n, ahead):
                    what, i, who = PREP[n]
                    if who != "dve":
                        return
                    dve.wait_ge(prep_full, count(batch, len(PREP), n + 1))
                    src = p_side[:] if ahead else ring[n % 4]
                    if what == "q":
                        for lt in range(LT):
                            for half in range(2):
                                def cols(ap, order):
                                    return ap.rearrange(order, u=UNITS, half=2, h=GROUPS)
                                ins = dve.scalar_tensor_tensor(
                                    out=cols(q_f[:, lt * C:(lt + 1) * C], "p (u h half d) -> p u h half d")[:, :, :, half, :],
                                    in0=cols(src[:, lt * C:(lt + 1) * C], "p (u half h d) -> p u half h d")[:, :, half, :, :],
                                    scalar=SCALE, in1=cols(bq_row[:], "p (u half h d) -> p u half h d")[:, :, half, :, :],
                                    op0=ALU.mult, op1=ALU.add)
                    else:
                        if i == 0 and ahead:
                            dve.wait_ge(v_copied, count(batch, UNITS, 0))
                        tiles, r, w = min(4, ST - 4 * i), rows_of(4 * i), KVH * HD
                        both = src[0:r, 0:tiles * P].rearrange("p (t n) -> p t n", n=P)
                        bias = bkv_row[0:r, :].unsqueeze(1).to_broadcast([r, tiles, P])
                        dve.tensor_tensor(k_f[0:r, 4 * i:4 * i + tiles, :], both[:, :, 0:w], bias[:, :, 0:w], ALU.add)
                        ins = dve.tensor_tensor(v_f[0:r, 4 * i:4 * i + tiles, :], both[:, :, w:], bias[:, :, w:], ALU.add)
                    ins.then_inc(prep_dve, 1)

                def row_max(batch, u, n, first):
                    lt, half, hh, k = n // (2 * UH), n // UH % 2, n // 2 % GROUPS, n % 2
                    lo, hi = ACHUNK[k], ACHUNK[k + 1]
                    if u == 0 and n in (0, A_PER_UNIT // 2):
                        dve.wait_ge(mask_loaded[lt], count(batch, 16, 16))
                    if n == 0 and not (first and u == 0):
                        dve.wait_ge(max_ready, count(batch, UNITS, u))
                    dve.wait_ge(max_full, count(batch, A_PER_BATCH, A_PER_UNIT * u + n + 1))
                    dve.sem_inc(max_seen, 1)
                    sc = p_max[:, n % 2].rearrange("p a n -> p (a n)")[:, 0:hi - lo]
                    dve.tensor_tensor_reduce(sc, sc, mask_max[:, lt, lo:hi], 1.0, NEG, ALU.add, ALU.max,
                                             max_part[:, lt, half, hh, k:k + 1]).then_inc(max_done, 1)
                    if n == A_PER_UNIT - 1:
                        dve.wait_ge(max_done, count(batch, A_PER_BATCH, A_PER_UNIT * (u + 1) + 1))
                        dve.wait_ge(pool_step, count(batch, POOL_PER_BATCH, POOL_START + MAX_STEPS * u))
                        dve.tensor_reduce(neg_max[:], max_part[:], AX.X, ALU.max, negate=True).then_inc(max_ready, 1)

                def normal(batch, u):
                    dve.wait_ge(o_turned, count(batch, UNITS, u + 2))
                    turned = p_side[:].rearrange("p (t e j c) -> p t e j c", t=LT, e=2, j=4)
                    dve.reciprocal(row_sum[:].rearrange("p t e j -> p (t e) j"),
                                   p_side[:].rearrange("p (k j c) -> p k j c", k=4, j=4)[:, :, :, HD]).then_inc(o_summed, 1)
                    dve.wait_ge(o_summed, count(batch, UNITS, u + 1))
                    reg, more = batch
                    for lt in range(LT):
                        ins = dve.tensor_tensor(
                            o_nat[:, more if reg is None else reg, lt, UH * HD * u:UH * HD * (u + 1)].rearrange("p (j e d) -> p e j d", e=2, d=HD),
                            turned[:, lt, :, :, 0:HD],
                            row_sum[:, lt].unsqueeze(3).to_broadcast([P, 2, 4, HD]), ALU.mult)
                    ins.then_inc(o_done, 1)

                def walk(items, reg, more=0, first=False):
                    for kind, batch, u, n in items:
                        batch = (reg, more + batch)
                        if kind == "max":
                            row_max(batch, u, n, first)
                        elif kind == "normal":
                            normal(batch, u)
                        elif kind == "prep":
                            prep(batch, n, not first)
                        elif kind == "split":
                            split(batch, u, n)
                        elif kind == "mask_any":
                            for lt in range(LT):
                                dve.wait_ge(mask_summed[lt], count(batch, 1, 1))
                            dve.tensor_scalar(mask_any[:], mask_sum[:], 0.0, None, ALU.is_gt).then_inc(mask_anyed, 1)
                        elif kind == "mask_flag":
                            dve.wait_ge(mask_counted, count(batch, 1, 1))
                            dve.tensor_scalar(mask_flag[:], p_side[0:1, 0:1], 0.5, None, ALU.is_gt).then_inc(mask_flagged, 1)

                walk(FIRST_STEP, None, first=True)
                with dve.Fori(0, B - 1) as b:
                    walk(STEP, b)
                walk(LAST_STEP, None, B - 1)


STAGES = [("turn_w", 8, "act"), ("turn_vec", 1, "act"), ("turn_o", B, "act"), ("out0", B, "dve"), ("turn_x", B, "dve"),
          ("mix", 4, "act"), ("m0", 4, "dve"), ("m1", 4, "dve"), ("dec1", 2, "act"), ("m2", 4, "dve"), ("dec2", 4, "act"),
          ("p1", 4, "act"), ("m3", 4, "dve"), ("p2", 4, "act"), ("m4", 4, "dve"), ("p3", 4, "act"), ("p4", 4, "act"),
          ("own", 4, "dve")]
for _n in range(CT * B):
    STAGES.append(("spread", 4, "dve"))
    if _n:
        STAGES.append(("sum", 1, "dve"))
STAGES += [("sum", 1, "dve"), ("mean", 4, "dve"), ("var", 4, "act"), ("out1", B, "dve"), ("turn_c", B, "dve"),
           ("fk", 4, "act"), ("fr", B, "act"), ("fv", B, "dve")]
COUNT, ROUNDS = {}, []
for _name, _count, _who in STAGES:
    for _ in range(_count):
        ROUNDS.append((_name, COUNT.get(_name, 0)))
        COUNT[_name] = COUNT.get(_name, 0) + 1
FIRST = {name: ROUNDS.index((name, 0)) for name in COUNT}


def mixing(nc, sem, held, loads_in, out):
    with ExitStack() as here:
        def sb(name, shape, dt=F32):
            return here.enter_context(nc.sbuf_tensor(name, shape, dt))

        ident, x_nat, o_nat, rows = held["ident_f"], held["x_nat"], held["o_nat"], held["rows"]
        w_t = sb("w_t", [P, len(TURNED), CT, C])
        cols = sb("cols", [P, CT * len(VECTORS)])
        state = sb("state", [P, CT, 2 * B])
        spread = sb("spread", [P, HD, NH // 2, HD])
        gather = sb("gather", [P, HD, NH // 2, HD])
        heads = sb("heads", [P, NH // 2, HD])
        eighth = sb("eighth", [P, NH // 2, HD])
        eps_col = sb("eps_col", [P, 1])
        power = sb("power", [P, B * LT])
        stats = sb("stats", [P, B * LT, 6])
        moments = sb("moments", [P, B * LT, 2])
        var_eps = sb("var_eps", [P, B * LT])
        rstd = sb("rstd", [P, B * LT])
        xa_t = sb("xa_t", [P, CT, B, L + 1])
        sx = sb("sx", [P, CT, B, L])
        xxx = sb("xxx", [P, CT, B, L])
        k_all = sb("k_all", [P, CT, B, L])
        v_all = sb("v_all", [P, CT, B, L])
        r_all = sb("r_all", [P, CT, B, L])
        g_all = sb("g_all", [P, CT, B, L])
        w_all = sb("w_all", [P, CT, B, L])
        area = sb("area", [P, 6 * HD * (L + 1)])
        bank = [here.enter_context(nc.psum_tensor(f"bank{n}", [P, BANK], F32)) for n in range(8)]

        FULL = CT * B * L

        def wide(n):
            return area[:, n * FULL:(n + 1) * FULL].rearrange("p (j b l) -> p j b l", j=CT, b=B)

        mixed = [wide(n) for n in range(3)]
        o_t = wide(3)
        lo_rank = area[:, 4 * FULL:4 * FULL + B * L]
        lo_last = area[:, 4 * FULL + B * L:5 * FULL]
        dec = area[:, 5 * FULL:5 * FULL + B * L]
        pad = HD * (L + 1)
        kv_in, states, read = ([area[:, (2 * k + n) * pad:(2 * k + n + 1) * pad].rearrange("p (t l) -> p t l", t=HD)
                                for n in range(2)] for k in range(3))

        def col(name, j):
            n = CT * VECTORS.index(name) + j
            return cols[:, n:n + 1]

        full = {name: sem(f"{name}_full") for name in COUNT}
        done = {name: sem(f"{name}_done") for name in COUNT}
        const_ready2 = sem("const_ready2")
        const_step = sem("const_step")
        bo_added = sem("bo_added")
        ln_stats = sem("ln_stats")
        ln_moments = sem("ln_moments")
        ln_eps = sem("ln_eps")
        ln_rstd = sem("ln_rstd")
        ln_applied = sem("ln_applied")
        gamma_done = sem("gamma_done")
        x1_ready = sem("x1_ready")
        shift_ready = sem("shift_ready")
        sx_ready = sem("sx_ready")
        xxx_ready = sem("xxx_ready")
        mixed_ready = [sem(f"mixed_ready{f}") for f in range(MIXES)]
        w_ready = sem("w_ready")
        silu_ready = sem("silu_ready")
        rku_ready = sem("rku_ready")
        s0_placed = sem("s0_placed")
        scanned = sem("scanned")
        read_ready = sem("read_ready")
        squared = sem("squared")
        inverted = sem("inverted")
        normed = sem("normed")
        scaled = sem("scaled")
        z_ready = sem("z_ready")
        shift2_ready = sem("shift2_ready")
        sx2_ready = sem("sx2_ready")
        ffn_in = sem("ffn_in")
        kk_ready = sem("kk_ready")
        out_ready = sem("out_ready")
        gn_halved = sem("gn_halved")
        stored = sem("stored")
        n_loads = 10 + len(TURNED) + len(VECTORS) + 2 * B

        def two(ap, n):
            return ap[:, 2 * n:2 * n + 2, :]

        def half(ps):
            return ps.rearrange("p (b l) -> p b l", b=2)

        def place(n):
            return n // 2, n % 2

        with nc.Block() as block:

            x_hat = area[:, 3 * FULL:4 * FULL].rearrange("p (b t c) -> p b t c", b=B, t=LT)

            def product(pool, n):
                j, b = n // B, n % B
                pool.wait_ge(scanned, n + 1)
                if n >= 2:
                    pool.wait_ge(full["sum"], n - 1)
                pool.tensor_tensor(read[n % 2][:, :, 0:L], states[n % 2][:, :, 0:L],
                                   r_all[:, j, b, :].unsqueeze(1).to_broadcast([P, HD, L]), ALU.mult).then_inc(read_ready, 1)

            @block.gpsimd
            def _(pool):
                for m, v in ((spread, 0.0), (gather, 1.0), (heads, 1.0)):
                    pool.memset(m[:], v).then_inc(const_step, 1)
                pool.memset(eps_col[:], EPS1)
                pool.memset(power[:], -0.5)
                pool.wait_ge(const_step, 3)
                pool.affine_select(out=spread[:], in_=spread[:], compare_op=ALU.not_equal, fill=1.0, base=0,
                                   pattern=[[-1, HD], [-HD, NH // 2], [0, HD]], channel_multiplier=1).then_inc(const_step, 1)
                steps = 4
                for m, pattern in ((heads, [[HD, NH // 2], [0, HD]]), (gather, [[0, HD], [HD, NH // 2], [0, HD]])):
                    pool.affine_select(out=m[:], in_=m[:], compare_op=ALU.is_ge, fill=0.0, base=0,
                                       pattern=[[-step, n] for step, n in pattern], channel_multiplier=1).then_inc(const_step, 1)
                    steps += 1
                    pool.wait_ge(const_step, steps)
                    pool.affine_select(out=m[:], in_=m[:], compare_op=ALU.is_ge, fill=0.0, base=HD - 1,
                                       pattern=pattern, channel_multiplier=-1).then_inc(const_step, 1)
                    steps += 1
                    pool.wait_ge(const_step, steps)
                pool.affine_select(out=gather[:], in_=gather[:], compare_op=ALU.is_equal, fill=0.0, base=0,
                                   pattern=[[1, HD], [0, NH // 2], [-1, HD]], channel_multiplier=0)
                pool.tensor_scalar(eighth[:], heads[:], 1.0 / HD, None, ALU.mult).then_inc(const_ready2, 1)
                pool.wait_ge(loads_in, 16 * n_loads)
                pool.tensor_tensor(x_nat[:].rearrange("p b t c -> p (b t) c"), x_nat[:].rearrange("p b t c -> p (b t) c"),
                                   rows[:, 0, :].unsqueeze(1).to_broadcast([P, B * LT, C]), ALU.add).then_inc(bo_added, 1)

                def root(n):
                    pool.wait_ge(ln_eps, n + 1)
                    pool.tensor_tensor(rstd[:], var_eps[:], power[:], ALU.pow).then_inc(ln_rstd, 1)

                root(0)
                root(1)
                pool.wait_ge(done["turn_vec"], 1)
                for j in range(CT):
                    ins = pool.tensor_scalar(xa_t[:, j, :, 0], state[:, j, 1:2 * B:2], 1.0, None, ALU.mult)
                ins.then_inc(shift_ready, 1)
                for f in range(MIXES):
                    for n in range(4):
                        nb, j = place(n)
                        pool.wait_ge(done[f"m{f}"], n + 1)
                        x_f = two(mixed[f % 3][:, j], nb)
                        pool.tensor_tensor(x_f, x_f, two(xa_t[:, j], nb)[:, :, 1:], ALU.add).then_inc(mixed_ready[f], 1)
                for n in range(CT * B):
                    j, b = n // B, n % B
                    if n < 2:
                        for f in range(1, MIXES):
                            pool.wait_ge(full[f"p{f}"], COUNT[f"p{f}"])
                        pool.wait_ge(full["own"], COUNT["own"])
                    else:
                        pool.wait_ge(read_ready, n - 1)
                    pool.tensor_scalar(states[n % 2][:, :, 0], held["s0"][:, j, b, :], 1.0, None, ALU.mult).then_inc(s0_placed, 1)
                    if n:
                        product(pool, n - 1)
                product(pool, CT * B - 1)
                root(2)

            @block.tensor
            def _(pe):
                pe.wait_ge(loads_in, 16 * n_loads)

                at = [0]

                def next_bank():
                    n = at[0]
                    at[0] += 1
                    if n >= 8:
                        name, k = ROUNDS[n - 8]
                        pe.wait_ge(done[name], k + 1)
                    return bank[n % 8]

                def starts(name):
                    assert at[0] == FIRST[name], (name, at[0])

                def turned(name, n, source):
                    out = next_bank()
                    for lt in range(LT):
                        for j in range(CT):
                            mm = pe.transpose(out[:, j * L + lt * P:j * L + (lt + 1) * P], source[:, n, lt, j * P:(j + 1) * P], ident[:])
                    mm.then_inc(full[name], 1)

                def rows_out(name, n, source, weight):
                    out = next_bank()
                    for lt in range(LT):
                        for j in range(CT):
                            mm = pe.matmul(out[:, lt * C:(lt + 1) * C], source[:, j, n, lt * P:(lt + 1) * P], weight[:, j, :],
                                           start=(j == 0), stop=(j == CT - 1))
                    mm.then_inc(full[name], 1)

                def channels_out(name, n, source, weight):
                    nb, jo = place(n)
                    out = next_bank()
                    for j in range(CT):
                        mm = pe.matmul(half(out), weight[:, j, jo * P:(jo + 1) * P], two(source[:, j], nb),
                                       start=(j == 0), stop=(j == CT - 1))
                    mm.then_inc(full[name], 1)

                for k in range(len(TURNED)):
                    out = next_bank()
                    for jo in range(CT):
                        for j in range(CT):
                            mm = pe.transpose(out[:, j * C + jo * P:j * C + (jo + 1) * P], held["w_nat"][:, k, jo, j * P:(j + 1) * P], ident[:])
                    mm.then_inc(full["turn_w"], 1)
                out = next_bank()
                V = CT * len(VECTORS)
                pe.transpose(out[:, 0:V], held["vec_nat"][:], ident[0:V, 0:V])
                for j in range(CT):
                    mm = pe.transpose(out[:, V + 2 * B * j:V + 2 * B * (j + 1)], held["state_nat"][:, j * P:(j + 1) * P], ident[0:2 * B, 0:2 * B])
                mm.then_inc(full["turn_vec"], 1)
                for b in range(B):
                    turned("turn_o", b, o_nat)
                for b in range(B):
                    pe.wait_ge(done["turn_o"], b + 1)
                    rows_out("out0", b, o_t, held["wo"])
                pe.wait_ge(ln_applied, 2)
                for b in range(B):
                    turned("turn_x", b, x_hat)
                starts("mix")
                pe.wait_ge(xxx_ready, CT)
                for n in range(4):
                    nb, last = n % 2, n // 2
                    out = next_bank()
                    lo, hi = ((MIXES - 1) * DM, MIXES * DM) if last else (0, (MIXES - 1) * DM)
                    for j in range(CT):
                        mm = pe.matmul(half(out[0:hi - lo, :]), held["maa_w1"][:, j, lo:hi], two(xxx[:, j], nb), start=(j == 0), stop=(j == CT - 1))
                    mm.then_inc(full["mix"], 1)

                def mix(f):
                    for n in range(4):
                        nb, j = place(n)
                        out = next_bank()
                        if f < MIXES - 1:
                            pe.wait_ge(done["mix"], nb + 1)
                            w, t = held["maa_w2"][f * DM:(f + 1) * DM, :], lo_rank[f * DM:(f + 1) * DM, :]
                        else:
                            pe.wait_ge(done["mix"], nb + 3)
                            w, t = held["maa_w2_last"][:], lo_last[0:DM, :]
                        pe.matmul(out[:], w[:, j * P:(j + 1) * P], t[:, nb * BANK:(nb + 1) * BANK], start=True, stop=True)\
                            .then_inc(full[f"m{f}"], 1)

                def project(f):
                    pe.wait_ge(done["turn_w"], f)
                    for n in range(4):
                        pe.wait_ge(mixed_ready[f], 2 * (n // 2) + 2)
                        channels_out(f"p{f}", n, mixed[f % 3], w_t[:, f - 1])

                mix(0)
                mix(1)
                starts("dec1")
                for n in range(2):
                    pe.wait_ge(mixed_ready[0], 2 * n + 2)
                    out = next_bank()
                    for j in range(CT):
                        mm = pe.matmul(half(out[0:DD, :]), held["decay_w1"][:, j, :], two(mixed[0][:, j], n), start=(j == 0), stop=(j == CT - 1))
                    mm.then_inc(full["dec1"], 1)
                mix(2)
                for n in range(4):
                    nb, j = place(n)
                    pe.wait_ge(done["dec1"], nb + 1)
                    out = next_bank()
                    pe.matmul(out[:], held["decay_w2"][:, j * P:(j + 1) * P], dec[0:DD, nb * BANK:(nb + 1) * BANK], start=True, stop=True)\
                        .then_inc(full["dec2"], 1)
                project(1)
                mix(3)
                project(2)
                mix(4)
                project(3)
                project(4)
                starts("own")
                pe.wait_ge(const_ready2, 1)
                for n in range(4):
                    nb, j = place(n)
                    pe.wait_ge(rku_ready, j + 1)
                    out = next_bank()
                    pe.matmul(half(out), heads[:].rearrange("p h s -> p (h s)"), two(mixed[2][:, j], nb), start=True, stop=True)\
                        .then_inc(full["own"], 1)

                def values_of(n):
                    j, b = n // B, n % B
                    for i in range(4):
                        out = next_bank()
                        for t in range(2):
                            mm = pe.matmul(out[:, t * L:(t + 1) * L], spread[:, 2 * i + t].rearrange("p h s -> p (h s)"), v_all[:, j, b, :],
                                           start=True, stop=True)
                        mm.then_inc(full["spread"], 1)

                def summed(n):
                    pe.wait_ge(read_ready, n + 1)
                    out = next_bank()
                    for t in range(HD):
                        mm = pe.matmul(out[:, 0:L], gather[:, t].rearrange("p h s -> p (h s)"), read[n % 2][:, t, 0:L],
                                       start=(t == 0), stop=(t == HD - 1))
                    mm.then_inc(full["sum"], 1)

                for n in range(CT * B):
                    values_of(n)
                    if n:
                        summed(n - 1)
                summed(CT * B - 1)
                starts("mean")
                for name, source, sem_in in (("mean", xxx, done["sum"]), ("var", r_all, squared)):
                    for n in range(4):
                        nb, j = place(n)
                        pe.wait_ge(sem_in, CT * B if name == "mean" else n + 1)
                        out = next_bank()
                        pe.matmul(half(out), eighth[:].rearrange("p h s -> p (h s)"), two(source[:, j], nb), start=True, stop=True)\
                            .then_inc(full[name], 1)
                for b in range(B):
                    pe.wait_ge(z_ready, 2 * (b // 2) + 2)
                    rows_out("out1", b, k_all, w_t[:, TURNED.index("Wo")])
                pe.wait_ge(ln_applied, 3)
                for b in range(B):
                    turned("turn_c", b, x_hat)
                for n in range(4):
                    pe.wait_ge(ffn_in, CT)
                    channels_out("fk", n, r_all, w_t[:, TURNED.index("fWk")])
                for b in range(B):
                    pe.wait_ge(ffn_in, 2 * CT)
                    rows_out("fr", b, v_all, w_t[:, TURNED.index("fWr")])
                for b in range(B):
                    pe.wait_ge(kk_ready, 2 * (b // 2) + 2)
                    rows_out("fv", b, k_all, w_t[:, TURNED.index("fWv")])
                assert at[0] == len(ROUNDS)

            def of_round(name, n):
                return bank[ROUNDS.index((name, n)) % 8]

            @block.scalar
            def _(act):
                def each(name):
                    for n in range(COUNT[name]):
                        act.wait_ge(full[name], n + 1)
                        yield n, of_round(name, n)

                for n, ps in each("turn_w"):
                    act.activation(w_t[:, n].rearrange("p j c -> p (j c)"), ps[:], ACT.Copy).then_inc(done["turn_w"], 1)
                V = CT * len(VECTORS)
                for n, ps in each("turn_vec"):
                    act.activation(cols[:], ps[:, 0:V], ACT.Copy)
                    act.activation(state[:].rearrange("p j n -> p (j n)"), ps[:, V:V + 2 * B * CT], ACT.Copy).then_inc(done["turn_vec"], 1)
                act.wait_ge(done["turn_vec"], 1)
                lo, hi = CT * VECTORS.index("gn_w"), CT * VECTORS.index("gn_b") + CT
                act.activation(cols[:, lo:hi], cols[:, lo:hi], ACT.Copy, scale=0.5).then_inc(gn_halved, 1)
                for n, ps in each("turn_o"):
                    act.activation(o_t[:, :, n, :], ps[:].rearrange("p (j l) -> p j l", j=CT), ACT.Copy).then_inc(done["turn_o"], 1)
                for n, ps in each("mix"):
                    nb, last = n % 2, n // 2
                    to = (lo_last[0:DM] if last else lo_rank)[:, nb * BANK:(nb + 1) * BANK]
                    act.activation(to, ps[0:DM, :] if last else ps[:], ACT.Tanh).then_inc(done["mix"], 1)
                for n, ps in each("dec1"):
                    act.activation(dec[0:DD, n * BANK:(n + 1) * BANK], ps[0:DD, :], ACT.Tanh).then_inc(done["dec1"], 1)
                for n, ps in each("dec2"):
                    nb, j = place(n)
                    w = two(w_all[:, j], nb)
                    act.activation(w, half(ps), ACT.Exp, bias=col("time_decay", j)).then_inc(done["dec2"], 1)
                    act.wait_ge(done["dec2"], n + 1)
                    act.activation(w, w, ACT.Exp, scale=-1.0).then_inc(w_ready, 1)
                for f, to in ((1, k_all), (2, v_all), (3, r_all), (4, g_all)):
                    for n, ps in each(f"p{f}"):
                        nb, j = place(n)
                        if f < 4:
                            act.activation(two(to[:, j], nb), half(ps), ACT.Copy).then_inc(done[f"p{f}"], 1)
                        else:
                            act.activation(two(to[:, j], nb), half(ps), ACT.Copy)
                            act.activation(two(xxx[:, j], nb), half(ps), ACT.Tanh, scale=0.5).then_inc(done[f"p{f}"], 1)
                for n in range(4):
                    nb, j = place(n)
                    act.wait_ge(done["mean"], n + 1)
                    act.activation(two(r_all[:, j], nb), two(k_all[:, j], nb), ACT.Square).then_inc(squared, 1)
                for n, ps in each("var"):
                    nb, j = place(n)
                    act.activation(two(v_all[:, j], nb), half(ps), ACT.Sqrt, bias=eps_col[:]).then_inc(done["var"], 1)
                for n, ps in each("fk"):
                    nb, j = place(n)
                    act.activation(two(k_all[:, j], nb), half(ps), ACT.Relu).then_inc(done["fk"], 1)
                    act.wait_ge(done["fk"], n + 1)
                    act.activation(two(k_all[:, j], nb), two(k_all[:, j], nb), ACT.Square).then_inc(kk_ready, 1)
                for n, ps in each("fr"):
                    act.activation(g_all[:].rearrange("p j b l -> p (j b l)")[:, n * BANK:(n + 1) * BANK], ps[:], ACT.Tanh, scale=0.5)\
                        .then_inc(done["fr"], 1)

            @block.vector
            def _(dve):
                def each(name, lo=0, hi=None):
                    for n in range(lo, hi or COUNT[name]):
                        dve.wait_ge(full[name], n + 1)
                        yield n, of_round(name, n)

                def norm(n, source, to, eps):
                    for k in range(B * LT):
                        ins = dve.bn_stats(stats[:, k, :], source[:, k // LT, k % LT, :])
                    ins.then_inc(ln_stats, 1)
                    dve.wait_ge(ln_stats, n + 1)
                    for k in range(B * LT):
                        ins = dve.bn_aggr(moments[:, k, :], stats[:, k, :])
                    ins.then_inc(ln_moments, 1)
                    dve.wait_ge(ln_moments, n + 1)
                    dve.tensor_scalar(var_eps[:], moments[:, :, 1], eps, None, ALU.add).then_inc(ln_eps, 1)
                    dve.wait_ge(ln_rstd, n + 1)
                    for k in range(B * LT):
                        ins = dve.tensor_scalar(to[:, k // LT, k % LT, :], source[:, k // LT, k % LT, :], moments[:, k, 0:1], rstd[:, k:k + 1],
                                                ALU.subtract, ALU.mult)
                    ins.then_inc(ln_applied, 1)
                    dve.wait_ge(ln_applied, n + 1)

                def all_rows(ap):
                    return ap.rearrange("p b t c -> p (b t) c")

                def row(n):
                    return rows[:, n, :].unsqueeze(1).to_broadcast([P, B * LT, C])

                dve.wait_ge(bo_added, 1)
                for b, ps in each("out0"):
                    dve.tensor_tensor(x_nat[:, b], ps[:].rearrange("p (t c) -> p t c", t=LT), x_nat[:, b], ALU.add).then_inc(done["out0"], 1)
                dve.wait_ge(done["out0"], B)
                norm(0, x_nat, o_nat, EPS0)
                dve.tensor_tensor(all_rows(o_nat[:]), all_rows(o_nat[:]), row(1), ALU.mult).then_inc(gamma_done, 1)
                dve.wait_ge(gamma_done, 1)
                dve.tensor_tensor(all_rows(o_nat[:]), all_rows(o_nat[:]), row(2), ALU.add).then_inc(x1_ready, 1)
                dve.wait_ge(x1_ready, 1)
                norm(1, o_nat, x_hat, EPS1)
                dve.wait_ge(shift_ready, 1)
                for b, ps in each("turn_x"):
                    for j in range(CT):
                        ins = dve.tensor_scalar(xa_t[:, j, b, 1:], ps[:, j * L:(j + 1) * L], col("ln1_w", j), col("ln1_b", j), ALU.mult, ALU.add)
                    ins.then_inc(done["turn_x"], 1)
                dve.wait_ge(done["turn_x"], B)
                dve.tensor_tensor(sx[:].rearrange("p j b l -> p (j b) l"), xa_t[:, :, :, 0:L].rearrange("p j b l -> p (j b) l"),
                                  xa_t[:, :, :, 1:].rearrange("p j b l -> p (j b) l"), ALU.subtract).then_inc(sx_ready, 1)
                dve.wait_ge(sx_ready, 1)
                for j in range(CT):
                    dve.scalar_tensor_tensor(out=xxx[:, j], in0=sx[:, j], scalar=col("maa_x", j), in1=xa_t[:, j, :, 1:],
                                             op0=ALU.mult, op1=ALU.add).then_inc(xxx_ready, 1)

                def mix(f):
                    if f >= 3:
                        dve.wait_ge(full["dec1" if f == 3 else "p1"], COUNT["dec1" if f == 3 else "p1"])
                    for n, ps in each(f"m{f}"):
                        nb, j = place(n)
                        dve.scalar_tensor_tensor(out=two(mixed[f % 3][:, j], nb), in0=half(ps), scalar=col("maa_" + "wkvrg"[f], j),
                                                 in1=two(sx[:, j], nb), op0=ALU.add, op1=ALU.mult).then_inc(done[f"m{f}"], 1)

                for f in range(MIXES):
                    mix(f)
                dve.wait_ge(done["p1"], 4)
                dve.wait_ge(done["p3"], 4)
                dve.wait_ge(full["p2"], 4)
                for j in range(CT):
                    dve.scalar_tensor_tensor(out=mixed[2][:, j], in0=r_all[:, j], scalar=col("faaaa", j), in1=k_all[:, j],
                                             op0=ALU.mult, op1=ALU.mult).then_inc(rku_ready, 1)
                dve.wait_ge(done["p2"], 4)
                for n, ps in each("own"):
                    nb, j = place(n)
                    dve.tensor_tensor(two(sx[:, j], nb), half(ps), two(v_all[:, j], nb), ALU.mult).then_inc(done["own"], 1)
                dve.wait_ge(done["p4"], 4)
                dve.scalar_tensor_tensor(out=g_all[:], in0=xxx[:], scalar=1.0, in1=g_all[:], op0=ALU.add, op1=ALU.mult).then_inc(silu_ready, 1)
                dve.wait_ge(w_ready, 4)
                dve.wait_ge(silu_ready, 1)

                def recur(n):
                    j, b = n // B, n % B
                    dve.wait_ge(s0_placed, n + 1)
                    for i, ps in each("spread", 4 * n, 4 * n + 4):
                        i -= 4 * n
                        dve.tensor_tensor(kv_in[n % 2][:, 2 * i:2 * i + 2, 0:L], half(ps),
                                          k_all[:, j, b, :].unsqueeze(1).to_broadcast([P, 2, L]), ALU.mult).then_inc(done["spread"], 1)
                    dve.wait_ge(done["spread"], 4 * n + 4)
                    if n >= 2:
                        dve.wait_ge(read_ready, n - 1)
                    for t in range(HD):
                        ins = dve.tensor_tensor_scan(states[n % 2][:, t, 1:], w_all[:, j, b, :], kv_in[n % 2][:, t, 0:L],
                                                     states[n % 2][:, t, 0:1], ALU.mult, ALU.add)
                    ins.then_inc(scanned, 1)

                def add_own(n):
                    j, b = n // B, n % B
                    for _, ps in each("sum", n, n + 1):
                        dve.tensor_tensor(xxx[:, j, b, :], ps[:, 0:L], sx[:, j, b, :], ALU.add).then_inc(done["sum"], 1)

                for n in range(CT * B):
                    recur(n)
                    if n:
                        add_own(n - 1)
                add_own(CT * B - 1)
                dve.wait_ge(done["sum"], CT * B)
                for n, ps in each("mean"):
                    nb, j = place(n)
                    dve.tensor_tensor(two(k_all[:, j], nb), two(xxx[:, j], nb), half(ps), ALU.subtract).then_inc(done["mean"], 1)
                dve.wait_ge(gn_halved, 1)
                for n in range(4):
                    nb, j = place(n)
                    dve.wait_ge(done["var"], n + 1)
                    v, d = two(v_all[:, j], nb), two(k_all[:, j], nb)
                    dve.reciprocal(v, v).then_inc(inverted, 1)
                    dve.wait_ge(inverted, n + 1)
                    dve.wait_ge(squared, n + 1)
                    dve.tensor_tensor(d, d, v, ALU.mult).then_inc(normed, 1)
                    dve.wait_ge(normed, n + 1)
                    dve.tensor_scalar(d, d, col("gn_w", j), col("gn_b", j), ALU.mult, ALU.add).then_inc(scaled, 1)
                    dve.wait_ge(scaled, n + 1)
                    dve.tensor_tensor(d, d, two(g_all[:, j], nb), ALU.mult).then_inc(z_ready, 1)
                for b, ps in each("out1"):
                    dve.tensor_tensor(x_nat[:, b], ps[:].rearrange("p (t c) -> p t c", t=LT), o_nat[:, b], ALU.add).then_inc(done["out1"], 1)
                dve.wait_ge(done["out1"], B)
                for j in range(CT):
                    ins = dve.tensor_copy(xa_t[:, j, :, 0], state[:, j, 0:2 * B:2])
                ins.then_inc(shift2_ready, 1)
                norm(2, x_nat, x_hat, EPS1)
                for b, ps in each("turn_c"):
                    for j in range(CT):
                        ins = dve.tensor_scalar(xa_t[:, j, b, 1:], ps[:, j * L:(j + 1) * L], col("ln2_w", j), col("ln2_b", j), ALU.mult, ALU.add)
                    ins.then_inc(done["turn_c"], 1)
                dve.wait_ge(done["turn_c"], B)
                dve.tensor_tensor(sx[:].rearrange("p j b l -> p (j b) l"), xa_t[:, :, :, 0:L].rearrange("p j b l -> p (j b) l"),
                                  xa_t[:, :, :, 1:].rearrange("p j b l -> p (j b) l"), ALU.subtract).then_inc(sx2_ready, 1)
                dve.wait_ge(sx2_ready, 1)
                for to, name in ((r_all, "fmaa_k"), (v_all, "fmaa_r")):
                    for j in range(CT):
                        dve.scalar_tensor_tensor(out=to[:, j], in0=sx[:, j], scalar=col(name, j), in1=xa_t[:, j, :, 1:],
                                                 op0=ALU.mult, op1=ALU.add).then_inc(ffn_in, 1)
                gate = g_all[:].rearrange("p j b l -> p (j b l)")
                for b, ps in each("fv"):
                    dve.wait_ge(done["fr"], b + 1)
                    g = gate[:, b * BANK:(b + 1) * BANK]
                    dve.scalar_tensor_tensor(out=g, in0=g, scalar=1.0, in1=ps[:], op0=ALU.add, op1=ALU.mult).then_inc(done["fv"], 1)
                    dve.wait_ge(done["fv"], b + 1)
                    dve.scalar_tensor_tensor(out=o_nat[:, b], in0=g.rearrange("p (t c) -> p t c", t=LT), scalar=0.5, in1=x_nat[:, b],
                                             op0=ALU.mult, op1=ALU.add).then_inc(out_ready, 1)

            @block.sync
            def _(sp):
                for b in range(B):
                    sp.wait_ge(out_ready, b + 1)
                    sp.dma_start(out[b].rearrange("(t p) c -> p t c", p=P), o_nat[:, b]).then_inc(stored, 16)
                sp.wait_ge(stored, 16 * B)


_INS = {'x': 'x', 'ctx_2048': 'ctx', 'mask_Bx1xSxS2_ff0': 'mask', 'L0_xattn_Wq': 'Wq', 'L0_xattn_bq': 'bq', 'L0_xattn_Wk': 'Wk0',
        'L0_xattn_bk': 'bk', 'L0_xattn_Wv': 'Wv0', 'L0_xattn_bv': 'bv', 'L0_xattn_Wo': 'Wo0', 'L0_xattn_bo': 'bo',
        'L0_xattn_gamma': 'gamma', 'L0_xattn_beta': 'beta'}
_INS.update({f'L1_xattn_{n}': n for n in (*VECTORS, *TURNED, 'maa_w1', 'maa_w2', 'decay_w1', 'decay_w2')})


def kernel(**inputs):
    import numpy as _np
    import concourse.bacc as _bacc
    from concourse import mybir as _mybir
    from concourse.bass_utils import run_bass_kernel_spmd as _run

    nc = _bacc.Bacc("TRN2", target_bir_lowering=False, num_devices=1)
    arrays, args = {}, {}
    for name, short in _INS.items():
        v = _np.ascontiguousarray(inputs[name])
        arrays[f"in_{name}_dram"] = v
        args[short] = nc.dram_tensor(f"in_{name}_dram", v.shape, _mybir.dt.from_np(v.dtype), kind="ExternalInput").ap()
    out = nc.dram_tensor("out_0_dram", (B, L, C), _mybir.dt.float32, kind="ExternalOutput").ap()
    build(nc, args, out)
    r = _run(nc, [arrays], core_ids=[0])
    return r.results[0]["out_0_dram"]
```

```python
from contextlib import ExitStack

import concourse.bass as bass
from concourse import mybir

ALU = mybir.AluOpType
ACT = mybir.ActivationFunctionType
AX = mybir.AxisListType
F32 = mybir.dt.float32
BF16 = mybir.dt.bfloat16
I32 = mybir.dt.int32

P = 128

B, L, C = 4, 256, 256
S = 1601
NH, KVH, HD = 32, 8, 8
GROUPS = NH // KVH
LT = L // P
CT = C // P
ST = -(-S // P)
SLAST = S - (ST - 1) * P
UNITS = KVH // 2
UH = 2 * GROUPS
SPLIT = 64
TERMS = 6
BANK = 512
SCALE = HD ** -0.5
NEG = -3.0e38
EPS0, EPS1 = 1e-6, 1e-5

Q_PART = (0, 0, 1, 1, 0, 2)
K_PART = (0, 1, 0, 1, 2, 0)

CHUNK_EDGES = (0, 401, 801, 1201, S)
CHUNKS_PER_ROW = len(CHUNK_EDGES) - 1
CHUNK_BANKS = -(-max(hi - lo for lo, hi in zip(CHUNK_EDGES, CHUNK_EDGES[1:])) // BANK)
MAX_BUFFERS, SCORE_BUFFERS = 3, 3
A_PER_UNIT = UH * LT * CHUNKS_PER_ROW
A_PER_BATCH = A_PER_UNIT * UNITS
E_PER_TILE = 4
E_PER_UNIT = E_PER_TILE * ST
E_PER_BATCH = E_PER_UNIT * UNITS

CTX_ROUNDS, KV_ROUNDS = -(-ST // 2), -(-ST // 4)
PREP = ([("ctxT", n, "act") for n in range(CTX_ROUNDS)] + [("xT", 0, "act"), ("q", 0, "dve")]
        + [("kv", n, "dve") for n in range(KV_ROUNDS)])
for _u in range(UNITS):
    PREP += [("qT", _u, "act"), ("kT", 2 * _u, "act"), ("kT", 2 * _u + 1, "dve")]
PREP_ACT = sum(r[2] == "act" for r in PREP)
PREP_DVE = len(PREP) - PREP_ACT
BEFORE_UNITS = len(PREP) - 3 * UNITS


def emptied(n):
    return sum(r[2] == "act" for r in PREP[:n]), sum(r[2] == "dve" for r in PREP[:n])


def count(batch, per_batch, n):
    reg, more = batch
    return more * per_batch + n if reg is None else reg * per_batch + (more * per_batch + n)


MIXES, DM, DD = 5, 32, 64
TURNED = ("Wk", "Wv", "Wr", "Wg", "Wo", "fWk", "fWr", "fWv")
VECTORS = ("ln1_w", "ln1_b", "ln2_w", "ln2_b", "maa_x", "maa_w", "maa_k", "maa_v", "maa_r", "maa_g",
           "time_decay", "faaaa", "gn_w", "gn_b", "fmaa_k", "fmaa_r")

LEAD, TURN = 5, 2
UNIT_LENGTH = 32
EXP_AT = (0.1, 0.25, 0.5, 0.75)
VALUES_AT = 1.0
AHEAD = LEAD + 3
PREP_START, PREP_EVERY = 14, 3.5


def order():
    tile = UNIT_LENGTH / ST
    items = []

    def add(at, *item):
        items.append((at, item))

    for g in range(UNITS + 2):
        for n in range(A_PER_UNIT):
            add(UNIT_LENGTH * g + n * UNIT_LENGTH / A_PER_UNIT, "max", g // UNITS, g % UNITS, n)
        if g <= UNITS:
            add(UNIT_LENGTH * (g + 1) + TURN - 0.9, "turn", g // UNITS, g % UNITS, 0)
    start, end = UNIT_LENGTH + AHEAD, UNIT_LENGTH * (UNITS + 1) + AHEAD
    for u in range(UNITS):
        after = UNIT_LENGTH * (u + 1) + LEAD
        for t in range(ST):
            for j in range(E_PER_TILE):
                add(after + tile * (t + EXP_AT[j]) + 0.1, "exp", 0, u, (t, j))
            if t:
                add(after + tile * (t + VALUES_AT), "values", 0, u, t - 1)
        add(after + UNIT_LENGTH + 0.05, "values", 0, u, ST - 1)
        add(after + UNIT_LENGTH + 0.06, "copy", 0, u, 0)
        add(after + UNIT_LENGTH + (2 * tile if u < UNITS - 1 else 1.5), "normal", 0, u, 0)

    def turned(at, batch, u):
        for k in range(3):
            add(at + 2 * k + 0.5, "prep", batch, 0, BEFORE_UNITS + 3 * u + k)
        add(at + 5.5, "v_copy", batch, u, 0)

    turned(start + 1, 0, UNITS - 1)
    at = start + PREP_START
    for n in range(BEFORE_UNITS):
        add(at + 0.4, "prep", 1, 0, n)
        at += PREP_EVERY
        if n in (CTX_ROUNDS + 1, BEFORE_UNITS - 1):
            which = 0 if n == CTX_ROUNDS + 1 else 1
            for k in range(5):
                add(at + 0.45 + k, "split", 1, which, k)
            add(at + 6.45, "copy_terms", 1, which, 0)
            if which:
                at += 7
    for u in range(UNITS - 1):
        turned(max(at, UNIT_LENGTH * (u + 2) + LEAD + 1), 1, u)
        at += 9
    after = UNIT_LENGTH * UNITS
    for lt in range(LT):
        add(after - 4 + 20 * lt + 0.7, "mask_sum", 1, lt, 0)
    add(after + 20 + 0.7, "mask_any", 1, 0, 0)
    add(after + 22 + 0.7, "mask_count", 1, 0, 0)
    add(after + 24 + 0.7, "mask_flag", 1, 0, 0)
    items.sort(key=lambda x: x[0])
    step = [item for at, item in items if (start <= at < end if item[0] == "max" else UNIT_LENGTH + TURN < at)]
    last = [item for item in step if item[1] == 0]

    first = []
    for n in range(BEFORE_UNITS + 3):
        if n == BEFORE_UNITS:
            first.append(("copy_terms", 0, 0, 0))
        if n == BEFORE_UNITS + 1:
            first.append(("copy_terms", 0, 1, 0))
        first.append(("prep", 0, 0, n))
        if n in (CTX_ROUNDS + 1, BEFORE_UNITS - 1):
            first += [("split", 0, int(n == BEFORE_UNITS - 1), k) for k in range(5)]
    first.append(("v_copy", 0, 0, 0))
    items = [x for x in items if (x[1][0] == "max" and x[0] < start) or (x[1][0] == "turn" and x[0] < start)]
    for u in range(1, UNITS - 1):
        for k in range(3):
            add(13 * (u - 1) + 4 * k + 3.5, "prep", 0, 0, BEFORE_UNITS + 3 * u + k)
        add(13 * u, "v_copy", 0, u, 0)
    add(13.2, "mask_sum", 0, 0, 0)
    add(25.2, "mask_sum", 0, 1, 0)
    for k, name in enumerate(("mask_any", "mask_count", "mask_flag")):
        add(28.2 + k, name, 0, 0, 0)
    items.sort(key=lambda x: x[0])
    return first + [item for _, item in items], step, last


FIRST_STEP, STEP, LAST_STEP = order()


def rows_of(tile):
    return SLAST if tile == ST - 1 else P


def build(nc, a, out):
    with ExitStack() as whole:
        def sb(name, shape, dt):
            return whole.enter_context(nc.sbuf_tensor(name, shape, dt))

        def sem(name):
            return whole.enter_context(nc.semaphore(name))

        held = {
            "ident_f": sb("ident_f", [P, P], F32),
            "x_nat": sb("x_nat", [P, B, LT, C], F32),
            "o_nat": sb("o_nat", [P, B, LT, C], F32),
            "w_nat": sb("w_nat", [P, len(TURNED), CT, C], F32),
            "wo": sb("wo", [P, CT, C], F32),
            "maa_w1": sb("maa_w1", [P, CT, MIXES * DM], F32),
            "maa_w2": sb("maa_w2", [P, C], F32),
            "maa_w2_last": sb("maa_w2_last", [DM, C], F32),
            "decay_w1": sb("decay_w1", [P, CT, DD], F32),
            "decay_w2": sb("decay_w2", [DD, C], F32),
            "rows": sb("rows", [P, 3, C], F32),
            "vec_nat": sb("vec_nat", [CT * len(VECTORS), P], F32),
            "state_nat": sb("state_nat", [2 * B, C], F32),
            "s0": sb("s0", [P, CT, B, HD], F32),
            "ctx_nat": sb("ctx_nat", [P, ST, C], F32),
        }
        loads_in = sem("loads_in")
        attention(nc, sem, held, loads_in, a)
        mixing(nc, sem, held, loads_in, out)


N_LOADS = 10 + len(TURNED) + len(VECTORS) + 2 * B


def load_second_part(eng, held, loads_in, a):
    pairs = [(held["x_nat"][:], a["x"].rearrange("b (t p) c -> p b t c", p=P)),
             (held["wo"][:], a["Wo0"].rearrange("(t p) n -> p t n", p=P)),
             (held["maa_w1"][:], a["maa_w1"].rearrange("(t p) n -> p t n", p=P)),
             (held["maa_w2"][:], a["maa_w2"][0:MIXES - 1].rearrange("f d c -> (f d) c")),
             (held["maa_w2_last"][:], a["maa_w2"][MIXES - 1]),
             (held["decay_w1"][:], a["decay_w1"].rearrange("(t p) n -> p t n", p=P)),
             (held["decay_w2"][:], a["decay_w2"])]
    pairs += [(held["rows"][:, n, :], a[name].partition_broadcast(P)) for n, name in enumerate(("bo", "gamma", "beta"))]
    pairs += [(held["w_nat"][:, n], a[name].rearrange("(t p) n -> p t n", p=P)) for n, name in enumerate(TURNED)]
    for n, name in enumerate(VECTORS):
        v = a[name]
        if len(v.shape) > 1:
            v = v.rearrange("h s a -> (h s a)")
        pairs.append((held["vec_nat"][CT * n:CT * (n + 1), :], v.rearrange("(t p) -> t p", p=P)))
    for b in range(B):
        pairs.append((held["state_nat"][2 * b:2 * b + 2, :], a["ctx"][b, 0:2, :]))
        pairs.append((held["s0"][:, :, b, :],
                      a["ctx"][b, 2:2 + HD, :].rearrange("r c -> (r c)").rearrange("(j p t) -> p j t", j=CT, t=HD)))
    assert len(pairs) == N_LOADS
    for to, of in pairs:
        eng.dma_start(to, of).then_inc(loads_in, 16)


def selectors_in(held):
    place = held["ctx_nat"][:].rearrange("p t c -> p (t c)")
    selectors, at = [], 0
    for shape in ([HD, NH // 2, HD],
                  [HD, NH // 2, HD],
                  [NH // 2, HD],
                  [NH // 2, HD],
                  [1]):
        size = 1
        for n in shape:
            size *= n
        view = place[:, at:at + size]
        if len(shape) == 3:
            view = view.rearrange("p (t h s) -> p t h s", t=shape[0], h=shape[1])
        elif len(shape) == 2:
            view = view.rearrange("p (h s) -> p h s", h=shape[0])
        selectors.append(view)
        at += size
    return selectors


def attention(nc, sem, held, loads_in, a):
    x, ctx_in, mask, Wq, bq, Wk, bk, Wv, bv = (a[n] for n in ("x", "ctx", "mask", "Wq", "bq", "Wk0", "bk", "Wv0", "bv"))
    ident_f, o_nat = held["ident_f"], held["o_nat"]
    with ExitStack() as here:
        def sb(name, shape, dt):
            return here.enter_context(nc.sbuf_tensor(name, shape, dt))

        def psum(name, shape, dt):
            return here.enter_context(nc.psum_tensor(name, shape, dt))

        ident_b = sb("ident_b", [P, P], BF16)
        wq = sb("wq", [P, CT, C], F32)
        wkv = sb("wkv", [P, CT, 2 * KVH * HD], F32)
        bq_row = sb("bq_row", [P, C], F32)
        bkv_row = sb("bkv_row", [P, 2 * KVH * HD], F32)
        ones_col = sb("ones_col", [P, 1], F32)
        x_bat = sb("x_bat", [P, LT, C], F32)
        ctx_nat = held["ctx_nat"]
        ctx_t = sb("ctx_t", [P, CT, ST * P], F32)
        mask_max = sb("mask_max", [P, LT, S], F32)
        mask_exp = sb("mask_exp", [P, LT, S], F32)
        mask_abs = sb("mask_abs", [P, S], BF16)
        mask_sum = sb("mask_sum", [P, LT], F32)
        mask_any = sb("mask_any", [P, LT], F32)
        mask_flag = sb("mask_flag", [1, 1], I32)
        x_t = sb("x_t", [P, CT, L], F32)
        q_f = sb("q_f", [P, LT * C], F32)
        q_rest = sb("q_rest", [P, LT * C], F32)
        q_aug = sb("q_aug", [P, LT, NH, SPLIT], BF16)
        k_f = sb("k_f", [P, ST, KVH * HD], F32)
        k_rest = sb("k_rest", [P, ST * KVH * HD], F32)
        k_aug = sb("k_aug", [P, ST, KVH, SPLIT], BF16)
        v_f = sb("v_f", [P, ST, KVH * HD], F32)
        v_aug = sb("v_aug", [P, ST, KVH, 32], F32)
        q_t = sb("q_t", [P, UNITS, 2, GROUPS, L], BF16)
        k_t = sb("k_t", [P, UNITS, ST * P], BF16)
        max_part = sb("max_part", [P, LT, 2, GROUPS, CHUNKS_PER_ROW], F32)
        zeros = sb("zeros", [P, LT, 2, GROUPS], F32)
        neg_max = sb("neg_max", [P, LT, 2, GROUPS], F32)
        max_rest = sb("max_rest", [P, 2, LT, 2, GROUPS], F32)
        max_split = sb("max_split", [P, LT, 2, 3, GROUPS], BF16)
        max_t = sb("max_t", [24, L], BF16)
        probs = sb("probs", [P, 2, E_PER_TILE, BANK], F32)
        pv_sb = sb("pv_sb", [P, BANK], F32)
        row_sum = sb("row_sum", [P, LT, 2, 4], F32)

        p_max = psum("p_max", [P, MAX_BUFFERS, CHUNK_BANKS, BANK], F32)
        p_sc = psum("p_sc", [P, SCORE_BUFFERS, BANK], F32)
        p_pv = psum("p_pv", [P, BANK], F32)
        p_side = psum("p_side", [P, BANK], F32)
        def t_buf(u, t):
            return (ST * u + t) % 2

        def block_of(aug, term):
            return aug.rearrange("p t h c -> p (t h) c")[:, :, term * HD:(term + 1) * HD]

        def operand(what, i, src):
            src_b = src.bitcast(BF16)
            if what == "qT":
                return [(q_t[SPLIT * half:SPLIT * (half + 1), i, half].rearrange("p h l -> p (h l)"),
                         src_b[SPLIT * half:SPLIT * (half + 1), :]) for half in range(2)]
            lo = 8 * (i % 2) * P
            hi = min(lo + 8 * P, S)
            return [(k_t[:, i // 2, lo:hi], src_b[:, 0:hi - lo])]

        ring = [*(p_max[:, k, 0, :] for k in range(MAX_BUFFERS)), *(p_sc[:, k, :] for k in range(4 - MAX_BUFFERS))]

        weights_in = sem("weights_in")
        ctx_loaded = sem("ctx_loaded")
        mask_loaded = [sem(f"mask_loaded{lt}") for lt in range(LT)]
        mask_exp_loaded = sem("mask_exp_loaded")
        v_copied = sem("v_copied")
        const_ready = sem("const_ready")
        bias_in = sem("bias_in")
        prep_full = sem("prep_full")
        prep_act = sem("prep_act")
        prep_dve = sem("prep_dve")
        operands_clear = sem("operands_clear")
        q_split = sem("q_split")
        k_split = sem("k_split")
        q_copied = sem("q_copied")
        k_copied = sem("k_copied")
        mask_summed = [sem(f"mask_summed{lt}") for lt in range(LT)]
        mask_counted = sem("mask_counted")
        mask_anyed = sem("mask_anyed")
        mask_flagged = sem("mask_flagged")
        max_full = sem("max_full")
        max_seen = sem("max_seen")
        flag_seen = sem("flag_seen")
        max_done = sem("max_done")
        max_ready = sem("max_ready")
        max_turned = sem("max_turned")
        max_copied = sem("max_copied")
        max_placed = sem("max_placed")
        sc_full = sem("sc_full")
        exp_done = sem("exp_done")
        pv_done = sem("pv_done")
        pv_copied = sem("pv_copied")
        o_turned = sem("o_turned")
        o_summed = sem("o_summed")
        bias_scaled = sem("bias_scaled")
        o_done = sem("o_done")
        pool_step = sem("pool_step")
        selector_step = sem("selector_step")

        POOL_START, MAX_STEPS = 5, 5
        POOL_PER_BATCH = UNITS * MAX_STEPS

        with nc.Block() as block:

            @block.sync
            def _(sp):
                sp.dma_start(wkv[:, :, 0:KVH * HD], Wk.rearrange("(t p) n -> p t n", p=P)).then_inc(weights_in, 16)
                sp.dma_start(wkv[:, :, KVH * HD:], Wv.rearrange("(t p) n -> p t n", p=P)).then_inc(weights_in, 16)
                sp.dma_start(wq[:], Wq.rearrange("(t p) n -> p t n", p=P)).then_inc(weights_in, 16)
                sp.sem_inc(max_placed, 16)

                def load_context(b):
                    sp.dma_start(x_bat[:], x[b, :, :].rearrange("(t p) c -> p t c", p=P)).then_inc(ctx_loaded, 16)
                    sp.dma_start(ctx_nat[:, 0:ST - 1, :],
                                 ctx_in[b, 0:(ST - 1) * P, :].rearrange("(t p) c -> p t c", p=P)).then_inc(ctx_loaded, 16)
                    sp.dma_start(ctx_nat[0:SLAST, ST - 1, :], ctx_in[b, (ST - 1) * P:S, :]).then_inc(ctx_loaded, 16)

                def load_mask(b, lt):
                    sp.dma_start(mask_max[:, lt, :], mask[b, 0, lt * P:(lt + 1) * P, :]).then_inc(mask_loaded[lt], 16)

                def load_mask_exp(b):
                    sp.dma_start(mask_exp[:], mask[b, 0, :, :].rearrange("(t p) s -> p t s", p=P)).then_inc(mask_exp_loaded, 16)

                def place_maxima(batch, u):
                    sp.wait_ge(max_copied, count(batch, UNITS, u + 1))
                    for half in range(2):
                        row = SPLIT * half + TERMS * HD
                        sp.dma_start(q_t[row:row + 3, u, half, :, :], max_t[12 * half:12 * half + 12, :]).then_inc(max_placed, 16)

                load_context(0)
                for lt in range(LT):
                    load_mask(0, lt)
                load_mask_exp(0)
                load_second_part(sp, held, loads_in, a)
                place_maxima((None, 0), 0)
                with sp.Fori(0, B - 1) as b:
                    sp.wait_ge(prep_act, b * PREP_ACT + (CTX_ROUNDS + 1))
                    load_context(b + 1)
                    for u in range(1, UNITS):
                        if u == UNITS - 1:
                            sp.wait_ge(max_done, b * A_PER_BATCH + (A_PER_BATCH - A_PER_UNIT // 2 + MAX_BUFFERS - 1))
                            sp.wait_ge(mask_summed[0], b + 1)
                            load_mask(b + 1, 0)
                        place_maxima((b, 0), u)
                    sp.wait_ge(max_done, b * A_PER_BATCH + (A_PER_BATCH + MAX_BUFFERS - 1))
                    sp.wait_ge(mask_summed[1], b + 1)
                    load_mask(b + 1, 1)
                    place_maxima((b, 1), 0)
                    sp.wait_ge(mask_exp_loaded, b * 16 + 16)
                    sp.wait_ge(sc_full, b * E_PER_BATCH + E_PER_BATCH)
                    load_mask_exp(b + 1)
                for u in range(1, UNITS):
                    place_maxima((None, B - 1), u)
                sp.wait_ge(max_placed, 16 + 32 * UNITS * B)
                sp.wait_ge(mask_exp_loaded, 16 * B)

            @block.gpsimd
            def _(pool):
                pool.memset(ident_f[:], 0.0).then_inc(pool_step, 1)
                pool.memset(ident_b[:], 0.0).then_inc(pool_step, 1)
                pool.memset(ones_col[:], 1.0)
                pool.memset(v_aug[:], 0.0).then_inc(pool_step, 1)
                pool.memset(zeros[:], 0.0).then_inc(pool_step, 1)
                pool.memset(v_f[:], 0.0).then_inc(pool_step, 1)
                pool.wait_ge(pool_step, POOL_START)
                for m in (ident_f, ident_b):
                    pool.affine_select(out=m[:], in_=m[:], compare_op=ALU.not_equal, fill=1.0, base=0,
                                       pattern=[[-1, P]], channel_multiplier=1)
                pool.memset(v_aug[:, :, :, HD:HD + 1], 1.0).then_inc(const_ready, 1)

                def split_maxima(batch, u):
                    pool.wait_ge(max_ready, count(batch, UNITS, u + 1))
                    pool.wait_ge(max_turned, count(batch, UNITS, u + 1))
                    value = neg_max[:]
                    for k in range(3):
                        part = max_split[:, :, :, k, :]
                        done = POOL_START + MAX_STEPS * u + 2 * k + 1
                        pool.tensor_tensor(part, value, zeros[:], ALU.add).then_inc(pool_step, 1)
                        pool.wait_ge(pool_step, count(batch, POOL_PER_BATCH, done))
                        if k < 2:
                            pool.tensor_tensor(max_rest[:, k], value, part, ALU.subtract).then_inc(pool_step, 1)
                            pool.wait_ge(pool_step, count(batch, POOL_PER_BATCH, done + 1))
                            value = max_rest[:, k]

                def copy_values(batch, u, first):
                    pool.wait_ge(prep_dve, count(batch, PREP_DVE, 1 + KV_ROUNDS))
                    if not first:
                        pool.wait_ge(pv_done, count(batch, UNITS * ST, ST * (u + 1) + 2 - UNITS * ST))
                    pool.tensor_tensor(v_aug[:, :, 2 * u:2 * u + 2, 0:HD],
                                       v_f[:, :, 2 * u * HD:2 * (u + 1) * HD].rearrange("p t (h d) -> p t h d", d=HD),
                                       zeros[:].rearrange("p t a h -> p (t a h)")[:, 0:2 * HD].rearrange("p (h d) -> p h d", d=HD)
                                       .unsqueeze(1).to_broadcast([P, ST, 2, HD]), ALU.add).then_inc(v_copied, 1)

                def walk(items, reg, first, more=0):
                    for kind, batch, u, _ in items:
                        if kind == "turn":
                            split_maxima((reg, more + batch), u)
                        elif kind == "v_copy":
                            copy_values((reg, more + batch), u, first)

                walk(FIRST_STEP, None, True)
                with pool.Fori(0, B - 1) as b:
                    walk(STEP, b, False)
                walk(LAST_STEP, None, False, B - 1)
                spread, gather, heads, eighth, eps_col = selectors_in(held)
                pool.wait_ge(prep_act, PREP_ACT * (B - 1) + CTX_ROUNDS)
                for m, v in ((spread, 0.0), (gather, 1.0), (heads, 1.0)):
                    pool.memset(m, v).then_inc(selector_step, 1)
                pool.memset(eps_col, EPS1)
                pool.wait_ge(selector_step, 3)
                pool.affine_select(out=spread, in_=spread, compare_op=ALU.not_equal, fill=1.0, base=0,
                                   pattern=[[-1, HD], [-HD, NH // 2], [0, HD]], channel_multiplier=1).then_inc(selector_step, 1)
                done = 4
                for m, pattern in ((heads, [[HD, NH // 2], [0, HD]]), (gather, [[0, HD], [HD, NH // 2], [0, HD]])):
                    pool.affine_select(out=m, in_=m, compare_op=ALU.is_ge, fill=0.0, base=0,
                                       pattern=[[-step, n] for step, n in pattern], channel_multiplier=1).then_inc(selector_step, 1)
                    done += 1
                    pool.wait_ge(selector_step, done)
                    pool.affine_select(out=m, in_=m, compare_op=ALU.is_ge, fill=0.0, base=HD - 1,
                                       pattern=pattern, channel_multiplier=-1).then_inc(selector_step, 1)
                    done += 1
                    pool.wait_ge(selector_step, done)
                pool.affine_select(out=gather, in_=gather, compare_op=ALU.is_equal, fill=0.0, base=0,
                                   pattern=[[1, HD], [0, NH // 2], [-1, HD]], channel_multiplier=0)
                pool.tensor_scalar(eighth, heads, 1.0 / HD, None, ALU.mult)
                pool.wait_ge(loads_in, 16 * N_LOADS)
                for b in range(B):
                    pool.tensor_tensor(held["x_nat"][:, b], held["x_nat"][:, b], held["rows"][:, 0, :].unsqueeze(1).to_broadcast([P, LT, C]), ALU.add)

            @block.tensor
            def _(pe):
                pe.sem_inc(pv_done, 2)
                pe.sem_inc(o_turned, 1)
                pe.sem_inc(max_turned, 1)
                pe.wait_ge(const_ready, 1)
                pe.wait_ge(weights_in, 48)

                def prep(batch, n, ahead):
                        what, i, _ = PREP[n]
                        if ahead:
                            out = p_side[:]
                            side_bank_free()
                            side_user[0] = ("prep", batch, n)
                        else:
                            out = ring[n % 4]
                            if n >= 4:
                                by_act, by_dve = emptied(n - 3)
                                pe.wait_ge(prep_act, by_act)
                                if by_dve:
                                    pe.wait_ge(prep_dve, by_dve)
                        out_b = out.bitcast(BF16)
                        if what == "ctxT":
                            if i == 0:
                                pe.wait_ge(ctx_loaded, count(batch, 48, 48))
                            for t in range(2 * i, min(2 * i + 2, ST)):
                                r = rows_of(t)
                                for j in range(CT):
                                    at = (2 * (t % 2) + j) * P
                                    mm = pe.transpose(out[:, at:at + r], ctx_nat[0:r, t, j * P:(j + 1) * P], ident_f[0:r, 0:r])
                        elif what == "xT":
                            for lt in range(LT):
                                for j in range(CT):
                                    mm = pe.transpose(out[:, j * L + lt * P:j * L + (lt + 1) * P],
                                                      x_bat[:, lt, j * P:(j + 1) * P], ident_f[:])
                        elif what == "q":
                            pe.wait_ge(prep_act, count(batch, PREP_ACT, CTX_ROUNDS + 1))
                            for lt in range(LT):
                                for j in range(CT):
                                    mm = pe.matmul(out[:, lt * C:(lt + 1) * C], x_t[:, j, lt * P:(lt + 1) * P], wq[:, j, :],
                                                   start=(j == 0), stop=(j == CT - 1))
                        elif what == "kv":
                            for t in range(4 * i, min(4 * i + 4, ST)):
                                r = rows_of(t)
                                for j in range(CT):
                                    mm = pe.matmul(out[0:r, (t % 4) * P:(t % 4 + 1) * P], ctx_t[:, j, t * P:t * P + r],
                                                   wkv[:, j, :], start=(j == 0), stop=(j == CT - 1))
                        elif what == "qT":
                            if i == 0:
                                pe.wait_ge(q_split, count(batch, 5, 5))
                                pe.wait_ge(q_copied, count(batch, 1, 1))
                            for hh in range(GROUPS):
                                for lt in range(LT):
                                    pair = q_aug[:, lt, UH * i + 2 * hh:UH * i + 2 * hh + 2, :].rearrange("p h c -> p (h c)")
                                    at = hh * L + lt * P
                                    mm = pe.transpose(out_b[:, at:at + P], pair, ident_b[:])
                        else:
                            if i == 0:
                                pe.wait_ge(k_split, count(batch, 5, 5))
                                pe.wait_ge(k_copied, count(batch, 1, 1))
                            for t in range(8 * (i % 2), min(8 * (i % 2) + 8, ST)):
                                r = rows_of(t) + rows_of(t) % 2
                                at = (t % 8) * P
                                mm = pe.transpose(out_b[:, at:at + r],
                                                  k_aug[0:r, t, i - i % 2:i - i % 2 + 2, :].rearrange("p h c -> p (h c)"), ident_b[0:r, 0:r])
                        mm.then_inc(prep_full, 1)

                def row_max(batch, u, n, first):
                    row, k = divmod(n, CHUNKS_PER_ROW)
                    lt, half, hh = row // UH, row // GROUPS % 2, row % GROUPS
                    a = A_PER_UNIT * u + n
                    if n == 0:
                        by_act, by_dve = emptied(BEFORE_UNITS + 3 * (u + 1))
                        pe.wait_ge(prep_act, count(batch, PREP_ACT, by_act))
                        pe.wait_ge(prep_dve, count(batch, PREP_DVE, by_dve))
                    if first and u == 0 and n < MAX_BUFFERS:
                        pe.wait_ge(prep_act, emptied(BEFORE_UNITS + 3)[0])
                    else:
                        pe.wait_ge(max_done, count(batch, A_PER_BATCH, max(a, MAX_BUFFERS - 1)))
                    for bank, s0 in enumerate(range(CHUNK_EDGES[k], CHUNK_EDGES[k + 1], BANK)):
                        s1 = min(s0 + BANK, CHUNK_EDGES[k + 1])
                        mm = pe.matmul(p_max[:, (A_PER_UNIT * u + n) % MAX_BUFFERS, bank, 0:s1 - s0], q_t[:, u, half, hh, lt * P:(lt + 1) * P],
                                       k_t[:, u, s0:s1], start=True, stop=True)
                    mm.then_inc(max_full, 1)

                def turn_maxima(batch, u):
                    pe.wait_ge(pool_step, count(batch, POOL_PER_BATCH, POOL_START + MAX_STEPS * (u + 1)))
                    side_bank_free()
                    side_user[0] = ("turn", batch, u)
                    for lt in range(LT):
                        mm = pe.transpose(p_side[0:24, :].bitcast(BF16)[:, lt * P:(lt + 1) * P],
                                          max_split[:, lt].rearrange("p a k h -> p (a k h)"), ident_b[:])
                    mm.then_inc(max_turned, 1)

                def scores(batch, u, t, j, masked):
                    e = E_PER_UNIT * u + E_PER_TILE * t + j
                    half, r = j // 2, rows_of(t)
                    heads = slice(2 * (j % 2), 2 * (j % 2) + 2)
                    if t == 0 and j == 0:
                        pe.wait_ge(max_placed, count(batch, 32 * UNITS, 32 * (u + 1) + 16))
                        if masked and u == 0:
                            pe.wait_ge(mask_exp_loaded, count(batch, 16, 16))
                    pe.wait_ge(exp_done, count(batch, E_PER_BATCH, max(e + 1, SCORE_BUFFERS)))
                    out = p_sc[0:r, e % SCORE_BUFFERS, :]
                    mm = pe.matmul(out, k_t[:, u, t * P:t * P + r], q_t[:, u, half, heads, :], start=True, stop=not masked)
                    if masked:
                        for h in range(2):
                            for lt in range(LT):
                                at = h * L + lt * P
                                mm = pe.matmul(out[:, at:at + P], mask_exp[:, lt, t * P:t * P + r], ident_f[:],
                                               start=False, stop=(lt == LT - 1 and h == 1))
                    mm.then_inc(sc_full, 1)

                def values(batch, u, t):
                    r = rows_of(t)
                    pe.wait_ge(exp_done, count(batch, E_PER_BATCH, E_PER_UNIT * u + E_PER_TILE * (t + 1) + SCORE_BUFFERS))
                    if t == 0:
                        pe.wait_ge(v_copied, count(batch, UNITS, u + 1))
                        pe.wait_ge(pv_copied, count(batch, UNITS, u + 1))
                    for j in range(4):
                        mm = pe.matmul(p_pv[32 * j:32 * j + 32, :], v_aug[0:r, t, 2 * u + j // 2, :], probs[0:r, t_buf(u, t), j, :],
                                       start=(t == 0), stop=(t == ST - 1), tile_position=(0, 32 * j))
                    mm.then_inc(pv_done, 1)

                def turn_output(batch, u):
                    pe.wait_ge(pv_copied, count(batch, UNITS, u + 2))
                    side_bank_free()
                    side_user[0] = ("normal", batch, u)
                    for lt in range(LT):
                        for e in range(2):
                            k = 2 * lt + e
                            mm = pe.transpose(p_side[:, k * P:(k + 1) * P], pv_sb[:, e * L + lt * P:e * L + (lt + 1) * P], ident_f[:])
                    mm.then_inc(o_turned, 1)

                def count_mask(batch):
                    pe.wait_ge(mask_anyed, count(batch, 1, 1))
                    side_bank_free()
                    side_user[0] = ("mask_count", batch, 0)
                    for lt in range(LT):
                        mm = pe.matmul(p_side[0:1, 0:1], mask_any[:, lt:lt + 1], ones_col[:], start=(lt == 0), stop=(lt == LT - 1))
                    mm.then_inc(mask_counted, 1)

                side_user = [None]

                def side_bank_free():
                    if side_user[0] is None:
                        return
                    kind, batch, n = side_user[0]
                    if kind == "prep":
                        if PREP[n][2] == "act":
                            pe.wait_ge(prep_act, count(batch, PREP_ACT, emptied(n + 1)[0]))
                        else:
                            pe.wait_ge(prep_dve, count(batch, PREP_DVE, emptied(n + 1)[1]))
                    elif kind == "mask_count":
                        pe.wait_ge(mask_flagged, count(batch, 1, 1))
                    elif kind == "turn":
                        pe.wait_ge(max_copied, count(batch, UNITS, n + 1))
                    elif kind == "normal":
                        pe.wait_ge(o_done, count(batch, UNITS, n + 2))
                    else:
                        pe.wait_ge(max_copied, count(batch, UNITS, 1))
                        pe.wait_ge(o_done, count(batch, UNITS, 1))

                def walk(items, reg, masked, more=0, first=False):
                    side_user[0] = None if first else ("step", (reg, more), 0)
                    for kind, batch, u, n in items:
                        batch = (reg, more + batch)
                        if kind == "max":
                            row_max(batch, u, n, first)
                        elif kind == "exp":
                            scores(batch, u, *n, masked)
                        elif kind == "values":
                            values(batch, u, n)
                        elif kind == "turn":
                            turn_maxima(batch, u)
                        elif kind == "normal":
                            turn_output(batch, u)
                        elif kind == "prep":
                            prep(batch, n, not first or n >= BEFORE_UNITS + 3)
                        elif kind == "mask_count":
                            count_mask(batch)

                def by_mask(items, reg, more=0):
                    pe.wait_ge(mask_flagged, count((reg, more), 1, 1))
                    pe.sem_inc(flag_seen, 1)
                    flag = pe.value_load(mask_flag[0:1, 0:1])
                    with pe.If(flag > 0):
                        walk(items, reg, True, more)
                    with pe.Else():
                        walk(items, reg, False, more)

                walk(FIRST_STEP, None, False, first=True)
                with pe.Fori(0, B - 1) as b:
                    by_mask(STEP, b)
                by_mask(LAST_STEP, None, B - 1)

            @block.scalar
            def _(act):
                act.dma_start(bq_row[:], bq.partition_broadcast(P)).then_inc(bias_in, 16)
                act.dma_start(bkv_row[:, 0:KVH * HD], bk.partition_broadcast(P)).then_inc(bias_in, 16)
                act.dma_start(bkv_row[:, KVH * HD:], bv.partition_broadcast(P)).then_inc(bias_in, 16)
                act.sem_inc(exp_done, SCORE_BUFFERS)
                act.sem_inc(pv_copied, 1)

                def copy_terms(batch, which):
                    aug, parts, split, copied = ((q_aug[:], Q_PART, q_split, q_copied), (k_aug[:], K_PART, k_split, k_copied))[which]
                    for term, part in enumerate(parts):
                        first = parts.index(part)
                        if term != first:
                            act.wait_ge(split, count(batch, 5, 2 * part + 1))
                            last = act.activation(block_of(aug, term), block_of(aug, first), ACT.Copy)
                    last.then_inc(copied, 1)

                def prep(batch, n, ahead):
                    what, i, who = PREP[n]
                    if who != "act":
                        return
                    act.wait_ge(prep_full, count(batch, len(PREP), n + 1))
                    src = p_side[:] if ahead else ring[n % 4]
                    if what == "ctxT":
                        tiles = min(2, ST - 2 * i)
                        w = rows_of(2 * i)
                        ins = act.activation(
                            ctx_t[:, :, 2 * i * P:(2 * i + tiles) * P].rearrange("p j (t s) -> p t j s", s=P)[:, :, :, 0:w],
                            src[:, 0:tiles * CT * P].rearrange("p (t j s) -> p t j s", j=CT, s=P)[:, :, :, 0:w], ACT.Copy)
                    elif what == "xT":
                        ins = act.activation(x_t[:].rearrange("p j l -> p (j l)"), src, ACT.Copy)
                    else:
                        for to, of in operand(what, i, src):
                            ins = act.activation(to, of, ACT.Copy)
                    ins.then_inc(prep_act, 1)

                def exponential(batch, u, t, j):
                    r, e = rows_of(t), E_PER_UNIT * u + E_PER_TILE * t + j
                    act.wait_ge(sc_full, count(batch, E_PER_BATCH, e + 1))
                    if j == 0:
                        act.wait_ge(pv_done, count(batch, UNITS * ST, ST * u + t + 1))
                    act.activation(probs[0:r, t_buf(u, t), j, :], p_sc[0:r, e % SCORE_BUFFERS, :], ACT.Exp).then_inc(exp_done, 1)

                def walk(items, reg, more=0, first=False):
                    for kind, batch, u, n in items:
                        batch = (reg, more + batch)
                        if kind == "exp":
                            exponential(batch, u, *n)
                        elif kind == "turn":
                            act.wait_ge(max_turned, count(batch, UNITS, u + 2))
                            act.wait_ge(max_placed, count(batch, 32 * UNITS, 32 * u + 16))
                            act.activation(max_t[:], p_side[0:24, :].bitcast(BF16)[:, 0:L], ACT.Copy).then_inc(max_copied, 1)
                        elif kind == "copy":
                            act.wait_ge(pv_done, count(batch, UNITS * ST, ST * (u + 1) + 2))
                            act.wait_ge(o_turned, count(batch, UNITS, u + 1))
                            act.activation(pv_sb[:], p_pv[:], ACT.Copy).then_inc(pv_copied, 1)
                        elif kind == "prep":
                            prep(batch, n, not first or n >= BEFORE_UNITS + 3)
                        elif kind == "copy_terms":
                            copy_terms(batch, u)
                        elif kind == "mask_sum":
                            act.wait_ge(mask_loaded[u], count(batch, 16, 16))
                            if not (first and u == 0):
                                act.wait_ge(mask_summed[1 - u], count(batch, 1, u))
                            act.activation(mask_abs[:], mask_max[:, u, :], ACT.Abs, accum_out=mask_sum[:, u:u + 1])\
                                .then_inc(mask_summed[u], 1)

                walk(FIRST_STEP, None, first=True)
                with act.Fori(0, B - 1) as b:
                    walk(STEP, b)
                walk(LAST_STEP, None, B - 1)

            @block.vector
            def _(dve):
                dve.sem_inc(max_done, MAX_BUFFERS - 1)
                dve.sem_inc(o_done, 1)
                dve.memset(q_aug[:], 0.0).then_inc(operands_clear, 1)
                dve.memset(k_aug[:], 0.0).then_inc(operands_clear, 1)
                dve.memset(k_f[:], 0.0).then_inc(operands_clear, 1)
                dve.memset(q_t[:], 0.0).then_inc(operands_clear, 1)
                dve.wait_ge(operands_clear, 4)
                dve.memset(k_aug[:, :, :, TERMS * HD:TERMS * HD + 3], 1.0).then_inc(operands_clear, 1)
                dve.wait_ge(const_ready, 1)
                dve.wait_ge(operands_clear, 5)
                dve.wait_ge(bias_in, 48)
                dve.tensor_scalar(bq_row[:], bq_row[:], SCALE, None, ALU.mult).then_inc(bias_scaled, 1)
                dve.wait_ge(bias_scaled, 1)

                def split(batch, which, step):
                    full, rest, aug, parts, done = (
                        (q_f[:], q_rest, q_aug[:], Q_PART, q_split),
                        (k_f[:].rearrange("p t n -> p (t n)"), k_rest, k_aug[:], K_PART, k_split))[which]

                    def left(k):
                        value = full if k == 0 else rest[:]
                        return value.rearrange("p (h d) -> p h d", d=HD)

                    k = step // 2
                    part = block_of(aug, parts.index(k))
                    if step:
                        dve.wait_ge(done, count(batch, 5, step))
                    else:
                        dve.wait_ge(prep_dve, count(batch, PREP_DVE, 1 + KV_ROUNDS if which else 1))
                    if step % 2 == 0:
                        dve.tensor_copy(part, left(k)).then_inc(done, 1)
                    else:
                        dve.tensor_tensor(left(k + 1), left(k), part, ALU.subtract).then_inc(done, 1)

                def prep(batch, n, ahead):
                    what, i, who = PREP[n]
                    if who != "dve":
                        return
                    dve.wait_ge(prep_full, count(batch, len(PREP), n + 1))
                    src = p_side[:] if ahead else ring[n % 4]
                    if what == "q":
                        for lt in range(LT):
                            for half in range(2):
                                def cols(ap, order):
                                    return ap.rearrange(order, u=UNITS, half=2, h=GROUPS)
                                ins = dve.scalar_tensor_tensor(
                                    out=cols(q_f[:, lt * C:(lt + 1) * C], "p (u h half d) -> p u h half d")[:, :, :, half, :],
                                    in0=cols(src[:, lt * C:(lt + 1) * C], "p (u half h d) -> p u half h d")[:, :, half, :, :],
                                    scalar=SCALE, in1=cols(bq_row[:], "p (u half h d) -> p u half h d")[:, :, half, :, :],
                                    op0=ALU.mult, op1=ALU.add)
                    elif what == "kT":
                        for to, of in operand(what, i, src):
                            ins = dve.tensor_copy(to, of)
                    else:
                        if i == 0 and ahead:
                            dve.wait_ge(v_copied, count(batch, UNITS, 0))
                        tiles, r, w = min(4, ST - 4 * i), rows_of(4 * i), KVH * HD
                        both = src[0:r, 0:tiles * P].rearrange("p (t n) -> p t n", n=P)
                        bias = bkv_row[0:r, :].unsqueeze(1).to_broadcast([r, tiles, P])
                        dve.tensor_tensor(k_f[0:r, 4 * i:4 * i + tiles, :], both[:, :, 0:w], bias[:, :, 0:w], ALU.add)
                        ins = dve.tensor_tensor(v_f[0:r, 4 * i:4 * i + tiles, :], both[:, :, w:], bias[:, :, w:], ALU.add)
                    ins.then_inc(prep_dve, 1)

                def row_max(batch, u, n, first):
                    row, k = divmod(n, CHUNKS_PER_ROW)
                    lt, half, hh = row // UH, row // GROUPS % 2, row % GROUPS
                    lo, hi = CHUNK_EDGES[k], CHUNK_EDGES[k + 1]
                    if u == 0 and n in (0, A_PER_UNIT // 2):
                        dve.wait_ge(mask_loaded[lt], count(batch, 16, 16))
                    if n == 0 and not (first and u == 0):
                        dve.wait_ge(max_ready, count(batch, UNITS, u))
                    dve.wait_ge(max_full, count(batch, A_PER_BATCH, A_PER_UNIT * u + n + 1))
                    dve.sem_inc(max_seen, 1)
                    sc = p_max[:, (A_PER_UNIT * u + n) % MAX_BUFFERS].rearrange("p a n -> p (a n)")[:, 0:hi - lo]
                    dve.tensor_tensor_reduce(sc, sc, mask_max[:, lt, lo:hi], 1.0, NEG, ALU.add, ALU.max,
                                             max_part[:, lt, half, hh, k:k + 1]).then_inc(max_done, 1)
                    if n == A_PER_UNIT - 1:
                        dve.wait_ge(max_done, count(batch, A_PER_BATCH, A_PER_UNIT * (u + 1) + MAX_BUFFERS - 1))
                        dve.wait_ge(pool_step, count(batch, POOL_PER_BATCH, POOL_START + MAX_STEPS * u))
                        dve.tensor_reduce(neg_max[:], max_part[:], AX.X, ALU.max, negate=True).then_inc(max_ready, 1)

                def normal(batch, u):
                    dve.wait_ge(o_turned, count(batch, UNITS, u + 2))
                    turned = p_side[:].rearrange("p (t e j c) -> p t e j c", t=LT, e=2, j=4)
                    dve.reciprocal(row_sum[:].rearrange("p t e j -> p (t e) j"),
                                   p_side[:].rearrange("p (k j c) -> p k j c", k=4, j=4)[:, :, :, HD]).then_inc(o_summed, 1)
                    dve.wait_ge(o_summed, count(batch, UNITS, u + 1))
                    reg, more = batch
                    for lt in range(LT):
                        ins = dve.tensor_tensor(
                            o_nat[:, more if reg is None else reg, lt, UH * HD * u:UH * HD * (u + 1)].rearrange("p (j e d) -> p e j d", e=2, d=HD),
                            turned[:, lt, :, :, 0:HD],
                            row_sum[:, lt].unsqueeze(3).to_broadcast([P, 2, 4, HD]), ALU.mult)
                    ins.then_inc(o_done, 1)

                def walk(items, reg, more=0, first=False):
                    for kind, batch, u, n in items:
                        batch = (reg, more + batch)
                        if kind == "max":
                            row_max(batch, u, n, first)
                        elif kind == "normal":
                            normal(batch, u)
                        elif kind == "prep":
                            prep(batch, n, not first or n >= BEFORE_UNITS + 3)
                        elif kind == "split":
                            split(batch, u, n)
                        elif kind == "mask_any":
                            for lt in range(LT):
                                dve.wait_ge(mask_summed[lt], count(batch, 1, 1))
                            dve.tensor_scalar(mask_any[:], mask_sum[:], 0.0, None, ALU.is_gt).then_inc(mask_anyed, 1)
                        elif kind == "mask_flag":
                            dve.wait_ge(mask_counted, count(batch, 1, 1))
                            dve.tensor_scalar(mask_flag[:], p_side[0:1, 0:1], 0.5, None, ALU.is_gt).then_inc(mask_flagged, 1)

                walk(FIRST_STEP, None, first=True)
                with dve.Fori(0, B - 1) as b:
                    walk(STEP, b)
                walk(LAST_STEP, None, B - 1)


CHUNKS = CT * B
ROUNDS_OF = {"turn_w": (1, "act"), "turn_vec": (1, "act"), "turn_o": (1, "act"), "out0": (1, "dve"), "turn_x": (1, "dve"),
             "mix": (1, "act"), "dec1": (1, "act"), "dec2": (1, "act"), "own": (1, "dve"), "spread": (HD // 2, "dve"), "sum": (1, "dve"),
             "mean": (1, "dve"), "var": (1, "act"), "inverse": (1, "dve"), "out1": (1, "dve"), "turn_c": (1, "dve"), "fk": (1, "act"),
             "fr": (1, "act"), "fv": (1, "dve")}
ROUNDS_OF.update({f"m{f}": (1, "dve") for f in range(MIXES)})
ROUNDS_OF.update({f"p{f}": (1, "act") for f in range(1, MIXES)})


def stage_order():
    stages = []

    def add(at, length, b, names):
        names = names.split()
        for k, name in enumerate(names):
            stages.append((at + length * k / len(names), (name, b)))

    for b in range(B):
        add(EARLY_AT[b], EARLY, b, "turn_o out0 stats0 apply0 gain0 stats1 apply1 turn_x shift1")
        at = EARLY + BATCH_STEP * b
        add(at, MIXED, b, "mix m0 m1 dec1 m2 dec2 p1 m3 p2 m4 p3 p4 own silu")
        at += MIXED
        n = CT * b
        stages += [(at, ("state", n)), (at + 0.01, ("spread", n)), (at + CHUNK, ("state", n + 1)), (at + CHUNK + 0.01, ("product", n)),
                   (at + CHUNK + 0.02, ("spread", n + 1)), (at + CHUNK + 2, ("sum", n)),
                   (at + 2 * CHUNK, ("product", n + 1)), (at + 2 * CHUNK + 2, ("sum", n + 1))]
        add(at + 2 * CHUNK + 3, TAIL, b, "mean var inverse out1 stats2 apply2 turn_c shift2 fk fr fv")
    stages.append((EARLY * 0.3, ("turn_vec", 0)))
    for n in range(len(TURNED)):
        stages.append((EARLY * (0.3 + 0.05 * n), ("turn_w", n)))
    return [stage for _, stage in sorted(stages, key=lambda x: x[0])]


EARLY_AT = (0, 0.3, 12, 12.3)
EARLY, BATCH_STEP, MIXED, CHUNK, TAIL = 12.6, 7.2, 18, 6, 38.4
STAGES = stage_order()
ROUNDS = [(name, i * ROUNDS_OF[name][0] + k) for name, i in STAGES if name in ROUNDS_OF for k in range(ROUNDS_OF[name][0])]
NORMS = [stage for stage in STAGES if stage[0].startswith("stats")]
APPLIES = [stage for stage in STAGES if stage[0].startswith("apply")]


def rounds(name, i):
    n = ROUNDS_OF[name][0]
    return range(i * n, (i + 1) * n)


def mixing(nc, sem, held, loads_in, out):
    with ExitStack() as here:
        def sb(name, shape, dt=F32):
            return here.enter_context(nc.sbuf_tensor(name, shape, dt))

        ident, x_nat, o_nat, rows = held["ident_f"], held["x_nat"], held["o_nat"], held["rows"]
        w_t = sb("w_t", [P, len(TURNED), CT, C])
        cols = sb("cols", [P, CT * len(VECTORS)])
        state = sb("state", [P, CT, 2 * B])
        spread, gather, heads, eighth, eps_col = selectors_in(held)
        power = sb("power", [P, B * LT])
        stats = sb("stats", [P, B * LT, 6])
        moments = sb("moments", [P, B * LT, 2])
        var_eps = sb("var_eps", [P, B * LT])
        rstd = sb("rstd", [P, B * LT])
        head_std = sb("head_std", [P, B, CT, LT, NH // 2])
        xa_t = sb("xa_t", [P, CT, B, L + 1])
        sx = sb("sx", [P, CT, B, L])
        xxx = sb("xxx", [P, CT, B, L])
        k_all = sb("k_all", [P, CT, B, L])
        v_all = sb("v_all", [P, CT, B, L])
        r_all = sb("r_all", [P, CT, B, L])
        g_all = sb("g_all", [P, CT, B, L])
        w_all = sb("w_all", [P, CT, B, L])
        mixed = [sb(f"mixed{n}", [P, CT, B, L]) for n in range(3)]
        kv_in = sb("kv_in", [P, HD, L])
        states = [sb(f"states{n}", [P, HD, L + 1]) for n in range(2)]
        read = [sb(f"read{n}", [P, HD, L]) for n in range(2)]
        bank = [here.enter_context(nc.psum_tensor(f"bank{n}", [P, BANK], F32)) for n in range(8)]

        low = held["w_nat"][:].rearrange("p n j c -> p (n j c)")
        lo_rank, lo_last, dec, low3 = (low[:, n * B * L:(n + 1) * B * L] for n in range(4))
        inv_wide = low3.rearrange("p (n j t c) -> p n j t c", n=2, j=CT, t=LT)
        o_t, x_hat, x_hat2, gate = k_all, v_all, w_all, g_all

        def col(name, j):
            n = CT * VECTORS.index(name) + j
            return cols[:, n:n + 1]

        full = {name: sem(f"{name}_full") for name in ROUNDS_OF}
        done = {name: sem(f"{name}_done") for name in ROUNDS_OF}
        power_ready = sem("power_ready")
        ln_stats = sem("ln_stats")
        ln_moments = sem("ln_moments")
        ln_eps = sem("ln_eps")
        ln_rstd = sem("ln_rstd")
        ln_applied = sem("ln_applied")
        gamma_done = sem("gamma_done")
        x1_ready = sem("x1_ready")
        shift_ready = sem("shift_ready")
        sx_ready = sem("sx_ready")
        xxx_ready = sem("xxx_ready")
        mixed_ready = [sem(f"mixed_ready{f}") for f in range(MIXES)]
        w_ready = sem("w_ready")
        silu_ready = sem("silu_ready")
        rku_ready = sem("rku_ready")
        s0_placed = sem("s0_placed")
        scanned = sem("scanned")
        read_ready = sem("read_ready")
        squared = sem("squared")
        inverted = sem("inverted")
        widened = sem("widened")
        scaled = sem("scaled")
        z_ready = sem("z_ready")
        shift2_ready = sem("shift2_ready")
        sx2_ready = sem("sx2_ready")
        ffn_in = sem("ffn_in")
        kk_ready = sem("kk_ready")
        out_ready = sem("out_ready")
        gn_halved = sem("gn_halved")
        stored = sem("stored")

        def halves(ps):
            return ps.rearrange("p (j l) -> p j l", j=CT)

        def bank_of(name, n):
            return bank[ROUNDS.index((name, n)) % 8]

        def walk(work):
            for name, i in STAGES:
                if name in work:
                    work[name](i)

        with nc.Block() as block:

            @block.gpsimd
            def _(pool):
                pool.memset(power[:], -0.5).then_inc(power_ready, 1)

                def root(norm, b):
                    n, k = NORMS.index((norm, b)), slice(LT * b, LT * (b + 1))
                    pool.wait_ge(power_ready, 1)
                    pool.wait_ge(ln_eps, n + 1)
                    pool.tensor_tensor(rstd[:, k], var_eps[:, k], power[:, k], ALU.pow).then_inc(ln_rstd, 1)

                def gain(b):
                    pool.wait_ge(ln_applied, APPLIES.index(("apply0", b)) + 1)
                    pool.tensor_tensor(o_nat[:, b], o_nat[:, b], rows[:, 1, :].unsqueeze(1).to_broadcast([P, LT, C]), ALU.mult)\
                        .then_inc(gamma_done, 1)

                def state_columns(_):
                    pool.wait_ge(done["turn_vec"], 1)
                    for j in range(CT):
                        ins = pool.tensor_scalar(xa_t[:, j, :, 0], state[:, j, 1:2 * B:2], 1.0, None, ALU.mult)
                    ins.then_inc(shift_ready, 1)

                def add_input(f, b):
                    pool.wait_ge(done[f"m{f}"], b + 1)
                    x_f = mixed[f % 3][:, :, b, :]
                    pool.tensor_tensor(x_f, x_f, xa_t[:, :, b, 1:], ALU.add).then_inc(mixed_ready[f], 1)

                def first_state(n):
                    b, j = n // CT, n % CT
                    if n >= 2:
                        pool.wait_ge(read_ready, n - 1)
                    pool.tensor_scalar(states[n % 2][:, :, 0], held["s0"][:, j, b, :], 1.0, None, ALU.mult).then_inc(s0_placed, 1)

                def product(n):
                    b, j = n // CT, n % CT
                    pool.wait_ge(scanned, n + 1)
                    if n >= 2:
                        pool.wait_ge(full["sum"], n - 1)
                    pool.tensor_tensor(read[n % 2][:], states[n % 2][:, :, 0:L],
                                       r_all[:, j, b, :].unsqueeze(1).to_broadcast([P, HD, L]), ALU.mult).then_inc(read_ready, 1)

                work = {"gain0": gain, "turn_vec": state_columns, "state": first_state, "product": product}
                work.update({norm: (lambda b, norm=norm: root(norm, b)) for norm in ("stats0", "stats1", "stats2")})
                work.update({f"m{f}": (lambda b, f=f: add_input(f, b)) for f in range(MIXES)})
                walk(work)

            @block.tensor
            def _(pe):
                at = [0]

                def next_bank(name, n):
                    here = at[0]
                    assert ROUNDS[here] == (name, n), (name, n, ROUNDS[here])
                    at[0] += 1
                    if here >= 8:
                        before, k = ROUNDS[here - 8]
                        pe.wait_ge(done[before], k + 1)
                    return bank[here % 8]

                def turned(name, b, rows_of_batch):
                    out = next_bank(name, b)
                    for lt in range(LT):
                        for j in range(CT):
                            mm = pe.transpose(out[:, j * L + lt * P:j * L + (lt + 1) * P], rows_of_batch(lt)[:, j * P:(j + 1) * P], ident[:])
                    mm.then_inc(full[name], 1)

                def rows_out(name, b, source, weight):
                    out = next_bank(name, b)
                    for lt in range(LT):
                        for j in range(CT):
                            mm = pe.matmul(out[:, lt * C:(lt + 1) * C], source[:, j, b, lt * P:(lt + 1) * P], weight[:, j, :],
                                           start=(j == 0), stop=(j == CT - 1))
                    mm.then_inc(full[name], 1)

                def channels_out(name, b, source, weight):
                    out = next_bank(name, b)
                    for jo in range(CT):
                        for j in range(CT):
                            mm = pe.matmul(halves(out)[:, jo, :], weight[:, j, jo * P:(jo + 1) * P], source[:, j, b, :],
                                           start=(j == 0), stop=(j == CT - 1))
                    mm.then_inc(full[name], 1)

                def turn_w(k):
                    out = next_bank("turn_w", k)
                    for jo in range(CT):
                        for j in range(CT):
                            mm = pe.transpose(out[:, j * C + jo * P:j * C + (jo + 1) * P], held["w_nat"][:, k, jo, j * P:(j + 1) * P], ident[:])
                    mm.then_inc(full["turn_w"], 1)

                def turn_vec(_):
                    out = next_bank("turn_vec", 0)
                    V = CT * len(VECTORS)
                    pe.transpose(out[:, 0:V], held["vec_nat"][:], ident[0:V, 0:V])
                    for j in range(CT):
                        mm = pe.transpose(out[:, V + 2 * B * j:V + 2 * B * (j + 1)], held["state_nat"][:, j * P:(j + 1) * P], ident[0:2 * B, 0:2 * B])
                    mm.then_inc(full["turn_vec"], 1)

                def turn_o(b):
                    turned("turn_o", b, lambda lt: o_nat[:, b, lt, :])

                def out0(b):
                    pe.wait_ge(done["turn_o"], b + 1)
                    rows_out("out0", b, o_t, held["wo"])

                def turn_x(b):
                    pe.wait_ge(ln_applied, APPLIES.index(("apply1", b)) + 1)
                    turned("turn_x", b, lambda lt: x_hat[:, lt, b, :])

                def mix(b):
                    pe.wait_ge(xxx_ready, CT * (b + 1))
                    out = halves(next_bank("mix", b))
                    for last, (lo, hi) in enumerate(((0, (MIXES - 1) * DM), ((MIXES - 1) * DM, MIXES * DM))):
                        for j in range(CT):
                            mm = pe.matmul(out[0:hi - lo, last, :], held["maa_w1"][:, j, lo:hi], xxx[:, j, b, :], start=(j == 0), stop=(j == CT - 1))
                    mm.then_inc(full["mix"], 1)

                def mixed_by(f, b):
                    pe.wait_ge(done["mix"], b + 1)
                    out = halves(next_bank(f"m{f}", b))
                    if f < MIXES - 1:
                        w, t = held["maa_w2"][f * DM:(f + 1) * DM, :], lo_rank[f * DM:(f + 1) * DM, :]
                    else:
                        w, t = held["maa_w2_last"][:], lo_last[0:DM, :]
                    for j in range(CT):
                        mm = pe.matmul(out[:, j, :], w[:, j * P:(j + 1) * P], t[:, b * L:(b + 1) * L], start=True, stop=True)
                    mm.then_inc(full[f"m{f}"], 1)

                def project(f, b):
                    pe.wait_ge(done["turn_w"], f)
                    pe.wait_ge(mixed_ready[f], b + 1)
                    channels_out(f"p{f}", b, mixed[f % 3], w_t[:, f - 1])

                def dec1(b):
                    pe.wait_ge(mixed_ready[0], b + 1)
                    out = next_bank("dec1", b)
                    for j in range(CT):
                        mm = pe.matmul(out[0:DD, 0:L], held["decay_w1"][:, j, :], mixed[0][:, j, b, :], start=(j == 0), stop=(j == CT - 1))
                    mm.then_inc(full["dec1"], 1)

                def dec2(b):
                    pe.wait_ge(done["dec1"], b + 1)
                    out = halves(next_bank("dec2", b))
                    for j in range(CT):
                        mm = pe.matmul(out[:, j, :], held["decay_w2"][:, j * P:(j + 1) * P], dec[0:DD, b * L:(b + 1) * L], start=True, stop=True)
                    mm.then_inc(full["dec2"], 1)

                def own(b):
                    pe.wait_ge(rku_ready, CT * (b + 1))
                    out = halves(next_bank("own", b))
                    pe.matmul(out, heads.rearrange("p h s -> p (h s)"), mixed[2][:, :, b, :], start=True, stop=True).then_inc(full["own"], 1)

                def spread_values(n):
                    b, j = n // CT, n % CT
                    for i in range(HD // 2):
                        out = next_bank("spread", 4 * n + i)
                        for t in range(2):
                            mm = pe.matmul(out[:, t * L:(t + 1) * L], spread[:, 2 * i + t].rearrange("p h s -> p (h s)"), v_all[:, j, b, :],
                                           start=True, stop=True)
                        mm.then_inc(full["spread"], 1)

                def sum_head(n):
                    pe.wait_ge(read_ready, n + 1)
                    out = next_bank("sum", n)
                    for t in range(HD):
                        mm = pe.matmul(out[:, 0:L], gather[:, t].rearrange("p h s -> p (h s)"), read[n % 2][:, t, :],
                                       start=(t == 0), stop=(t == HD - 1))
                    mm.then_inc(full["sum"], 1)

                def head_mean(b):
                    pe.wait_ge(done["sum"], CT * (b + 1))
                    out = halves(next_bank("mean", b))
                    pe.matmul(out, eighth.rearrange("p h s -> p (h s)"), xxx[:, :, b, :], start=True, stop=True).then_inc(full["mean"], 1)

                def variance(b):
                    pe.wait_ge(squared, b + 1)
                    out = next_bank("var", b)[:, 0:CT * LT * NH // 2].rearrange("p (j t h) -> p j t h", j=CT, t=LT)
                    for j in range(CT):
                        for lt in range(LT):
                            mm = pe.matmul(out[:, j, lt, :], r_all[:, j, b, lt * P:(lt + 1) * P], eighth[:, :, 0], start=True, stop=True)
                    mm.then_inc(full["var"], 1)

                def inverse(b):
                    pe.wait_ge(widened, b + 1)
                    out = halves(next_bank("inverse", b))
                    for j in range(CT):
                        for lt in range(LT):
                            mm = pe.matmul(out[:, j, lt * P:(lt + 1) * P], inv_wide[:, b % 2, j, lt, :], ident[:], start=True, stop=True)
                    mm.then_inc(full["inverse"], 1)

                def out1(b):
                    pe.wait_ge(z_ready, b + 1)
                    rows_out("out1", b, k_all, w_t[:, TURNED.index("Wo")])

                def turn_c(b):
                    pe.wait_ge(ln_applied, APPLIES.index(("apply2", b)) + 1)
                    turned("turn_c", b, lambda lt: x_hat2[:, lt, b, :])

                def fk(b):
                    pe.wait_ge(ffn_in, 2 * CT * b + CT)
                    channels_out("fk", b, r_all, w_t[:, TURNED.index("fWk")])

                def fr(b):
                    pe.wait_ge(ffn_in, 2 * CT * (b + 1))
                    rows_out("fr", b, v_all, w_t[:, TURNED.index("fWr")])

                def fv(b):
                    pe.wait_ge(kk_ready, b + 1)
                    rows_out("fv", b, k_all, w_t[:, TURNED.index("fWv")])

                work = {"turn_w": turn_w, "turn_vec": turn_vec, "turn_o": turn_o, "out0": out0, "turn_x": turn_x, "mix": mix,
                        "dec1": dec1, "dec2": dec2, "own": own, "spread": spread_values, "sum": sum_head, "mean": head_mean, "var": variance,
                        "inverse": inverse, "out1": out1,
                        "turn_c": turn_c, "fk": fk, "fr": fr, "fv": fv}
                work.update({f"m{f}": (lambda b, f=f: mixed_by(f, b)) for f in range(MIXES)})
                work.update({f"p{f}": (lambda b, f=f: project(f, b)) for f in range(1, MIXES)})
                walk(work)
                assert at[0] == len(ROUNDS)

            @block.scalar
            def _(act):
                def each(name, i):
                    for n in rounds(name, i):
                        act.wait_ge(full[name], n + 1)
                        yield n, bank_of(name, n)

                def turn_w(k):
                    for n, ps in each("turn_w", k):
                        act.activation(w_t[:, n].rearrange("p j c -> p (j c)"), ps[:], ACT.Copy).then_inc(done["turn_w"], 1)

                def turn_vec(_):
                    V = CT * len(VECTORS)
                    for n, ps in each("turn_vec", 0):
                        act.activation(cols[:], ps[:, 0:V], ACT.Copy)
                        act.activation(state[:].rearrange("p j n -> p (j n)"), ps[:, V:V + 2 * B * CT], ACT.Copy).then_inc(done["turn_vec"], 1)
                    act.wait_ge(done["turn_vec"], 1)
                    lo, hi = CT * VECTORS.index("gn_w"), CT * VECTORS.index("gn_b") + CT
                    act.activation(cols[:, lo:hi], cols[:, lo:hi], ACT.Copy, scale=0.5).then_inc(gn_halved, 1)

                def turn_o(b):
                    for _, ps in each("turn_o", b):
                        act.activation(o_t[:, :, b, :], halves(ps), ACT.Copy).then_inc(done["turn_o"], 1)

                def mix(b):
                    act.wait_ge(full["turn_w"], len(TURNED))
                    for _, ps in each("mix", b):
                        act.activation(lo_rank[:, b * L:(b + 1) * L], halves(ps)[:, 0, :], ACT.Tanh)
                        act.activation(lo_last[0:DM, b * L:(b + 1) * L], halves(ps)[0:DM, 1, :], ACT.Tanh).then_inc(done["mix"], 1)

                def dec1(b):
                    for _, ps in each("dec1", b):
                        act.activation(dec[0:DD, b * L:(b + 1) * L], ps[0:DD, 0:L], ACT.Tanh).then_inc(done["dec1"], 1)

                def dec2(b):
                    for _, ps in each("dec2", b):
                        for j in range(CT):
                            ins = act.activation(w_all[:, j, b, :], halves(ps)[:, j, :], ACT.Exp, bias=col("time_decay", j))
                        ins.then_inc(done["dec2"], 1)
                    act.wait_ge(done["dec2"], b + 1)
                    act.activation(w_all[:, :, b, :], w_all[:, :, b, :], ACT.Exp, scale=-1.0).then_inc(w_ready, 1)

                def projected(f, b):
                    to = {1: k_all, 2: v_all, 3: r_all, 4: g_all}[f]
                    for _, ps in each(f"p{f}", b):
                        ins = act.activation(to[:, :, b, :], halves(ps), ACT.Copy)
                        if f == 4:
                            ins = act.activation(xxx[:, :, b, :], halves(ps), ACT.Tanh, scale=0.5)
                        ins.then_inc(done[f"p{f}"], 1)

                def mean(b):
                    act.wait_ge(done["mean"], b + 1)
                    act.activation(r_all[:, :, b, :], k_all[:, :, b, :], ACT.Square).then_inc(squared, 1)

                def var(b):
                    for _, ps in each("var", b):
                        act.activation(head_std[:, b], ps[:, 0:CT * LT * NH // 2].rearrange("p (j t h) -> p j t h", j=CT, t=LT),
                                       ACT.Sqrt, bias=eps_col).then_inc(done["var"], 1)

                def inverse(b):
                    act.wait_ge(inverted, b + 1)
                    if b >= 2:
                        act.wait_ge(full["inverse"], b - 1)
                    wide = inv_wide[:, b % 2].rearrange("p j t (h s) -> p (j t) h s", s=HD)
                    std = head_std[:, b].rearrange("p j t h -> p (j t) h")
                    act.activation(wide, std.unsqueeze(3).to_broadcast([P, CT * LT, NH // 2, HD]), ACT.Copy).then_inc(widened, 1)
                    act.wait_ge(done["inverse"], b + 1)
                    for j in range(CT):
                        d = k_all[:, j, b, :]
                        ins = act.activation(d, d, ACT.Identity, scale=col("gn_w", j), bias=col("gn_b", j))
                    ins.then_inc(scaled, 1)

                def fk(b):
                    for _, ps in each("fk", b):
                        act.activation(k_all[:, :, b, :], halves(ps), ACT.Relu).then_inc(done["fk"], 1)
                    act.wait_ge(done["fk"], b + 1)
                    act.activation(k_all[:, :, b, :], k_all[:, :, b, :], ACT.Square).then_inc(kk_ready, 1)

                def fr(b):
                    for _, ps in each("fr", b):
                        act.activation(gate[:, :, b, :], halves(ps), ACT.Tanh, scale=0.5).then_inc(done["fr"], 1)

                work = {"turn_w": turn_w, "turn_vec": turn_vec, "turn_o": turn_o, "mix": mix, "dec1": dec1, "dec2": dec2,
                        "mean": mean, "var": var, "inverse": inverse, "fk": fk, "fr": fr}
                work.update({f"p{f}": (lambda b, f=f: projected(f, b)) for f in range(1, MIXES)})
                walk(work)

            @block.vector
            def _(dve):
                def each(name, i):
                    for n in rounds(name, i):
                        dve.wait_ge(full[name], n + 1)
                        yield n, bank_of(name, n)

                def out0(b):
                    for _, ps in each("out0", b):
                        dve.tensor_tensor(x_nat[:, b], halves(ps), x_nat[:, b], ALU.add).then_inc(done["out0"], 1)

                def row_stats(norm, b):
                    n, k = NORMS.index((norm, b)), slice(LT * b, LT * (b + 1))
                    source = {"stats0": x_nat, "stats1": o_nat, "stats2": x_nat}[norm]
                    dve.wait_ge({"stats0": done["out0"], "stats1": x1_ready, "stats2": done["out1"]}[norm], b + 1)
                    for lt in range(LT):
                        ins = dve.bn_stats(stats[:, b * LT + lt, :], source[:, b, lt, :])
                    ins.then_inc(ln_stats, 1)
                    dve.wait_ge(ln_stats, n + 1)
                    for lt in range(LT):
                        ins = dve.bn_aggr(moments[:, b * LT + lt, :], stats[:, b * LT + lt, :])
                    ins.then_inc(ln_moments, 1)
                    dve.wait_ge(ln_moments, n + 1)
                    dve.tensor_scalar(var_eps[:, k], moments[:, k, 1], EPS0 if norm == "stats0" else EPS1, None, ALU.add).then_inc(ln_eps, 1)

                def apply(norm, b):
                    dve.wait_ge(ln_rstd, NORMS.index((norm.replace("apply", "stats"), b)) + 1)
                    for lt in range(LT):
                        source, to = {"apply0": (x_nat[:, b, lt, :], o_nat[:, b, lt, :]), "apply1": (o_nat[:, b, lt, :], x_hat[:, lt, b, :]),
                                      "apply2": (x_nat[:, b, lt, :], x_hat2[:, lt, b, :])}[norm]
                        k = b * LT + lt
                        ins = dve.tensor_scalar(to, source, moments[:, k, 0:1], rstd[:, k:k + 1], ALU.subtract, ALU.mult)
                    ins.then_inc(ln_applied, 1)

                def gain(b):
                    dve.wait_ge(gamma_done, b + 1)
                    dve.tensor_tensor(o_nat[:, b], o_nat[:, b], rows[:, 2, :].unsqueeze(1).to_broadcast([P, LT, C]), ALU.add)\
                        .then_inc(x1_ready, 1)

                def turned(name, b, weight, bias):
                    for _, ps in each(name, b):
                        for j in range(CT):
                            ins = dve.tensor_scalar(xa_t[:, j, b, 1:], halves(ps)[:, j, :], col(weight, j), col(bias, j), ALU.mult, ALU.add)
                        ins.then_inc(done[name], 1)

                def turn_x(b):
                    dve.wait_ge(done["turn_vec"], 1)
                    turned("turn_x", b, "ln1_w", "ln1_b")

                def turn_c(b):
                    dve.tensor_copy(xa_t[:, :, b, 0], state[:, :, 2 * b]).then_inc(shift2_ready, 1)
                    turned("turn_c", b, "ln2_w", "ln2_b")

                def shifted(name, b, ready):
                    dve.wait_ge(done[name], b + 1)
                    x_b = xa_t[:, :, b, :]
                    dve.tensor_tensor(sx[:, :, b, :], x_b[:, :, 0:L], x_b[:, :, 1:], ALU.subtract).then_inc(ready, 1)
                    dve.wait_ge(ready, b + 1)

                def shift1(b):
                    dve.wait_ge(shift_ready, 1)
                    shifted("turn_x", b, sx_ready)
                    for j in range(CT):
                        dve.scalar_tensor_tensor(out=xxx[:, j, b, :], in0=sx[:, j, b, :], scalar=col("maa_x", j), in1=xa_t[:, j, b, 1:],
                                                 op0=ALU.mult, op1=ALU.add).then_inc(xxx_ready, 1)

                def shift2(b):
                    dve.wait_ge(shift2_ready, b + 1)
                    shifted("turn_c", b, sx2_ready)
                    for to, name in ((r_all, "fmaa_k"), (v_all, "fmaa_r")):
                        for j in range(CT):
                            dve.scalar_tensor_tensor(out=to[:, j, b, :], in0=sx[:, j, b, :], scalar=col(name, j), in1=xa_t[:, j, b, 1:],
                                                     op0=ALU.mult, op1=ALU.add).then_inc(ffn_in, 1)

                def mix(f, b):
                    if f >= 3:
                        dve.wait_ge(full["dec1" if f == 3 else "p1"], b + 1)
                    for _, ps in each(f"m{f}", b):
                        for j in range(CT):
                            ins = dve.scalar_tensor_tensor(out=mixed[f % 3][:, j, b, :], in0=halves(ps)[:, j, :], scalar=col("maa_" + "wkvrg"[f], j),
                                                           in1=sx[:, j, b, :], op0=ALU.add, op1=ALU.mult)
                        ins.then_inc(done[f"m{f}"], 1)

                def own(b):
                    dve.wait_ge(done["p1"], b + 1)
                    dve.wait_ge(done["p3"], b + 1)
                    dve.wait_ge(full["p2"], b + 1)
                    for j in range(CT):
                        dve.scalar_tensor_tensor(out=mixed[2][:, j, b, :], in0=r_all[:, j, b, :], scalar=col("faaaa", j), in1=k_all[:, j, b, :],
                                                 op0=ALU.mult, op1=ALU.mult).then_inc(rku_ready, 1)
                    dve.wait_ge(done["p2"], b + 1)
                    for _, ps in each("own", b):
                        dve.tensor_tensor(sx[:, :, b, :], halves(ps), v_all[:, :, b, :], ALU.mult).then_inc(done["own"], 1)

                def silu(b):
                    dve.wait_ge(done["p4"], b + 1)
                    dve.scalar_tensor_tensor(out=g_all[:, :, b, :], in0=xxx[:, :, b, :], scalar=1.0, in1=g_all[:, :, b, :],
                                             op0=ALU.add, op1=ALU.mult).then_inc(silu_ready, 1)

                def recur(n):
                    b, j = n // CT, n % CT
                    dve.wait_ge(w_ready, b + 1)
                    dve.wait_ge(silu_ready, b + 1)
                    if n:
                        dve.wait_ge(scanned, n)
                    for i, ps in each("spread", n):
                        t = 2 * (i - 4 * n)
                        dve.tensor_tensor(kv_in[:, t:t + 2, :], halves(ps),
                                          k_all[:, j, b, :].unsqueeze(1).to_broadcast([P, 2, L]), ALU.mult).then_inc(done["spread"], 1)
                    dve.wait_ge(done["spread"], 4 * n + 4)
                    dve.wait_ge(s0_placed, n + 1)
                    for t in range(HD):
                        ins = dve.tensor_tensor_scan(states[n % 2][:, t, 1:], w_all[:, j, b, :], kv_in[:, t, :],
                                                     states[n % 2][:, t, 0:1], ALU.mult, ALU.add)
                    ins.then_inc(scanned, 1)

                def add_own(n):
                    b, j = n // CT, n % CT
                    for _, ps in each("sum", n):
                        dve.tensor_tensor(xxx[:, j, b, :], ps[:, 0:L], sx[:, j, b, :], ALU.add).then_inc(done["sum"], 1)

                def mean(b):
                    dve.wait_ge(done["sum"], CT * (b + 1))
                    for _, ps in each("mean", b):
                        dve.tensor_tensor(k_all[:, :, b, :], xxx[:, :, b, :], halves(ps), ALU.subtract).then_inc(done["mean"], 1)

                def var(b):
                    dve.wait_ge(done["var"], b + 1)
                    dve.reciprocal(head_std[:, b], head_std[:, b]).then_inc(inverted, 1)

                def inverse(b):
                    dve.wait_ge(gn_halved, 1)
                    d = k_all[:, :, b, :]
                    for _, ps in each("inverse", b):
                        dve.tensor_tensor(d, d, halves(ps), ALU.mult).then_inc(done["inverse"], 1)
                    dve.wait_ge(scaled, b + 1)
                    dve.tensor_tensor(d, d, g_all[:, :, b, :], ALU.mult).then_inc(z_ready, 1)

                def out1(b):
                    for _, ps in each("out1", b):
                        dve.tensor_tensor(x_nat[:, b], halves(ps), o_nat[:, b], ALU.add).then_inc(done["out1"], 1)

                def fv(b):
                    dve.wait_ge(done["fr"], b + 1)
                    y = gate[:, :, b, :]
                    for _, ps in each("fv", b):
                        dve.scalar_tensor_tensor(out=y, in0=y, scalar=1.0, in1=halves(ps), op0=ALU.add, op1=ALU.mult).then_inc(done["fv"], 1)
                    dve.wait_ge(done["fv"], b + 1)
                    dve.scalar_tensor_tensor(out=o_nat[:, b], in0=y, scalar=0.5, in1=x_nat[:, b], op0=ALU.mult, op1=ALU.add).then_inc(out_ready, 1)

                work = {"out0": out0, "gain0": gain, "turn_x": turn_x, "turn_c": turn_c, "shift1": shift1, "shift2": shift2, "own": own, "silu": silu,
                        "spread": recur, "sum": add_own, "mean": mean, "var": var, "inverse": inverse,
                        "out1": out1, "fv": fv}
                work.update({f"stats{n}": (lambda b, n=n: row_stats(f"stats{n}", b)) for n in range(3)})
                work.update({f"apply{n}": (lambda b, n=n: apply(f"apply{n}", b)) for n in range(3)})
                work.update({f"m{f}": (lambda b, f=f: mix(f, b)) for f in range(MIXES)})
                walk(work)

            @block.sync
            def _(sp):
                for b in range(B):
                    sp.wait_ge(out_ready, b + 1)
                    sp.dma_start(out[b].rearrange("(t p) c -> p t c", p=P), o_nat[:, b]).then_inc(stored, 16)
                sp.wait_ge(stored, 16 * B)


_INS = {'x': 'x', 'ctx_2048': 'ctx', 'mask_Bx1xSxS2_ff0': 'mask', 'L0_xattn_Wq': 'Wq', 'L0_xattn_bq': 'bq', 'L0_xattn_Wk': 'Wk0',
        'L0_xattn_bk': 'bk', 'L0_xattn_Wv': 'Wv0', 'L0_xattn_bv': 'bv', 'L0_xattn_Wo': 'Wo0', 'L0_xattn_bo': 'bo',
        'L0_xattn_gamma': 'gamma', 'L0_xattn_beta': 'beta'}
_INS.update({f'L1_xattn_{n}': n for n in (*VECTORS, *TURNED, 'maa_w1', 'maa_w2', 'decay_w1', 'decay_w2')})


def kernel(**inputs):
    import numpy as _np
    import concourse.bacc as _bacc
    from concourse import mybir as _mybir
    from concourse.bass_utils import run_bass_kernel_spmd as _run

    nc = _bacc.Bacc("TRN2", target_bir_lowering=False, num_devices=1)
    arrays, args = {}, {}
    for name, short in _INS.items():
        v = _np.ascontiguousarray(inputs[name])
        arrays[f"in_{name}_dram"] = v
        args[short] = nc.dram_tensor(f"in_{name}_dram", v.shape, _mybir.dt.from_np(v.dtype), kind="ExternalInput").ap()
    out = nc.dram_tensor("out_0_dram", (B, L, C), _mybir.dt.float32, kind="ExternalOutput").ap()
    build(nc, args, out)
    r = _run(nc, [arrays], core_ids=[0])
    return r.results[0]["out_0_dram"]
```
